# Optimizing a Trainium2 kernel written in Bass

```python
import numpy as np
import jax
import jax.numpy as jnp

def _softmax(x, axis=-1):
    return jax.nn.softmax(x, axis=axis)

def _gelu(x):
    return jax.nn.gelu(x, approximate=True)

def _silu(x):
    return jax.nn.silu(x)

def _sigmoid(x):
    return jax.nn.sigmoid(x)

def _layernorm(x, axis=-1, eps=1e-05):
    m = jnp.mean(x, axis=axis, keepdims=True)
    v = jnp.var(x, axis=axis, keepdims=True)
    return (x - m) / jnp.sqrt(v + eps)

def _scatter_add(tgt, idx, src, axis=0):
    return tgt.at[idx].add(src)

def _segment_sum(src, seg, n):
    return jax.ops.segment_sum(src, seg, n)
kernel_name = 'mk_seq_postln_d1_jaxref_r4_fa6ba5'

def setup_inputs(seed: int=0):
    np.random.seed(seed)
    _w = jnp.asarray

    def _L0_attn_setup():
        import jax, jax.numpy as jnp
        import numpy as np
        B, T, DM = (2, 1024, 512)
        H, HKV, HD, CHUNK = (16, 4, 128, 128)
        N_REP = H // HKV

        def _chunked_attention(q, k, v):
            b, h, tq, d = q.shape
            tk = k.shape[2]
            n_chunks = tk // CHUNK
            scale = 1.0 / np.sqrt(d).astype(np.float32)
            k_chunks = k.reshape(b, h, n_chunks, CHUNK, d).transpose(2, 0, 1, 3, 4)
            v_chunks = v.reshape(b, h, n_chunks, CHUNK, d).transpose(2, 0, 1, 3, 4)
            starts = (jnp.arange(n_chunks) * CHUNK).astype(jnp.int32)
            q_pos = jnp.arange(tq)[:, None]

            def step(carry, xs):
                m, s, o = carry
                kc, vc, st = xs
                scores = scale * jnp.einsum('bhqd,bhkd->bhqk', q, kc)
                k_pos = st + jnp.arange(CHUNK)[None, :]
                mask = k_pos > q_pos
                scores = jnp.where(mask[None, None], -jnp.inf, scores)
                chunk_max = scores.max(axis=-1)
                new_max = jnp.maximum(m, chunk_max)
                exp_new = jnp.exp(scores - new_max[..., None])
                chunk_sum = exp_new.sum(axis=-1)
                scale_prev = jnp.exp(m - new_max)
                new_sum = scale_prev * s + chunk_sum
                new_out = scale_prev[..., None] * o + jnp.einsum('bhqk,bhkd->bhqd', exp_new, vc)
                return ((new_max, new_sum, new_out), None)
            init = (jnp.full((b, h, tq), -jnp.inf, jnp.float32), jnp.zeros((b, h, tq), jnp.float32), jnp.zeros((b, h, tq, d), jnp.float32))
            (m, s, o), _ = jax.lax.scan(step, init, (k_chunks, v_chunks, starts))
            return o / s[..., None]
        key = jax.random.key(seed)
        ks = jax.random.split(key, 5)
        s = 0.02
        return {'x': jax.random.normal(ks[0], (B, T, DM), jnp.float32), 'wq': jax.random.normal(ks[1], (DM, H * HD), jnp.float32) * s, 'wk': jax.random.normal(ks[2], (DM, HKV * HD), jnp.float32) * s, 'wv': jax.random.normal(ks[3], (DM, HKV * HD), jnp.float32) * s, 'wo': jax.random.normal(ks[4], (H * HD, DM), jnp.float32) * s}
    _L0_attn_in = _L0_attn_setup()

    def _L0_ffn_setup():
        import jax, jax.numpy as jnp
        import numpy as np
        TOP_K = 2
        key = jax.random.key(seed)
        ks = jax.random.split(key, 7)
        B, S, H = (2, 512, 512)
        E, A, NS = (8, 64, 4096)
        x = jax.random.normal(ks[0], (B, S, H), jnp.float32)
        gate_w = jax.random.normal(ks[1], (E, H), jnp.float32) * 0.01
        W = jax.random.normal(ks[2], (H, H), jnp.float32) * 0.02
        atoms = jax.random.normal(ks[3], (A, NS), jnp.float32) * 0.02
        expert_atom_weights = jax.random.normal(ks[4], (E, A), jnp.float32) * 0.1
        importance = jax.random.normal(ks[5], (E, NS), jnp.float32) * 0.1
        mask_idx = jax.random.randint(ks[6], (NS,), 0, H * H, jnp.int32)
        return dict(x=x, gate_w=gate_w, W=W, atoms=atoms, expert_atom_weights=expert_atom_weights, importance=importance, mask_idx=mask_idx)
    _L0_ffn_in = _L0_ffn_setup()
    _d = {'L0_attn_x': _L0_attn_in['x'], 'L0_attn_wq': _L0_attn_in['wq'], 'L0_attn_wk': _L0_attn_in['wk'], 'L0_attn_wv': _L0_attn_in['wv'], 'L0_attn_wo': _L0_attn_in['wo'], 'L0_ffn_gate_w': _L0_ffn_in['gate_w'], 'L0_ffn_W': _L0_ffn_in['W'], 'L0_ffn_atoms': _L0_ffn_in['atoms'], 'L0_ffn_expert_atom_weights': _L0_ffn_in['expert_atom_weights'], 'L0_ffn_importance': _L0_ffn_in['importance'], 'L0_ffn_mask_idx': _L0_ffn_in['mask_idx']}
    _x0 = _d['L0_attn_x']
    _d['L0_attn_x'] = jax.random.normal(jax.random.fold_in(jax.random.key(seed), 1), (8, 512, 512), dtype=_x0.dtype)
    del _x0
    return _d

def reference(L0_attn_x, L0_attn_wq, L0_attn_wk, L0_attn_wv, L0_attn_wo, L0_ffn_gate_w, L0_ffn_W, L0_ffn_atoms, L0_ffn_expert_atom_weights, L0_ffn_importance, L0_ffn_mask_idx):

    def _L0_attn_ref(x, wq, wk, wv, wo):
        import jax, jax.numpy as jnp
        import numpy as np
        B, T, DM = (2, 1024, 512)
        H, HKV, HD, CHUNK = (16, 4, 128, 128)
        N_REP = H // HKV

        def _chunked_attention(q, k, v):
            b, h, tq, d = q.shape
            tk = k.shape[2]
            n_chunks = tk // CHUNK
            scale = 1.0 / np.sqrt(d).astype(np.float32)
            k_chunks = k.reshape(b, h, n_chunks, CHUNK, d).transpose(2, 0, 1, 3, 4)
            v_chunks = v.reshape(b, h, n_chunks, CHUNK, d).transpose(2, 0, 1, 3, 4)
            starts = (jnp.arange(n_chunks) * CHUNK).astype(jnp.int32)
            q_pos = jnp.arange(tq)[:, None]

            def step(carry, xs):
                m, s, o = carry
                kc, vc, st = xs
                scores = scale * jnp.einsum('bhqd,bhkd->bhqk', q, kc)
                k_pos = st + jnp.arange(CHUNK)[None, :]
                mask = k_pos > q_pos
                scores = jnp.where(mask[None, None], -jnp.inf, scores)
                chunk_max = scores.max(axis=-1)
                new_max = jnp.maximum(m, chunk_max)
                exp_new = jnp.exp(scores - new_max[..., None])
                chunk_sum = exp_new.sum(axis=-1)
                scale_prev = jnp.exp(m - new_max)
                new_sum = scale_prev * s + chunk_sum
                new_out = scale_prev[..., None] * o + jnp.einsum('bhqk,bhkd->bhqd', exp_new, vc)
                return ((new_max, new_sum, new_out), None)
            init = (jnp.full((b, h, tq), -jnp.inf, jnp.float32), jnp.zeros((b, h, tq), jnp.float32), jnp.zeros((b, h, tq, d), jnp.float32))
            (m, s, o), _ = jax.lax.scan(step, init, (k_chunks, v_chunks, starts))
            return o / s[..., None]
        b, t, _ = x.shape
        q = (x @ wq).reshape(b, t, H, HD)
        k = (x @ wk).reshape(b, t, HKV, HD)
        v = (x @ wv).reshape(b, t, HKV, HD)
        k = jnp.repeat(k, N_REP, axis=2)
        v = jnp.repeat(v, N_REP, axis=2)
        q = q.transpose(0, 2, 1, 3)
        k = k.transpose(0, 2, 1, 3)
        v = v.transpose(0, 2, 1, 3)
        out = _chunked_attention(q, k, v)
        out = out.transpose(0, 2, 1, 3).reshape(b, t, H * HD)
        return out @ wo

    def _L0_ffn_ref(x, gate_w, W, atoms, expert_atom_weights, importance, mask_idx):
        import jax, jax.numpy as jnp
        import numpy as np
        TOP_K = 2
        B, S, H = x.shape
        xt = x.reshape(-1, H)
        logits = jnp.clip(xt @ gate_w.T, -50.0, 50.0)
        top_w, top_idx = jax.lax.top_k(logits, TOP_K)
        rw = jax.nn.softmax(top_w, axis=-1)
        deltas = jax.nn.softmax(expert_atom_weights, axis=-1) @ atoms
        weighted = deltas * jax.nn.sigmoid(importance)
        rows = mask_idx // H
        cols = mask_idx % H
        vals = jnp.einsum('tk,tks->ts', rw, weighted[top_idx])
        xg = xt[:, cols]
        contrib = jax.ops.segment_sum((xg * vals).T, rows, num_segments=H)
        out = xt @ W.T + contrib.T
        return out.reshape(B, S, H)
    x = L0_attn_x
    x = _layernorm(x + _L0_attn_ref(x, L0_attn_wq, L0_attn_wk, L0_attn_wv, L0_attn_wo), axis=-1)
    x = _layernorm(x + _L0_ffn_ref(x, L0_ffn_gate_w, L0_ffn_W, L0_ffn_atoms, L0_ffn_expert_atom_weights, L0_ffn_importance, L0_ffn_mask_idx), axis=-1)
    return x

_drawn_inputs = setup_inputs


def setup_inputs(seed=0):
    import zlib

    import numpy as np

    out = dict(_drawn_inputs(seed))
    spreads = {}
    factors = {'L0_attn_wq': 6.124,
     'L0_attn_wk': 6.101,
     'L0_ffn_gate_w': 21.846,
     'L0_ffn_atoms': 8.0,
     'L0_ffn_expert_atom_weights': 8.0,
     'L0_ffn_importance': 43.329}
    for name, (base, spread) in spreads.items():
        noise = np.random.default_rng([zlib.crc32(name.encode()), seed]).standard_normal(out[name].shape)
        drawn = base * np.exp(spread * noise) if base else spread * noise
        out[name] = jnp.asarray(drawn.astype(out[name].dtype))
    for name, factor in factors.items():
        out[name] = (out[name] * factor).astype(out[name].dtype)
    return out
```

```python
from contextlib import ExitStack

import concourse.bass as bass
from concourse import mybir

F32 = mybir.dt.float32
F32R = mybir.dt.float32r
BF16 = mybir.dt.bfloat16
I32 = mybir.dt.int32
U32 = mybir.dt.uint32
ALU = mybir.AluOpType
ACT = mybir.ActivationFunctionType
AX = mybir.AxisListType

P = 128
NB, T, DM = 8, 512, 512
H, HKV, HD = 16, 4, 128
G = H // HKV
C = DM // P
TT = T // P
NIT = NB * HKV
NE, NA, NS = 8, 64, 4096
NJ = NS // P
NT = NB * TT
SCALE = float(HD) ** -0.5
EPS = 1e-5
MASKED = -1e38
SHIFT = DM.bit_length() - 1

ROWS = [(3, 0, 0), (2, 1, 0), (0, 1, 384), (1, 2, 0)]
KEYS = [(0, 0, 0), (1, 1, 0), (3, 1, 384), (2, 2, 0)]
PACK = 1280
ROW_AT = {i: 512 * bank + col for i, bank, col in ROWS}
KEY_AT = {j: 512 * bank + col for j, bank, col in KEYS}
UNIT = [(0, 512), (512, 1024), (1024, 1280)]

BANK_S, BANK_PT, BANK_A, BANK_B, BANK_C = 0, 3, 5, 6, 7


def build(nc, x, wq, wk, wv, wo, gate_w, w_ffn, atoms, eaw, importance, mask_idx, out):
    r_dram = nc.dram_tensor("attn_residual", (NT, P, DM), F32, kind="Internal").ap()
    d_dram = nc.dram_tensor("expert_weights", (DM * DM + P, NE), F32, kind="Internal").ap()
    x_rows = x.rearrange("b (t p) d -> b p t d", p=P)
    r_store = r_dram.rearrange("(b t) p d -> b p t d", b=NB)
    out_rows = out.rearrange("b (t p) d -> (b t) p d", p=P)
    wq_v = wq.rearrange("(c p) n -> p c n", p=P)
    wk_v = wk.rearrange("(c p) n -> p c n", p=P)
    wv_v = wv.rearrange("(c p) n -> p c n", p=P)
    wo_v = wo.rearrange("(h p) n -> p h n", p=P)

    with ExitStack() as top:
        def sem(name):
            return top.enter_context(nc.semaphore(name))

        ident = top.enter_context(nc.sbuf_tensor("ident", [P, P], F32))
        gateT = top.enter_context(nc.sbuf_tensor("gateT", [P, C, NE], F32))
        psum = top.enter_context(nc.psum_tensor("psum", [P, 8, 512], F32))
        causal_bf = top.enter_context(nc.sbuf_tensor("causal_bf", [P, P], BF16))
        ident_bf = top.enter_context(nc.sbuf_tensor("ident_bf", [P, P], BF16))
        row_i = top.enter_context(nc.sbuf_tensor("row_i", [P, NJ], I32))
        entry_sum = top.enter_context(nc.sbuf_tensor("entry_sum", [P, NJ, NE], F32))
        s_passed = sem("waits_passed")
        expert_entries(nc, sem, psum, ident, ident_bf, causal_bf, gateT, row_i, entry_sum, d_dram, gate_w, w_ffn,
                       atoms, eaw, importance, mask_idx)
        attention(nc, sem, s_passed, psum, ident, ident_bf, causal_bf, row_i, entry_sum, x_rows, r_store, d_dram, wq_v, wk_v,
                  wv_v, wo_v)
        experts(nc, sem, s_passed, psum, ident, gateT, r_dram, d_dram, out_rows)


def expert_entries(nc, sem, psum, ident, ident_bf, causal_bf, gateT, row_i, entry_sum, d_dram, gate_w, w_ffn, atoms,
                   eaw, importance, mask_idx):
    with ExitStack() as ctx:
        def sb(name, shape, dt=F32):
            return ctx.enter_context(nc.sbuf_tensor(name, shape, dt))

        idx_i, idx_r_i, idx_c_i = sb("idx_i", [P, NJ], I32), sb("idx_r_i", [P, NJ], I32), sb("idx_c_i", [P, NJ], I32)
        idx_f, row_f, dup, gap_f = sb("idx_f", [P, NJ]), sb("row_f", [P, NJ]), sb("dup", [P, NJ]), sb("gap_f", [P, NJ])
        spare_i, spare_f = sb("spare_i", [P, 1], I32), sb("spare_f", [P, 1])
        entry = sb("entry", [P, NJ, NE])
        same = sb("same", [P, 2, P])
        lower, lower_out = sb("lower", [P, P]), sb("lower_out", [P, P])
        small = sb("small", [NE, 4])
        eaw_sb, eaw_e, eawT = sb("eaw_sb", [NE, NA]), sb("eaw_e", [NE, NA]), sb("eawT", [NA, NE])
        atoms_sb, imp_sb = sb("atoms_sb", [NA, NS]), sb("imp_sb", [NE, NS])
        gate_sb = sb("gate_sb", [NE, DM])
        w_sb, wT = sb("w_sb", [P, TT, DM]), sb("wT", [P, C, DM])
        fill_sb = sb("fill_sb", [P, 2, DM * NE])

        s_const_step, s_const = sem("consts_step"), sem("consts_ready")
        s_idx_in, s_eaw_in, s_gate_in = sem("idx_loaded"), sem("mixture_loaded"), sem("gate_loaded")
        s_imp_in, s_w_in, s_atoms_in = sem("importance_loaded"), sem("w_ffn_loaded"), sem("atoms_loaded")
        s_fill, s_fill_out = sem("fill_ready"), [sem("fill_even_stored"), sem("fill_odd_stored")]
        s_chain = sem("dve_chain")
        s_max, s_exp, s_mix, s_mixT_pe, s_mixT = (sem("mixture_max"), sem("mixture_exp"), sem("mixture_ready"),
                                                  sem("mixture_turned"), sem("mixtureT_ready"))
        s_wT_pe, s_wT = sem("w_ffn_turned"), sem("w_ffnT_ready")
        s_impT, s_imp_e, s_mixed, s_entry = (sem("importance_turned"), sem("importance_exp"), sem("atoms_mixed"),
                                             sem("entries_ready"))
        s_gap, s_idx_row, s_same, s_sum = (sem("indices_ready"), sem("index_rows_ready"), sem("equal_indices_ready"),
                                           sem("entry_sums_ready"))
        block = ctx.enter_context(nc.Block())

        @block.sync
        def _(sp):
            sp.dma_start(w_sb[:], w_ffn.rearrange("(t p) d -> p t d", p=P)).then_inc(s_w_in, 16)
            sp.dma_start(atoms_sb[:], atoms).then_inc(s_atoms_in, 16)
            sp.dma_start(imp_sb[:], importance).then_inc(s_imp_in, 16)
            for c in range(C):
                sp.wait_ge(s_fill, c + 1)
                sp.dma_start(d_dram[c * P * DM:(c + 1) * P * DM, :].rearrange("(p r) e -> p (r e)", p=P),
                             fill_sb[:, c % 2]).then_inc(s_fill_out[c % 2], 16)
            sp.wait_ge(s_fill_out[0], 32)
            sp.wait_ge(s_fill_out[1], 32)

        @block.gpsimd
        def _(pool):
            pool.dma_start(idx_i[:], mask_idx.rearrange("(p j) -> p j", p=P)).then_inc(s_idx_in, 16)
            pool.dma_start(eaw_sb[:], eaw).then_inc(s_eaw_in, 16)
            pool.dma_start(gate_sb[:], gate_w).then_inc(s_gate_in, 16)
            pool.memset(ident[:], 0.0).then_inc(s_const_step, 1)
            pool.memset(causal_bf[:], 0.0).then_inc(s_const_step, 1)
            pool.memset(lower[:], 1.0).then_inc(s_const_step, 1)
            pool.wait_ge(s_const_step, 3)
            pool.affine_select(out=ident[:], in_=ident[:], compare_op=ALU.not_equal, fill=1.0, base=0,
                               pattern=[[-1, P]], channel_multiplier=1).then_inc(s_const, 1)
            pool.affine_select(out=causal_bf[:], in_=causal_bf[:], compare_op=ALU.is_ge, fill=MASKED, base=0,
                               pattern=[[-1, P]], channel_multiplier=1).then_inc(s_const, 1)
            pool.affine_select(out=lower[:], in_=lower[:], compare_op=ALU.is_gt, fill=0.0, base=0,
                               pattern=[[-1, P]], channel_multiplier=1).then_inc(s_const, 1)
            pool.iota(spare_i[:], pattern=[[0, 1]], base=DM * DM, channel_multiplier=1).then_inc(s_const, 1)
            pool.wait_ge(s_const, 4)
            pool.tensor_copy(ident_bf[:], ident[:]).then_inc(s_const, 1)
            for c in range(C):
                pool.wait_ge(s_wT, c + 1)
                if c >= 2:
                    pool.wait_ge(s_fill_out[c % 2], 16)
                pool_round(pool, fill_sb[:, c % 2].rearrange("p (r e) -> p r e", e=NE),
                                 wT[:, c, :].unsqueeze(2).broadcast_to([P, DM, NE])).then_inc(s_fill, 1)

        @block.tensor
        def _(pe):
            pe.wait_ge(s_const, 5)
            pe.wait_ge(s_w_in, 16)
            for c in range(C):
                for t in range(TT):
                    last = pe.transpose(psum[:, c, t * P:(t + 1) * P], w_sb[:, t, c * P:(c + 1) * P], ident[:])
                last.then_inc(s_wT_pe, 1)
            pe.wait_ge(s_gate_in, 16)
            for c in range(C):
                pe.transpose(psum[:, 5, c * NE:(c + 1) * NE], gate_sb[:, c * P:(c + 1) * P], ident[0:NE, 0:NE])
            pe.wait_ge(s_mix, 1)
            pe.transpose(psum[0:NA, 5, 64:64 + NE], eaw_e[:], ident[0:NE, 0:NE]).then_inc(s_mixT_pe, 1)
            pe.wait_ge(s_imp_in, 16)
            for j in range(NJ):
                last = pe.transpose(psum[:, 4, j * NE:(j + 1) * NE], imp_sb[:, j:NS:NJ], ident[0:NE, 0:NE])
            last.then_inc(s_impT, 1)
            pe.wait_ge(s_atoms_in, 16)
            pe.wait_ge(s_mixT, 2)
            for j in range(NJ):
                last = pe.matmul(psum[:, 6, j * NE:(j + 1) * NE], atoms_sb[:, j:NS:NJ], eawT[:], start=True, stop=True)
            last.then_inc(s_mixed, 1)
            pe.wait_ge(s_gap, 1)
            pe.wait_ge(s_entry, 1)
            pe.wait_ge(s_wT, C)
            for j in range(NJ):
                if j >= 2:
                    pe.wait_ge(s_same, j - 1)
                pe.transpose(psum[:, (5, 7)[j % 2], 0:P], idx_f[:, j:j + 1].broadcast_to([P, P]), ident[:]).then_inc(s_idx_row, 1)
                if j:
                    pe.wait_ge(s_same, j)
                    pe.matmul(psum[:, 0, (j - 1) * NE:j * NE], same[:, (j - 1) % 2, :], entry[:, j - 1, :],
                              start=True, stop=True).then_inc(s_sum, 1)
            pe.wait_ge(s_same, NJ)
            pe.matmul(psum[:, 0, (NJ - 1) * NE:NJ * NE], same[:, (NJ - 1) % 2, :], entry[:, NJ - 1, :],
                      start=True, stop=True).then_inc(s_sum, 1)

        @block.scalar
        def _(act):
            act.wait_ge(s_max, 1)
            act.activation(eaw_e[:], eaw_sb[:], ACT.Exp, bias=small[:, 0:1], accum_out=small[:, 1:2]).then_inc(s_exp, 1)
            act.wait_ge(s_impT, 1)
            act.activation(entry[:].rearrange("p j e -> p (j e)"), psum[:, 4, 0:NJ * NE], ACT.Exp,
                           scale=-1.0).then_inc(s_imp_e, 1)

        @block.vector
        def _(dve):
            chain = 0

            def after(ins):
                nonlocal chain
                chain += 1
                ins.then_inc(s_chain, 1)
                dve.wait_ge(s_chain, chain)

            dve.wait_ge(s_eaw_in, 16)
            dve.tensor_reduce(small[:, 0:1], eaw_sb[:], AX.X, ALU.max, negate=True).then_inc(s_max, 1)
            dve.wait_ge(s_idx_in, 16)
            dve.tensor_copy(idx_f[:], idx_i[:])
            dve.tensor_scalar(idx_r_i[:], idx_i[:], SHIFT, None, ALU.logical_shift_right)
            after(dve.tensor_scalar(idx_c_i[:], idx_i[:], DM - 1, SHIFT, ALU.bitwise_and, ALU.logical_shift_left))
            dve.wait_ge(s_exp, 1)
            after(dve.reciprocal(small[:, 2:3], small[:, 1:2]))
            dve.tensor_scalar(eaw_e[:], eaw_e[:], small[:, 2:3], None, ALU.mult).then_inc(s_mix, 1)
            after(dve.tensor_tensor(row_f[:], idx_r_i[:], idx_c_i[:], ALU.add))
            for c in range(C):
                dve.wait_ge(s_wT_pe, c + 1)
                dve.tensor_copy(wT[:, c], psum[:, c, :]).then_inc(s_wT, 1)
            dve.wait_ge(s_mixT_pe, 1)
            dve.tensor_copy(eawT[:], psum[0:NA, 5, 64:64 + NE]).then_inc(s_mixT, 1)
            dve.tensor_copy(gateT[:].rearrange("p c e -> p (c e)"), psum[:, 5, 0:C * NE]).then_inc(s_mixT, 1)
            dve.wait_ge(s_const, 4)
            after(dve.tensor_copy(spare_f[:], spare_i[:]))
            dve.tensor_scalar(gap_f[:], row_f[:], -1.0, spare_f[:, 0:1], ALU.mult, ALU.add).then_inc(s_gap, 1)
            flat = entry[:].rearrange("p j e -> p (j e)")
            dve.wait_ge(s_imp_e, 1)
            after(dve.tensor_scalar(flat, flat, 1.0, None, ALU.add))
            after(dve.reciprocal(flat, flat))
            dve.wait_ge(s_mixed, 1)
            dve.tensor_tensor(flat, psum[:, 6, 0:NJ * NE], flat, ALU.mult).then_inc(s_entry, 1)
            for j in range(NJ):
                dve.wait_ge(s_idx_row, j + 1)
                if j >= 2:
                    dve.wait_ge(s_sum, j - 1)
                dve.tensor_scalar(same[:, j % 2], psum[:, (5, 7)[j % 2], 0:P], idx_f[:, j:j + 1], None,
                                  ALU.is_equal).then_inc(s_same, 1)
                dve.wait_ge(s_same, j + 1)
                after(dve.tensor_tensor_reduce(lower_out[:], same[:, j % 2], lower[:], 1.0, 0.0, ALU.mult, ALU.add,
                                               dup[:, j:j + 1]))
            dve.wait_ge(s_gap, 1)
            after(dve.tensor_scalar(dup[:], dup[:], 1.0, None, ALU.min))
            after(dve.tensor_tensor(dup[:], dup[:], gap_f[:], ALU.mult))
            after(dve.tensor_tensor(dup[:], dup[:], row_f[:], ALU.add))
            after(dve.tensor_copy(row_i[:], dup[:]))
            dve.wait_ge(s_sum, NJ)
            after(dve.tensor_copy(entry_sum[:].rearrange("p j e -> p (j e)"), psum[:, 0, 0:NJ * NE]))


def wait_apart(eng, semaphore, count, passed):
    eng.wait_ge(semaphore, count)
    eng.sem_inc(passed, 1)


def pool_round(pool, out, in_):
    return pool.tensor_scalar(out, in_, 1.0, 1.0, ALU.mult, ALU.mult)


def run(eng, iteration):
    def batch(b, last_kind):
        with eng.Fori(0, HKV - 1) as g:
            iteration(b, g, b * HKV + g, "group")
        iteration(b, HKV - 1, b * HKV + HKV - 1, last_kind)

    with eng.Fori(0, NB - 1) as b:
        batch(b, "batch")
    batch(NB - 1, "end")


def attention(nc, sem, s_passed, psum, ident, ident_bf, causal_bf, row_i, entry_sum, x_rows, r_store, d_dram, wq_v, wk_v,
              wv_v, wo_v):
    with ExitStack() as ctx:
        def sb(name, shape, dt=F32):
            return ctx.enter_context(nc.sbuf_tensor(name, shape, dt))

        x_in = sb("x_in", [P, TT, DM])
        y_acc = sb("y_acc", [P, TT, DM])
        xT_hi, xT_lo = sb("xT_hi", [P, C, T], F32R), sb("xT_lo", [P, C, T], F32R)
        wo_raw = sb("wo_raw", [P, H, DM])
        wo_hi, wo_lo = sb("wo_hi", [P, G, DM], F32R), sb("wo_lo", [P, G, DM], F32R)
        wv_hi, wv_lo = sb("wv_hi", [P, C, HKV * HD], F32R), sb("wv_lo", [P, C, HKV * HD], F32R)
        w_raw = sb("w_raw", [P, 1 + G, C, HD])
        w_hi, w_lo = sb("w_hi", [P, 1 + G, C, HD], F32R), sb("w_lo", [P, 1 + G, C, HD], F32R)
        v_raw = sb("v_raw", [P, TT, HKV * HD])
        v_hi, v_lo = sb("v_hi", [P, TT, HD], F32R), sb("v_lo", [P, TT, HD], F32R)
        kT_hi, kT_lo = sb("kT_hi", [P, T], F32R), sb("kT_lo", [P, T], F32R)
        qT_hi, qT_lo = sb("qT_hi", [P, 2, T], F32R), sb("qT_lo", [P, 2, T], F32R)
        probs = sb("probs", [P, 2, PACK])
        pT_hi, pT_lo = sb("pT_hi", [P, PACK], F32R), sb("pT_lo", [P, PACK], F32R)
        oT_hi, oT_lo = sb("oT_hi", [P, G, T], F32R), sb("oT_lo", [P, G, T], F32R)
        neg_max = sb("neg_max", [P, 2, TT])
        row_sum = sb("row_sum", [P, 2, TT])
        row_inv = sb("row_inv", [P, 2, TT])
        row_now = sb("row_now", [P, 1], I32)
        entry_now = sb("entry_now", [P, NE])

        s_x_in = sem("x_loaded")
        s_w_in = [sem(f"weight_slot_{j}_loaded") for j in range(1 + G)]
        s_wo_in = sem("wo_loaded")
        s_wv_in = sem("wv_loaded")
        s_scatter = sem("entries_scattered")
        s_r_out = sem("residual_stored")
        s_w_split = sem("weight_slots_split")
        s_vg = sem("v_group_split")
        s_wo = sem("wo_heads_split")
        s_wv_hi, s_wv = sem("wv_hi_ready"), sem("wv_split")
        s_pool_step = sem("pool_step")
        s_seed = sem("y_seeded")
        s_norm = sem("probs_normalized")
        s_qk = sem("score_banks_ready")
        s_max = sem("score_maxima_ready")
        s_exp = sem("score_banks_exped")
        s_inv = sem("row_inv_ready")
        s_pt, s_pt_hi, s_pt_lo = sem("pT_units_ready"), sem("pT_hi_ready"), sem("pT_lo_ready")
        s_q, s_q_hi, s_q_lo = sem("qT_ready"), sem("qT_hi_ready"), sem("qT_lo_ready")
        s_k, s_k_hi, s_k_lo = sem("kT_ready"), sem("kT_hi_ready"), sem("kT_lo_ready")
        s_o, s_o_hi, s_o_lo = sem("oT_ready"), sem("oT_hi_ready"), sem("oT_lo_ready")
        s_xt, s_xt_hi, s_xt_lo = sem("xT_ready"), sem("xT_hi_ready"), sem("xT_lo_ready")
        s_v, s_v_raw = sem("v_ready"), sem("v_raw_ready")
        s_y, s_y_acc = sem("y_tiles_ready"), sem("y_tiles_added")
        s_entry = sem("entry_copied")
        block = ctx.enter_context(nc.Block())

        @block.sync
        def _(sp):
            sp.dma_start(x_in[:], x_rows[0]).then_inc(s_x_in, 16)

            def load_slot(j, g):
                src = wk_v[:, :, bass.ds(g * HD, HD)] if j == 0 else wq_v[:, :, bass.ds((g * G + j - 1) * HD, HD)]
                sp.dma_start(w_raw[:, j], src).then_inc(s_w_in[j], 16)

            for j in range(1 + G):
                load_slot(j, 0)
            sp.dma_start(wo_raw[:, 0:C, :], wv_v).then_inc(s_wv_in, 16)
            sp.wait_ge(s_wv, 1)
            sp.dma_start(wo_raw[:], wo_v).then_inc(s_wo_in, 16)

            def next_slots(it, g_next):
                for j in range(1 + G):
                    sp.wait_ge(s_w_split, (it + 1) * (1 + G) + j + 1)
                    load_slot(j, g_next)

            for j in range(1 + G):
                sp.wait_ge(s_w_split, j + 1)
                load_slot(j, 1)
            sp.wait_ge(s_seed, 1)
            sp.wait_ge(s_xt, C)
            sp.dma_start(x_in[:], x_rows[1]).then_inc(s_x_in, 16)

            def groups(b, last_batch):
                with sp.Fori(0, HKV - 2) as g:
                    next_slots(b * HKV + g, g + 2)
                if not last_batch:
                    next_slots(b * HKV + HKV - 2, 0)
                wait_apart(sp, s_y_acc, TT + (b * HKV + HKV) * TT, s_passed)
                sp.dma_start(r_store[bass.ds(b, 1)].rearrange("a p t d -> (a p) t d"), y_acc[:]).then_inc(s_r_out, 16)
                if not last_batch:
                    next_slots(b * HKV + HKV - 1, 1)

            with sp.Fori(0, NB - 2) as b:
                groups(b, False)
                wait_apart(sp, s_seed, b + 2, s_passed)
                wait_apart(sp, s_xt, (b + 2) * C, s_passed)
                sp.dma_start(x_in[:], x_rows[bass.ds(b + 2, 1)].rearrange("a p t d -> (a p) t d")).then_inc(s_x_in, 16)
            groups(NB - 2, False)
            groups(NB - 1, True)
            sp.wait_ge(s_r_out, 16 * NB)

        @block.gpsimd
        def _(pool):
            def split_slot(j, k):
                pool_round(pool, w_hi[:, j], w_raw[:, j]).then_inc(s_pool_step, 1)
                wait_apart(pool, s_pool_step, k + 1, s_passed)
                pool.tensor_tensor(w_lo[:, j], w_raw[:, j], w_hi[:, j].bitcast(F32), ALU.subtract).then_inc(s_w_split, 1)

            def split_v(g, k):
                src = v_raw[:, :, bass.ds(g * HD, HD)]
                pool.tensor_copy(v_hi[:], src).then_inc(s_pool_step, 1)
                wait_apart(pool, s_pool_step, k + 1, s_passed)
                pool.tensor_tensor(v_lo[:], src, v_hi[:].bitcast(F32), ALU.subtract).then_inc(s_vg, 1)

            def split_wo(g, h, k):
                src = wo_raw[:, bass.ds(g * G + h, 1), :].rearrange("p a n -> p (a n)")
                pool.tensor_copy(wo_hi[:, h], src).then_inc(s_pool_step, 1)
                wait_apart(pool, s_pool_step, k + 1, s_passed)
                pool.tensor_tensor(wo_lo[:, h], src, wo_hi[:, h].bitcast(F32), ALU.subtract).then_inc(s_wo, 1)

            def normalize(n, buf):
                wait_apart(pool, s_inv, n + 1, s_passed)
                for i in range(TT):
                    a = ROW_AT[i]
                    p = probs[:, buf, a:a + (i + 1) * P]
                    last = pool.tensor_scalar(p, p, row_inv[:, buf, i:i + 1], 1.0, ALU.mult, ALU.mult)
                last.then_inc(s_norm, 1)

            def slot(it_next, j, k):
                wait_apart(pool, s_w_in[j], 16 * (it_next + 1), s_passed)
                if j == 0:
                    wait_apart(pool, s_k, it_next, s_passed)
                else:
                    wait_apart(pool, s_q, (it_next - 1) * G + j, s_passed)
                split_slot(j, k)

            for j in range(1 + G):
                pool.wait_ge(s_w_in[j], 16)
                split_slot(j, j)
            pool.wait_ge(s_x_in, 16)
            pool_round(pool, y_acc[:], x_in[:]).then_inc(s_seed, 1)
            pool.wait_ge(s_v_raw, TT)
            split_v(0, 1 + G)
            pool.wait_ge(s_wo_in, 16)
            normalize(0, 0)
            SETUP_STEPS = 1 + G + 1
            STEPS = 1 + G + 1 + G

            def iteration(b, g, it, kind):
                k0 = SETUP_STEPS + it * STEPS
                n0 = it * G
                k = 0
                has_next = kind != "end"
                if has_next:
                    slot(it + 1, 0, k0)
                    k = 1
                normalize(n0 + 1, 1)
                split_wo(g, 0, k0 + k)
                k += 1
                if has_next:
                    slot(it + 1, 1, k0 + k)
                    k += 1
                normalize(n0 + 2, 0)
                split_wo(g, 1, k0 + k)
                k += 1
                if has_next:
                    slot(it + 1, 2, k0 + k)
                    k += 1
                normalize(n0 + 3, 1)
                split_wo(g, 2, k0 + k)
                split_wo(g, 3, k0 + k + 1)
                k += 2
                wait_apart(pool, s_scatter, 16 * (it + 1), s_passed)
                pool.tensor_copy(row_now[:], row_i[:, bass.ds(it, 1)]).then_inc(s_entry, 1)
                pool.tensor_copy(entry_now[:], entry_sum[:, bass.ds(it, 1), :].rearrange("p a e -> p (a e)")).then_inc(s_entry, 1)
                wait_apart(pool, s_entry, 2 * it + 2, s_passed)
                pool.indirect_dma_start(out=d_dram, out_offset=bass.IndirectOffsetOnAxis(ap=row_now[:, 0:1], axis=0),
                                        in_=entry_now[:], in_offset=None, compute_op=ALU.add).then_inc(s_scatter, 16)
                if has_next:
                    slot(it + 1, 3, k0 + k)
                    k += 1
                    normalize(n0 + 4, 0)
                if kind == "group":
                    wait_apart(pool, s_o, n0 + G, s_passed)
                    split_v(g + 1, k0 + k)
                    k += 1
                if has_next:
                    slot(it + 1, 4, k0 + k)
                    k += 1
                if kind == "batch":
                    wait_apart(pool, s_x_in, 16 * (b + 2), s_passed)
                    wait_apart(pool, s_r_out, 16 * (b + 1), s_passed)
                    pool_round(pool, y_acc[:], x_in[:]).then_inc(s_seed, 1)
                    wait_apart(pool, s_v_raw, (b + 2) * TT, s_passed)
                    split_v(0, k0 + k)

            pool.dma_start(d_dram[DM * DM:DM * DM + P, :], entry_sum[:, 0, :]).then_inc(s_scatter, 16)
            run(pool, iteration)
            pool.wait_ge(s_scatter, 16 * (NIT + 1))

        @block.tensor
        def _(pe):
            def three(dst, hi_s, lo_s, hi_m, lo_m, start, stop, skip=False):
                pe.matmul(dst, hi_s, hi_m, start=start, stop=False)
                pe.matmul(dst, hi_s, lo_m, start=False, stop=False)
                return pe.matmul(dst, lo_s, hi_m, start=False, stop=stop)

            def scores(n, buf, first=False):
                pe.wait_ge(s_q_lo, n + 1)
                for i, bank, col in ROWS:
                    w = (i + 1) * P
                    dst = psum[:, BANK_S + bank, col:col + w]
                    if not first and col == 0:
                        pe.wait_ge(s_exp, 3 * n - 3 + bank + 1)
                    q = (qT_hi[:, buf, i * P:(i + 1) * P], qT_lo[:, buf, i * P:(i + 1) * P])
                    three(dst, *q, kT_hi[:, 0:w], kT_lo[:, 0:w], True, False)
                    last = pe.matmul(dst[:, i * P:w], ident_bf[:], causal_bf[:], start=False, stop=True)
                    if i != 2:
                        last.then_inc(s_qk, 1)

            def transposes(n, buf, last_unit):
                if last_unit:
                    pe.wait_ge(s_pt_lo, 3 * n + 4)
                else:
                    pe.wait_ge(s_norm, n + 1)
                    pe.wait_ge(s_pt_lo, 3 * n + 3)
                for j, unit, col in KEYS:
                    if (unit == 2) != last_unit:
                        continue
                    for i in range(j, TT):
                        at = col + (i - j) * P
                        src = ROW_AT[i] + j * P
                        last = pe.transpose(psum[:, BANK_PT + unit % 2, at:at + P], probs[:, buf, src:src + P], ident[:])
                    if j != 1:
                        last.then_inc(s_pt, 1)

            def values(n, first_of_group, it):
                if first_of_group:
                    pe.wait_ge(s_vg, it + 1)
                    pe.wait_ge(s_y_acc, it * TT + TT)
                else:
                    pe.wait_ge(s_o_lo, n)
                for j, unit, _ in KEYS:
                    if j != 3:
                        pe.wait_ge(s_pt_lo, 3 * n + 3 + unit + 1)
                    a, w = KEY_AT[j], T - j * P
                    last = three(psum[:, BANK_B, j * P:T], v_hi[:, j], v_lo[:, j], pT_hi[:, a:a + w], pT_lo[:, a:a + w],
                                 j == 0, j == KEYS[-1][0])
                last.then_inc(s_o, 1)

            def project(slot, done):
                for c in range(C):
                    last = three(psum[:, BANK_A, :], w_hi[:, slot, c], w_lo[:, slot, c], xT_hi[:, c], xT_lo[:, c],
                                 c == 0, c == C - 1)
                last.then_inc(done, 1)

            def query(n, h, it):
                pe.wait_ge(s_w_split, it * (1 + G) + h + 2)
                if h == 0:
                    pe.wait_ge(s_k_lo, it + 1)
                else:
                    pe.wait_ge(s_q_lo, n)
                project(1 + h, s_q)

            def key(it):
                pe.wait_ge(s_w_split, it * (1 + G) + 1)
                project(0, s_k)

            def turn_x(b, first):
                pe.wait_ge(s_x_in, 16 * (b + 1))
                if not first:
                    pe.wait_ge(s_q_lo, b * HKV * G)
                    pe.wait_ge(s_y_acc, TT + (b * HKV - 1) * TT)
                for c in range(C):
                    if c >= 2:
                        pe.wait_ge(s_xt_lo, b * C + c - 1)
                    for t in range(TT):
                        last = pe.transpose(psum[:, (BANK_A, BANK_C)[c % 2], t * P:(t + 1) * P],
                                            x_in[:, t, c * P:(c + 1) * P], ident[:])
                    last.then_inc(s_xt, 1)

            def value_rows(b, first):
                for t in range(TT):
                    if t >= 2:
                        pe.wait_ge(s_v_raw, b * TT + t - 1)
                    elif not first:
                        pe.wait_ge(s_y_acc, TT + b * HKV * TT - 1 + t)
                    for c in range(C):
                        last = three(psum[:, (BANK_C, BANK_B)[t % 2], :], xT_hi[:, c, t * P:(t + 1) * P],
                                     xT_lo[:, c, t * P:(t + 1) * P], wv_hi[:, c], wv_lo[:, c], c == 0, c == C - 1)
                    last.then_inc(s_v, 1)

            def out_rows(t, it):
                if t == 0:
                    pe.wait_ge(s_o_lo, (it + 1) * G)
                    pe.wait_ge(s_wo, (it + 1) * G)
                if t != 1:
                    pe.wait_ge(s_y_acc, TT + it * TT + t - 1)
                for h in range(G):
                    last = three(psum[:, (BANK_C, BANK_B)[t % 2], :], oT_hi[:, h, t * P:(t + 1) * P],
                                 oT_lo[:, h, t * P:(t + 1) * P], wo_hi[:, h], wo_lo[:, h], h == 0, h == G - 1)
                last.then_inc(s_y, 1)

            turn_x(0, True)
            pe.wait_ge(s_xt_lo, C)
            key(0)
            query(0, 0, 0)
            scores(0, 0, True)
            query(1, 1, 0)
            pe.wait_ge(s_wv, 2)
            value_rows(0, True)

            def iteration(b, g, it, kind):
                n = it * G
                scores(n + 1, 1)
                transposes(n, 0, False)
                query(n + 2, 2, it)
                transposes(n, 0, True)
                values(n, True, it)
                scores(n + 2, 0)
                transposes(n + 1, 1, False)
                query(n + 3, 3, it)
                transposes(n + 1, 1, True)
                values(n + 1, False, it)
                scores(n + 3, 1)
                transposes(n + 2, 0, False)
                if kind == "batch":
                    turn_x(b + 1, False)
                    transposes(n + 2, 0, True)
                    values(n + 2, False, it)
                    pe.wait_ge(s_xt_lo, (b + 2) * C)
                    key(it + 1)
                elif kind == "group":
                    pe.wait_ge(s_q_lo, n + 4)
                    key(it + 1)
                    transposes(n + 2, 0, True)
                    values(n + 2, False, it)
                else:
                    transposes(n + 2, 0, True)
                    values(n + 2, False, it)
                transposes(n + 3, 1, False)
                if kind != "end":
                    query(n + 4, 0, it + 1)
                transposes(n + 3, 1, True)
                values(n + 3, False, it)
                if kind != "end":
                    scores(n + 4, 0)
                out_rows(0, it)
                out_rows(1, it)
                if kind != "end":
                    query(n + 5, 1, it + 1)
                out_rows(2, it)
                out_rows(3, it)
                if kind == "batch":
                    value_rows(b + 1, False)

            run(pe, iteration)

        @block.scalar
        def _(act):
            def exps(n, buf):
                for i, bank, col in ROWS:
                    if i != 0:
                        act.wait_ge(s_max, 3 * n + bank + 1)
                    w, a = (i + 1) * P, ROW_AT[i]
                    last = act.activation(probs[:, buf, a:a + w], psum[:, BANK_S + bank, col:col + w], ACT.Exp,
                                          bias=neg_max[:, buf, i:i + 1],
                                          accum_out=row_sum[:, buf, i:i + 1])
                    if i != 2:
                        last.then_inc(s_exp, 1)

            def pT(n, units):
                for u in units:
                    a, z = UNIT[u]
                    act.wait_ge(s_pt, 3 * n + u + 1)
                    act.copy(pT_hi[:, a:z], psum[:, BANK_PT + u % 2, 0:z - a]).then_inc(s_pt_hi, 1)

            def qT(n, buf):
                act.wait_ge(s_q, n + 1)
                act.mul(qT_hi[:, buf], psum[:, BANK_A, :], SCALE).then_inc(s_q_hi, 1)

            def kT(it):
                act.wait_ge(s_k, it + 1)
                act.copy(kT_hi[:], psum[:, BANK_A, :]).then_inc(s_k_hi, 1)

            def oT(n, h):
                act.wait_ge(s_o, n + 1)
                act.copy(oT_hi[:, h], psum[:, BANK_B, :]).then_inc(s_o_hi, 1)

            def xT(b):
                for c in range(C):
                    act.wait_ge(s_xt, b * C + c + 1)
                    act.copy(xT_hi[:, c], psum[:, (BANK_A, BANK_C)[c % 2], :]).then_inc(s_xt_hi, 1)

            def v(b):
                for t in range(TT):
                    act.wait_ge(s_v, b * TT + t + 1)
                    act.copy(v_raw[:, t], psum[:, (BANK_C, BANK_B)[t % 2], :]).then_inc(s_v_raw, 1)

            xT(0)
            kT(0)
            qT(0, 0)
            exps(0, 0)
            qT(1, 1)
            act.wait_ge(s_wv_in, 16)
            act.copy(wv_hi[:], wo_raw[:, 0:C, :]).then_inc(s_wv_hi, 1)
            v(0)

            def iteration(b, g, it, kind):
                n = it * G
                exps(n + 1, 1)
                pT(n, (0, 1))
                pT(n, (2,))
                qT(n + 2, 0)
                oT(n, 0)
                exps(n + 2, 0)
                pT(n + 1, (0, 1))
                pT(n + 1, (2,))
                qT(n + 3, 1)
                oT(n + 1, 1)
                exps(n + 3, 1)
                pT(n + 2, (0, 1))
                if kind == "batch":
                    xT(b + 1)
                if kind == "group":
                    kT(it + 1)
                pT(n + 2, (2,))
                oT(n + 2, 2)
                if kind == "batch":
                    kT(it + 1)
                pT(n + 3, (0, 1))
                if kind != "end":
                    qT(n + 4, 0)
                pT(n + 3, (2,))
                oT(n + 3, 3)
                if kind != "end":
                    exps(n + 4, 0)
                    qT(n + 5, 1)
                if kind == "batch":
                    v(b + 1)

            run(act, iteration)

        @block.vector
        def _(dve):
            def maxima(n, buf):
                for i, bank, col in ROWS:
                    if i != 0:
                        dve.wait_ge(s_qk, 3 * n + bank + 1)
                    last = dve.tensor_reduce(neg_max[:, buf, i:i + 1], psum[:, BANK_S + bank, col:col + (i + 1) * P],
                                             AX.X, ALU.max, negate=True)
                    if i != 2:
                        last.then_inc(s_max, 1)

            def inverse(n, buf):
                dve.wait_ge(s_exp, 3 * n + 3)
                dve.reciprocal(row_inv[:, buf], row_sum[:, buf]).then_inc(s_inv, 1)

            def softmax(n, buf):
                maxima(n, buf)
                inverse(n, buf)

            def low(lo, hi, src, done):
                dve.tensor_tensor(lo, src, hi.bitcast(F32), ALU.subtract).then_inc(done, 1)

            def pT(n, units):
                for u in units:
                    a, z = UNIT[u]
                    dve.wait_ge(s_pt_hi, 3 * n + u + 1)
                    low(pT_lo[:, a:z], pT_hi[:, a:z], psum[:, BANK_PT + u % 2, 0:z - a], s_pt_lo)

            def qT(n, buf):
                dve.wait_ge(s_q_hi, n + 1)
                dve.scalar_tensor_tensor(out=qT_lo[:, buf], in0=psum[:, BANK_A, :], scalar=SCALE,
                                         in1=qT_hi[:, buf].bitcast(F32), op0=ALU.mult, op1=ALU.subtract).then_inc(s_q_lo, 1)

            def kT(it):
                dve.wait_ge(s_k_hi, it + 1)
                low(kT_lo[:], kT_hi[:], psum[:, BANK_A, :], s_k_lo)

            def oT(n, h):
                dve.wait_ge(s_o_hi, n + 1)
                low(oT_lo[:, h], oT_hi[:, h], psum[:, BANK_B, :], s_o_lo)

            def xT(b):
                for c in range(C):
                    dve.wait_ge(s_xt_hi, b * C + c + 1)
                    low(xT_lo[:, c], xT_hi[:, c], psum[:, (BANK_A, BANK_C)[c % 2], :], s_xt_lo)

            def add_rows(it, t):
                dve.wait_ge(s_y, it * TT + t + 1)
                dve.tensor_tensor(y_acc[:, t], psum[:, (BANK_C, BANK_B)[t % 2], :], y_acc[:, t], ALU.add).then_inc(s_y_acc, 1)

            dve.memset(neg_max[:], 0.0).then_inc(s_pt_lo, 3)
            dve.memset(row_inv[:], 0.0).then_inc(s_y_acc, TT)
            xT(0)
            kT(0)
            qT(0, 0)
            softmax(0, 0)
            qT(1, 1)
            dve.wait_ge(s_wv_hi, 1)
            dve.tensor_tensor(wv_lo[:], wo_raw[:, 0:C, :], wv_hi[:].bitcast(F32), ALU.subtract).then_inc(s_wv, 2)

            def iteration(b, g, it, kind):
                n = it * G
                softmax(n + 1, 1)
                pT(n, (0, 1))
                pT(n, (2,))
                qT(n + 2, 0)
                oT(n, 0)
                softmax(n + 2, 0)
                pT(n + 1, (0, 1))
                pT(n + 1, (2,))
                qT(n + 3, 1)
                oT(n + 1, 1)
                softmax(n + 3, 1)
                pT(n + 2, (0, 1))
                if kind == "batch":
                    xT(b + 1)
                if kind == "group":
                    kT(it + 1)
                pT(n + 2, (2,))
                oT(n + 2, 2)
                if kind == "batch":
                    kT(it + 1)
                pT(n + 3, (0, 1))
                if kind != "end":
                    qT(n + 4, 0)
                pT(n + 3, (2,))
                oT(n + 3, 3)
                if kind != "end":
                    softmax(n + 4, 0)
                add_rows(it, 0)
                add_rows(it, 1)
                if kind != "end":
                    qT(n + 5, 1)
                add_rows(it, 2)
                add_rows(it, 3)

            run(dve, iteration)


def experts(nc, sem, s_passed, psum, ident, gateT, r_dram, d_dram, out_rows):
    with ExitStack() as ctx:
        def sb(name, shape, dt=F32):
            return ctx.enter_context(nc.sbuf_tensor(name, shape, dt))

        stage = sb("stage", [P, 2, DM * NE])
        d_hi, d_lo = sb("d_hi", [P, C, NE, DM], F32R), sb("d_lo", [P, C, NE, DM], F32R)
        r_in, x1, y_out = sb("r_in", [P, 2, DM]), sb("x1", [P, 2, DM]), sb("y_out", [P, 2, DM])
        z = sb("z", [P, DM])
        x1T = sb("x1T", [P, C, P])
        x1T_hi, x1T_lo = sb("x1T_hi", [P, 2, C, P], F32R), sb("x1T_lo", [P, 2, C, P], F32R)
        stats, mean_var, std = sb("stats", [P, 6]), sb("mean_var", [P, 2]), sb("std", [P, 2])
        logits, best, best_at = sb("logits", [P, NE]), sb("best", [P, 8]), sb("best_at", [P, 8], U32)
        best_f, gap, share = sb("best_f", [P, 2]), sb("gap", [P, 2]), sb("share", [P, 2])
        number_i, number = sb("number_i", [P, NE], I32), sb("number", [P, NE])
        is_second, weight = sb("is_second", [P, NE]), sb("weight", [P, 2, NE])

        s_d_in = [sem("d_even_loaded"), sem("d_odd_loaded")]
        s_d_hi, s_d_lo, s_d_lo_pool = sem("d_hi_ready"), sem("d_lo_ready"), sem("d_lo_pool_ready")
        s_number_i = sem("numbers_ready")
        s_r_in = [sem("r_even_loaded"), sem("r_odd_loaded")]
        s_x1, s_x1T_pe, s_x1T, s_x1T_hi, s_x1T_lo = (sem("x1_ready"), sem("x1_turned"), sem("x1T_ready"),
                                                     sem("x1T_hi_ready"), sem("x1T_lo_ready"))
        s_logits, s_var, s_std = sem("logits_ready"), sem("variances_ready"), sem("std_ready")
        s_gap, s_gap_e = sem("gate_gap_ready"), sem("gate_gap_exp")
        s_weight = sem("expert_shares_ready")
        s_out_e, s_added = sem("expert_outputs_ready"), sem("expert_outputs_added")
        s_y, s_y_out = sem("y_ready"), [sem("y_even_stored"), sem("y_odd_stored")]
        s_chain = sem("dve_chain_experts")
        block = ctx.enter_context(nc.Block())
        DVE_E = 5

        def by_expert(c, e):
            return stage[:, c % 2].rearrange("p (r e) -> p e r", e=NE)[:, e]

        @block.sync
        def _(sp):
            for k in range(2):
                sp.dma_start(r_in[:, k], r_dram[k]).then_inc(s_r_in[k], 16)
            for c in range(C):
                if c >= 2:
                    sp.wait_ge(s_d_lo, DVE_E * (c - 1))
                    sp.wait_ge(s_d_lo_pool, (NE - DVE_E) * (c - 1))
                sp.dma_start(stage[:, c % 2], d_dram[c * P * DM:(c + 1) * P * DM, :].rearrange("(p r) e -> p (r e)", p=P)
                             ).then_inc(s_d_in[c % 2], 16)
            with sp.Fori(0, NT // 2 - 1) as i:
                for k in range(2):
                    wait_apart(sp, s_x1, 2 * i + k + 1, s_passed)
                    sp.dma_start(r_in[:, k], r_dram[bass.ds(2 * i + 2 + k, 1)].rearrange("a p d -> (a p) d")
                                 ).then_inc(s_r_in[k], 16)

        @block.gpsimd
        def _(pool):
            pool.iota(number_i[:], pattern=[[1, NE]], base=0, channel_multiplier=0).then_inc(s_number_i, 1)
            for c in range(C):
                for e in range(DVE_E, NE):
                    pool.wait_ge(s_d_hi, c * NE + e + 1)
                    pool.tensor_tensor(d_lo[:, c, e], by_expert(c, e), d_hi[:, c, e].bitcast(F32),
                                       ALU.subtract).then_inc(s_d_lo_pool, 1)

        @block.tensor
        def _(pe):
            def turn_and_gate(t, buf):
                pe.wait_ge(s_x1, t + 1)
                for c in range(C):
                    last = pe.transpose(psum[:, 0, c * P:(c + 1) * P], x1[:, buf, c * P:(c + 1) * P], ident[:])
                last.then_inc(s_x1T_pe, 1)
                pe.wait_ge(s_x1T, t + 1)
                for c in range(C):
                    last = pe.matmul(psum[:, 1, 0:NE], x1T[:, c], gateT[:, c], start=c == 0, stop=c == C - 1)
                last.then_inc(s_logits, 1)

            def expert_outputs(t, buf):
                pe.wait_ge(s_x1T_lo, t + 1)
                for e in range(NE):
                    dst = psum[:, 2 + e % 4, :]
                    pe.wait_ge(s_added, t * NE + e + 1)
                    for c in range(C):
                        pe.matmul(dst, x1T_hi[:, buf, c], d_hi[:, c, e], start=c == 0, stop=False)
                        pe.matmul(dst, x1T_hi[:, buf, c], d_lo[:, c, e], start=False, stop=False)
                        last = pe.matmul(dst, x1T_lo[:, buf, c], d_hi[:, c, e], start=False, stop=c == C - 1)
                    last.then_inc(s_out_e, 1)

            turn_and_gate(0, 0)
            pe.wait_ge(s_d_lo, DVE_E * C)
            pe.wait_ge(s_d_lo_pool, (NE - DVE_E) * C)
            with pe.Fori(0, NT // 2 - 1) as i:
                turn_and_gate(2 * i + 1, 1)
                expert_outputs(2 * i, 0)
                turn_and_gate(2 * i + 2, 0)
                expert_outputs(2 * i + 1, 1)
            turn_and_gate(NT - 1, 1)
            expert_outputs(NT - 2, 0)
            expert_outputs(NT - 1, 1)

        @block.scalar
        def _(act):
            def std_of(norm):
                act.wait_ge(s_var, norm + 1)
                act.activation(std[:, 0:1], std[:, 1:2], ACT.Sqrt).then_inc(s_std, 1)

            def turned(t, buf):
                act.wait_ge(s_x1T_pe, t + 1)
                act.copy(x1T[:].rearrange("p c n -> p (c n)"), psum[:, 0, :]).then_inc(s_x1T, 1)
                act.wait_ge(s_x1T, t + 1)
                act.copy(x1T_hi[:, buf], x1T[:]).then_inc(s_x1T_hi, 1)
                act.wait_ge(s_gap, t + 1)
                act.activation(gap[:, 1:2], gap[:, 0:1], ACT.Exp).then_inc(s_gap_e, 1)

            def store(t, buf, row):
                act.wait_ge(s_y, t + 1)
                act.dma_start(row, y_out[:, buf]).then_inc(s_y_out[buf], 16)

            def tile(t, buf):
                std_of(2 * t + 1)
                turned(t + 1, 1 - buf)
                std_of(2 * t + 2)
                store(t, buf, out_rows[bass.ds(t, 1)].rearrange("a p d -> (a p) d"))

            std_of(0)
            turned(0, 0)
            for c in range(C):
                act.wait_ge(s_d_in[c % 2], 16 * (c // 2 + 1))
                for e in range(NE):
                    act.copy(d_hi[:, c, e], by_expert(c, e)).then_inc(s_d_hi, 1)
            with act.Fori(0, NT // 2 - 1) as i:
                tile(2 * i, 0)
                tile(2 * i + 1, 1)
            std_of(2 * NT - 3)
            turned(NT - 1, 1)
            std_of(2 * NT - 2)
            store(NT - 2, 0, out_rows[NT - 2])
            std_of(2 * NT - 1)
            store(NT - 1, 1, out_rows[NT - 1])
            for k in range(2):
                act.wait_ge(s_y_out[k], 16 * (NT // 2 + 1))

        @block.vector
        def _(dve):
            FIRST, SECOND = 11, 3

            def after(ins, count):
                ins.then_inc(s_chain, 1)
                wait_apart(dve, s_chain, count, s_passed)

            def layer_norm(dst, src, chain, norm):
                after(dve.bn_stats(stats[:], src), chain + 1)
                after(dve.bn_aggr(mean_var[:], stats[:]), chain + 2)
                dve.tensor_scalar(std[:, 1:2], mean_var[:, 1:2], EPS, None, ALU.add).then_inc(s_var, 1)
                dve.wait_ge(s_std, norm + 1)
                after(dve.reciprocal(std[:, 1:2], std[:, 0:1]), chain + 3)
                return dve.tensor_scalar(dst, src, mean_var[:, 0:1], std[:, 1:2], ALU.subtract, ALU.mult)

            def first(t, buf, chain, norm, loaded):
                dve.wait_ge(s_r_in[buf], loaded)
                layer_norm(x1[:, buf], r_in[:, buf], chain, norm).then_inc(s_x1, 1)
                dve.wait_ge(s_x1T_hi, t + 1)
                dve.tensor_tensor(x1T_lo[:, buf], x1T[:], x1T_hi[:, buf].bitcast(F32), ALU.subtract).then_inc(s_x1T_lo, 1)
                dve.wait_ge(s_logits, t + 1)
                after(dve.tensor_scalar(logits[:], psum[:, 1, 0:NE], 50.0, -50.0, ALU.min, ALU.max), chain + 4)
                after(dve.max(best[:], logits[:]), chain + 5)
                dve.tensor_tensor(gap[:, 0:1], best[:, 1:2], best[:, 0:1], ALU.subtract).then_inc(s_gap, 1)
                after(dve.max_index(best_at[:], best[:], logits[:]), chain + 6)
                after(dve.tensor_copy(best_f[:], best_at[:, 0:2]), chain + 7)
                dve.wait_ge(s_gap_e, t + 1)
                after(dve.tensor_scalar(share[:, 0:1], gap[:, 1:2], 1.0, None, ALU.add), chain + 8)
                after(dve.reciprocal(share[:, 0:1], share[:, 0:1]), chain + 9)
                after(dve.tensor_tensor(share[:, 1:2], share[:, 0:1], gap[:, 1:2], ALU.mult), chain + 10)
                dve.tensor_scalar(weight[:, buf], number[:], best_f[:, 0:1], share[:, 0:1], ALU.is_equal, ALU.mult)
                after(dve.tensor_scalar(is_second[:], number[:], best_f[:, 1:2], share[:, 1:2], ALU.is_equal, ALU.mult),
                      chain + 11)
                dve.tensor_tensor(weight[:, buf], weight[:, buf], is_second[:], ALU.add).then_inc(s_weight, 1)

            def second(t, buf, chain, norm, stored):
                dve.wait_ge(s_weight, t + 1)
                for e in range(NE):
                    dve.wait_ge(s_out_e, t * NE + e + 1)
                    if e:
                        dve.wait_ge(s_added, 4 + t * NE + e)
                    dve.scalar_tensor_tensor(out=z[:], in0=psum[:, 2 + e % 4, :], scalar=weight[:, buf, e:e + 1],
                                             in1=x1[:, buf] if e == 0 else z[:], op0=ALU.mult, op1=ALU.add
                                             ).then_inc(s_added, 1)
                dve.wait_ge(s_added, 4 + (t + 1) * NE)
                dve.wait_ge(s_y_out[buf], stored)
                layer_norm(y_out[:, buf], z[:], chain, norm).then_inc(s_y, 1)

            dve.memset(z[:], 0.0).then_inc(s_added, 4)
            for k in range(2):
                dve.memset(y_out[:, k], 0.0).then_inc(s_y_out[k], 16)
            dve.wait_ge(s_number_i, 1)
            dve.tensor_copy(number[:], number_i[:])
            first(0, 0, 0, 0, 16)
            for c in range(C):
                for e in range(DVE_E):
                    dve.wait_ge(s_d_hi, c * NE + e + 1)
                    dve.tensor_tensor(d_lo[:, c, e], by_expert(c, e), d_hi[:, c, e].bitcast(F32),
                                      ALU.subtract).then_inc(s_d_lo, 1)
            with dve.Fori(0, NT // 2 - 1) as i:
                for k in range(2):
                    t = 2 * i + k
                    chain = FIRST + t * (FIRST + SECOND)
                    first(t + 1, 1 - k, chain, 2 * t + 1, 16 * (i + 1 + k))
                    second(t, k, chain + FIRST, 2 * t + 2, 16 * (i + 1))
            t, chain = NT - 2, FIRST + (NT - 2) * (FIRST + SECOND)
            first(t + 1, 1, chain, 2 * t + 1, 16 * (NT // 2))
            second(t, 0, chain + FIRST, 2 * t + 2, 16 * (NT // 2))
            dve.wait_ge(s_y, NT - 1)
            second(t + 1, 1, chain + FIRST + SECOND, 2 * t + 3, 16 * (NT // 2))


_INS = ['L0_attn_x', 'L0_attn_wq', 'L0_attn_wk', 'L0_attn_wv', 'L0_attn_wo', 'L0_ffn_gate_w', 'L0_ffn_W',
        'L0_ffn_atoms', 'L0_ffn_expert_atom_weights', 'L0_ffn_importance', 'L0_ffn_mask_idx']
_OUTS = [((NB, T, DM), 'float32')]


def kernel(**inputs):
    import numpy as _np
    import concourse.bacc as _bacc
    from concourse import mybir as _mybir
    from concourse.bass_utils import run_bass_kernel_spmd as _run

    nc = _bacc.Bacc("TRN2", target_bir_lowering=False, num_devices=1)
    arrays, args = {}, []
    for name in _INS:
        a = _np.ascontiguousarray(inputs[name])
        arrays[f"in_{name}_dram"] = a
        args.append(nc.dram_tensor(f"in_{name}_dram", a.shape, _mybir.dt.from_np(a.dtype), kind="ExternalInput").ap())
    for i, (shape, dtype) in enumerate(_OUTS):
        dt = _mybir.dt.from_np(_np.dtype(dtype))
        args.append(nc.dram_tensor(f"out_{i}_dram", shape, dt, kind="ExternalOutput").ap())
    build(nc, *args)
    r = _run(nc, [arrays], core_ids=[0])
    got = tuple(r.results[0][f"out_{i}_dram"] for i in range(len(_OUTS)))
    return got[0]
```

```python
from contextlib import ExitStack

import concourse.bass as bass
from concourse import mybir

F32 = mybir.dt.float32
F32R = mybir.dt.float32r
BF16 = mybir.dt.bfloat16
I32 = mybir.dt.int32
U32 = mybir.dt.uint32
ALU = mybir.AluOpType
ACT = mybir.ActivationFunctionType
AX = mybir.AxisListType

P = 128
NB, T, DM = 8, 512, 512
H, HKV, HD = 16, 4, 128
G = H // HKV
C = DM // P
TT = T // P
NIT = NB * HKV
NE, NA, NS = 8, 64, 4096
NJ = NS // P
NT = NB * TT
SCALE = float(HD) ** -0.5
EPS = 1e-5
MASKED = -1e38
CAP = NB * T
ETILES = CAP // P
TILES = (2 * CAP + NE * (P - 1)) // P
GROUP = 4
TURNS = -(-TILES // GROUP)
JT = GROUP * TURNS
P_SHIFT = P.bit_length() - 1
PLACE_SHIFT = (NE * ETILES).bit_length() - 1
SHIFT = DM.bit_length() - 1

ROWS = [(3, 0, 0), (2, 1, 0), (0, 1, 384), (1, 2, 0)]
KEYS = [(0, 0, 0), (1, 1, 0), (3, 1, 384), (2, 2, 0)]
PACK = 1280
ROW_AT = {i: 512 * bank + col for i, bank, col in ROWS}
KEY_AT = {j: 512 * bank + col for j, bank, col in KEYS}
UNIT = [(0, 512), (512, 1024), (1024, 1280)]

BANK_S, BANK_PT, BANK_A, BANK_B, BANK_C = 0, 3, 5, 6, 7


class Routing:

    def __init__(self, sb, sem, psum, r_dram, x1_dram, table):
        self.psum, self.r_dram, self.x1_dram, self.table = psum, r_dram, x1_dram, table
        self.gate = sb("route_gate", [P, NE, DM])
        self.rows = sb("route_rows", [P, DM])
        self.product = sb("route_product", [P, 2, DM])
        self.product8 = sb("route_product8", [P, 2, NE])
        self.stats = sb("route_stats", [P, 6])
        self.mean_var = sb("route_mean_var", [P, 2])
        self.var_eps = sb("route_var_eps", [P, 1])
        self.rstd = sb("route_rstd", [P, 1])
        self.minus_half = sb("route_minus_half", [P, 1])
        self.logits = sb("route_logits", [P, NE])
        self.clipped = sb("route_clipped", [P, NE])
        self.best = sb("route_best", [P, 8])
        self.best_at = sb("route_best_at", [P, 8], U32)
        self.gap = sb("route_gap", [P, 2])
        self.number = sb("route_number", [P, NE])
        self.expert = sb("route_expert", [P, 2])
        self.rank = sb("route_rank", [P, 2])
        self.chosen = sb("route_chosen", [P, 3, NE])
        self.counts = sb("route_counts", [P, NE])
        self.ranks = sb("route_ranks", [P, NE])
        self.rank_i = sb("route_rank_i", [P, 2], I32)
        self.tile_i = sb("route_tile_i", [P, 2], I32)
        self.place_i = sb("route_place_i", [P, 2], I32)
        self.tile_f = sb("route_tile_f", [P, 2])
        self.place_tile = sb("route_place_tile", [P, 2], I32)
        self.tokens = sb("route_tokens", [P, NT], I32)
        self.token_now = sb("route_token_now", [P, 1], I32)
        self.share_sum = sb("route_share_sum", [P, 1])
        self.row_i = sb("route_row_i", [P, 2 * NT], I32)
        self.experts = sb("route_experts", [P, 2, NT])
        self.all_ranks = sb("route_all_ranks", [P, 2, NT])
        self.shares = sb("route_shares", [P, 2, NT])
        self.passed = sem("route_waits_passed")
        self.s_rows_in = sem("route_rows_in")
        self.s_chain = sem("route_chain")
        self.s_var = sem("route_var")
        self.s_rstd_ready = sem("route_rstd_ready")
        self.s_x1_ready = sem("route_x1_ready")
        self.s_x1_out = sem("route_x1_out")
        self.s_gap_ready = sem("route_gap_ready")
        self.s_gap_exp = sem("route_gap_exp")
        self.s_chosen_ready = sem("route_chosen_ready")
        self.s_ranked = sem("route_ranked")
        self.s_ranks_read = sem("route_ranks_read")
        self.s_place_ready = sem("route_place_ready")
        self.s_placed = sem("route_placed")
        self.s_token_copied = sem("route_token_copied")


def build(nc, x, wq, wk, wv, wo, gate_w, w_ffn, atoms, eaw, importance, mask_idx, out):
    r_dram = nc.dram_tensor("attn_residual", (NT, P, DM), F32, kind="Internal").ap()
    d_dram = nc.dram_tensor("expert_weights", (DM * DM + P, NE), F32, kind="Internal").ap()
    x_rows = x.rearrange("b (t p) d -> b p t d", p=P)
    x1_dram = nc.dram_tensor("x1", (NT * P, DM), F32, kind="Internal").ap()
    table = nc.dram_tensor("expert_tokens", (NE * CAP, 1), I32, kind="Internal").ap()
    y_dram = nc.dram_tensor("expert_rows", (JT * P, DM), F32, kind="Internal").ap()
    r_store = r_dram.rearrange("(b t) p d -> b p t d", b=NB)
    out_rows = out.rearrange("b (t p) d -> (b t) p d", p=P)
    wq_v = wq.rearrange("(c p) n -> p c n", p=P)
    wk_v = wk.rearrange("(c p) n -> p c n", p=P)
    wv_v = wv.rearrange("(c p) n -> p c n", p=P)
    wo_v = wo.rearrange("(h p) n -> p h n", p=P)

    with ExitStack() as top:
        def sem(name):
            return top.enter_context(nc.semaphore(name))

        ident = top.enter_context(nc.sbuf_tensor("ident", [P, P], F32))
        lower = top.enter_context(nc.sbuf_tensor("lower", [P, P], F32))
        upper = top.enter_context(nc.sbuf_tensor("upper", [P, P], F32))
        ones = top.enter_context(nc.sbuf_tensor("ones", [P, P], F32))
        psum = top.enter_context(nc.psum_tensor("psum", [P, 8, 512], F32))
        causal_bf = top.enter_context(nc.sbuf_tensor("causal_bf", [P, P], BF16))
        ident_bf = top.enter_context(nc.sbuf_tensor("ident_bf", [P, P], BF16))
        row_i = top.enter_context(nc.sbuf_tensor("row_i", [P, NJ], I32))
        entry_sum = top.enter_context(nc.sbuf_tensor("entry_sum", [P, NJ, NE], F32))
        s_passed = sem("waits_passed")
        def sb(name, shape, dt=F32):
            return top.enter_context(nc.sbuf_tensor(name, shape, dt))

        R = Routing(sb, sem, psum, r_dram, x1_dram, table)
        expert_entries(nc, sem, psum, ident, ident_bf, causal_bf, lower, upper, ones, R, row_i, entry_sum, d_dram,
                       gate_w, w_ffn, atoms, eaw, importance, mask_idx)
        attention(nc, sem, s_passed, psum, ident, ident_bf, causal_bf, upper, ones, R, row_i, entry_sum, x_rows,
                  r_store, d_dram, wq_v, wk_v, wv_v, wo_v)
        experts(nc, sem, s_passed, psum, ident, upper, ones, R, d_dram, y_dram, out_rows)


def route_load(sp, R, tt, row):
    wait_apart(sp, R.s_x1_out, 16 * (tt + 1), R.passed)
    wait_apart(sp, R.s_ranks_read, tt + 1, R.passed)
    sp.dma_start(R.rows[:], row).then_inc(R.s_rows_in, 16)


def route_store(sp, R, tt, row):
    wait_apart(sp, R.s_x1_ready, tt + 1, R.passed)
    sp.dma_start(row, R.rows[:]).then_inc(R.s_x1_out, 16)


def route_rstd(pool, R, tt):
    wait_apart(pool, R.s_var, tt + 1, R.passed)
    pool.tensor_tensor(R.rstd[:], R.var_eps[:], R.minus_half[:], ALU.pow).then_inc(R.s_rstd_ready, 1)


def route_place(pool, R, tt):
    wait_apart(pool, R.s_placed, 32 * (tt + 1), R.passed)
    pool.tensor_copy(R.token_now[:], R.tokens[:, bass.ds(tt, 1)]).then_inc(R.s_token_copied, 1)
    wait_apart(pool, R.s_token_copied, tt + 1, R.passed)
    wait_apart(pool, R.s_place_ready, tt + 1, R.passed)
    for k in range(2):
        pool.indirect_dma_start(out=R.table, out_offset=bass.IndirectOffsetOnAxis(ap=R.place_tile[:, k:k + 1], axis=0),
                                in_=R.token_now[:], in_offset=None).then_inc(R.s_placed, 16)


def route_exp(act, R, tt):
    act.wait_ge(R.s_gap_ready, tt + 1)
    act.activation(R.gap[:, 1:2], R.gap[:, 0:1], ACT.Exp).then_inc(R.s_gap_exp, 1)


def route_ranks(pe, R, tt, upper, ones, bank):
    pe.wait_ge(R.s_chosen_ready, tt + 1)
    pe.wait_ge(R.s_ranks_read, tt + 1)
    pe.matmul(R.psum[:, bank, 0:NE], upper[:], R.chosen[:, 2], start=True, stop=False)
    pe.matmul(R.psum[:, bank, 0:NE], ones[:], R.counts[:], start=False, stop=True).then_inc(R.s_ranked, 1)


CHAIN = 26


def route_step(dve, R, tt, k, ins):
    ins.then_inc(R.s_chain, 1)
    wait_apart(dve, R.s_chain, tt * CHAIN + k, R.passed)


def route_variance(dve, R, tt):
    dve.wait_ge(R.s_rows_in, 16 * (tt + 1))
    route_step(dve, R, tt, 1, dve.bn_stats(R.stats[:], R.rows[:]))
    route_step(dve, R, tt, 2, dve.bn_aggr(R.mean_var[:], R.stats[:]))
    dve.tensor_scalar(R.var_eps[:], R.mean_var[:, 1:2], EPS, None, ALU.add).then_inc(R.s_var, 1)


def route_normalize(dve, R, tt):
    dve.wait_ge(R.s_rstd_ready, tt + 1)
    dve.tensor_scalar(R.rows[:], R.rows[:], R.mean_var[:, 0:1], R.rstd[:], ALU.subtract, ALU.mult).then_inc(R.s_x1_ready, 1)
    dve.wait_ge(R.s_x1_ready, tt + 1)


def route_logits(dve, R, tt, experts):
    for e in experts:
        dve.tensor_tensor_reduce(R.product[:, e % 2], R.rows[:], R.gate[:, e], 1.0, 0.0, ALU.mult, ALU.add,
                                 R.logits[:, e:e + 1]).then_inc(R.s_chain, 1)
        if e:
            wait_apart(dve, R.s_chain, tt * CHAIN + 2 + e, R.passed)


def route_choose(dve, R, tt):
    step = lambda k, ins: route_step(dve, R, tt, k, ins)
    wait_apart(dve, R.s_chain, tt * CHAIN + 10, R.passed)
    step(11, dve.tensor_scalar(R.clipped[:], R.logits[:], 50.0, -50.0, ALU.min, ALU.max))
    step(12, dve.max(R.best[:], R.clipped[:]))
    dve.tensor_tensor(R.gap[:, 0:1], R.best[:, 1:2], R.best[:, 0:1], ALU.subtract).then_inc(R.s_gap_ready, 1)
    step(13, dve.max_index(R.best_at[:], R.best[:], R.clipped[:]))
    step(14, dve.tensor_copy(R.expert[:], R.best_at[:, 0:2]))
    for k in range(2):
        last = dve.tensor_scalar(R.chosen[:, k], R.number[:], R.expert[:, k:k + 1], None, ALU.is_equal)
    step(15, last)
    dve.tensor_tensor(R.chosen[:, 2], R.chosen[:, 0], R.chosen[:, 1], ALU.add).then_inc(R.s_chosen_ready, 1)
    dve.tensor_copy(R.experts[:, :, bass.ds(tt, 1)].rearrange("p k a -> p (k a)"), R.expert[:])
    dve.wait_ge(R.s_gap_exp, tt + 1)
    step(16, dve.tensor_scalar(R.share_sum[:], R.gap[:, 1:2], 1.0, None, ALU.add))
    step(17, dve.reciprocal(R.share_sum[:], R.share_sum[:]))
    dve.tensor_copy(R.shares[:, 0, bass.ds(tt, 1)], R.share_sum[:])
    dve.tensor_tensor(R.shares[:, 1, bass.ds(tt, 1)], R.share_sum[:], R.gap[:, 1:2], ALU.mult)


def route_locate(dve, R, tt, bank):
    step = lambda k, ins: route_step(dve, R, tt, k, ins)
    dve.wait_ge(R.s_ranked, tt + 1)
    dve.tensor_copy(R.ranks[:], R.psum[:, bank, 0:NE]).then_inc(R.s_ranks_read, 1)
    wait_apart(dve, R.s_ranks_read, tt + 2, R.passed)
    step(18, dve.tensor_copy(R.share_sum[:], R.share_sum[:]))
    step(19, dve.tensor_tensor(R.counts[:], R.counts[:], R.chosen[:, 2], ALU.add))
    for k in range(2):
        step(20 + k, dve.tensor_tensor_reduce(R.product8[:, k], R.ranks[:], R.chosen[:, k], 1.0, 0.0, ALU.mult, ALU.add,
                                              R.rank[:, k:k + 1]))
    step(22, dve.tensor_copy(R.rank_i[:], R.rank[:]))
    step(23, dve.tensor_scalar(R.tile_i[:], R.rank_i[:], P_SHIFT, None, ALU.logical_shift_right))
    step(24, dve.tensor_scalar(R.place_i[:], R.rank_i[:], P - 1, PLACE_SHIFT, ALU.bitwise_and, ALU.logical_shift_left))
    step(25, dve.scalar_tensor_tensor(out=R.tile_f[:], in0=R.expert[:], scalar=float(ETILES), in1=R.tile_i[:],
                                      op0=ALU.mult, op1=ALU.add))
    dve.tensor_copy(R.all_ranks[:, :, bass.ds(tt, 1)].rearrange("p k a -> p (k a)"), R.rank[:])
    dve.wait_ge(R.s_placed, 32 * (tt + 1))
    dve.tensor_tensor(R.place_tile[:], R.tile_f[:], R.place_i[:], ALU.add).then_inc(R.s_place_ready, 1)
    step(26, dve.tensor_copy(R.expert[:], R.expert[:]))


def expert_entries(nc, sem, psum, ident, ident_bf, causal_bf, lower, upper, ones, R, row_i, entry_sum, d_dram, gate_w,
                   w_ffn, atoms, eaw, importance, mask_idx):
    with ExitStack() as ctx:
        def sb(name, shape, dt=F32):
            return ctx.enter_context(nc.sbuf_tensor(name, shape, dt))

        idx_i, idx_r_i, idx_c_i = sb("idx_i", [P, NJ], I32), sb("idx_r_i", [P, NJ], I32), sb("idx_c_i", [P, NJ], I32)
        idx_f, row_f, dup, gap_f = sb("idx_f", [P, NJ]), sb("row_f", [P, NJ]), sb("dup", [P, NJ]), sb("gap_f", [P, NJ])
        spare_i, spare_f = sb("spare_i", [P, 1], I32), sb("spare_f", [P, 1])
        entry = sb("entry", [P, NJ, NE])
        same = sb("same", [P, 2, P])
        lower_out = sb("lower_out", [P, P])
        zeros_i = sb("zeros_i", [P, NE * ETILES], I32)
        number_i = sb("number_i", [P, NE], I32)
        small = sb("small", [NE, 4])
        eaw_sb, eaw_e, eawT = sb("eaw_sb", [NE, NA]), sb("eaw_e", [NE, NA]), sb("eawT", [NA, NE])
        atoms_sb, imp_sb = sb("atoms_sb", [NA, NS]), sb("imp_sb", [NE, NS])
        w_sb, wT = sb("w_sb", [P, TT, DM]), sb("wT", [P, C, DM])
        fill_sb = sb("fill_sb", [P, 2, DM * NE])

        s_const_step, s_const = sem("consts_step"), sem("consts_ready")
        s_idx_in, s_eaw_in, s_gate_in = sem("idx_loaded"), sem("mixture_loaded"), sem("gate_loaded")
        s_imp_in, s_w_in, s_atoms_in = sem("importance_loaded"), sem("w_ffn_loaded"), sem("atoms_loaded")
        s_fill, s_fill_out = sem("fill_ready"), [sem("fill_even_stored"), sem("fill_odd_stored")]
        s_chain = sem("dve_chain")
        s_max, s_exp, s_mix, s_mixT_pe, s_mixT = (sem("mixture_max"), sem("mixture_exp"), sem("mixture_ready"),
                                                  sem("mixture_turned"), sem("mixtureT_ready"))
        s_wT_pe, s_wT = sem("w_ffn_turned"), sem("w_ffnT_ready")
        s_impT, s_imp_e, s_mixed, s_entry = (sem("importance_turned"), sem("importance_exp"), sem("atoms_mixed"),
                                             sem("entries_ready"))
        s_gap, s_idx_row, s_same, s_sum = (sem("indices_ready"), sem("index_rows_ready"), sem("equal_indices_ready"),
                                           sem("entry_sums_ready"))
        block = ctx.enter_context(nc.Block())

        @block.sync
        def _(sp):
            sp.dma_start(w_sb[:], w_ffn.rearrange("(t p) d -> p t d", p=P)).then_inc(s_w_in, 16)
            sp.dma_start(atoms_sb[:], atoms).then_inc(s_atoms_in, 16)
            sp.dma_start(imp_sb[:], importance).then_inc(s_imp_in, 16)
            for c in range(C):
                sp.wait_ge(s_fill, c + 1)
                sp.dma_start(d_dram[c * P * DM:(c + 1) * P * DM, :].rearrange("(p r) e -> p (r e)", p=P),
                             fill_sb[:, c % 2]).then_inc(s_fill_out[c % 2], 16)
            sp.wait_ge(s_fill_out[0], 32)
            sp.wait_ge(s_fill_out[1], 32)

        @block.gpsimd
        def _(pool):
            pool.dma_start(idx_i[:], mask_idx.rearrange("(p j) -> p j", p=P)).then_inc(s_idx_in, 16)
            pool.dma_start(eaw_sb[:], eaw).then_inc(s_eaw_in, 16)
            pool.dma_start(R.gate[:].rearrange("p e d -> p (e d)"),
                           gate_w.rearrange("e d -> (e d)").unsqueeze(0).broadcast_to([P, NE * DM])).then_inc(s_gate_in, 16)
            pool.memset(ident[:], 0.0).then_inc(s_const_step, 1)
            pool.memset(ones[:], 1.0)
            pool.memset(upper[:], 1.0)
            pool.memset(R.minus_half[:], -0.5)
            pool.memset(R.counts[:], 0.0)
            pool.memset(zeros_i[:], 0)
            pool.memset(causal_bf[:], 0.0).then_inc(s_const_step, 1)
            pool.memset(lower[:], 1.0).then_inc(s_const_step, 1)
            pool.wait_ge(s_const_step, 3)
            pool.affine_select(out=ident[:], in_=ident[:], compare_op=ALU.not_equal, fill=1.0, base=0,
                               pattern=[[-1, P]], channel_multiplier=1).then_inc(s_const, 1)
            pool.affine_select(out=causal_bf[:], in_=causal_bf[:], compare_op=ALU.is_ge, fill=MASKED, base=0,
                               pattern=[[-1, P]], channel_multiplier=1).then_inc(s_const, 1)
            pool.affine_select(out=lower[:], in_=lower[:], compare_op=ALU.is_gt, fill=0.0, base=0,
                               pattern=[[-1, P]], channel_multiplier=1).then_inc(s_const, 1)
            pool.affine_select(out=upper[:], in_=upper[:], compare_op=ALU.is_gt, fill=0.0, base=0,
                               pattern=[[1, P]], channel_multiplier=-1)
            pool.iota(R.tokens[:], pattern=[[P, NT]], base=0, channel_multiplier=1)
            pool.iota(number_i[:], pattern=[[1, NE]], base=0, channel_multiplier=0)
            pool.iota(spare_i[:], pattern=[[0, 1]], base=DM * DM, channel_multiplier=1).then_inc(s_const, 1)
            pool.wait_ge(s_const, 4)
            pool.tensor_copy(ident_bf[:], ident[:]).then_inc(s_const, 1)
            pool.tensor_copy(R.number[:], number_i[:])
            halves = R.table.rearrange("(h p n) a -> h p (n a)", h=2, p=P // 2)
            for half in range(2):
                pool.dma_start(halves[half], zeros_i[0:P // 2]).then_inc(R.s_placed, 16)
            for c in range(C):
                pool.wait_ge(s_wT, c + 1)
                if c >= 2:
                    pool.wait_ge(s_fill_out[c % 2], 16)
                pool_round(pool, fill_sb[:, c % 2].rearrange("p (r e) -> p r e", e=NE),
                                 wT[:, c, :].unsqueeze(2).broadcast_to([P, DM, NE])).then_inc(s_fill, 1)
            pool.wait_ge(s_gate_in, 16)
            pool.wait_ge(R.s_placed, 32)

        @block.tensor
        def _(pe):
            pe.wait_ge(s_const, 5)
            pe.wait_ge(s_w_in, 16)
            for c in range(C):
                for t in range(TT):
                    last = pe.transpose(psum[:, c, t * P:(t + 1) * P], w_sb[:, t, c * P:(c + 1) * P], ident[:])
                last.then_inc(s_wT_pe, 1)
            pe.wait_ge(s_mix, 1)
            pe.transpose(psum[0:NA, 5, 64:64 + NE], eaw_e[:], ident[0:NE, 0:NE]).then_inc(s_mixT_pe, 1)
            pe.wait_ge(s_imp_in, 16)
            for j in range(NJ):
                last = pe.transpose(psum[:, 4, j * NE:(j + 1) * NE], imp_sb[:, j:NS:NJ], ident[0:NE, 0:NE])
            last.then_inc(s_impT, 1)
            pe.wait_ge(s_atoms_in, 16)
            pe.wait_ge(s_mixT, 1)
            for j in range(NJ):
                last = pe.matmul(psum[:, 6, j * NE:(j + 1) * NE], atoms_sb[:, j:NS:NJ], eawT[:], start=True, stop=True)
            last.then_inc(s_mixed, 1)
            pe.wait_ge(s_gap, 1)
            pe.wait_ge(s_entry, 1)
            pe.wait_ge(s_wT, C)
            for j in range(NJ):
                if j >= 2:
                    pe.wait_ge(s_same, j - 1)
                pe.transpose(psum[:, (5, 7)[j % 2], 0:P], idx_f[:, j:j + 1].broadcast_to([P, P]), ident[:]).then_inc(s_idx_row, 1)
                if j:
                    pe.wait_ge(s_same, j)
                    pe.matmul(psum[:, 0, (j - 1) * NE:j * NE], same[:, (j - 1) % 2, :], entry[:, j - 1, :],
                              start=True, stop=True).then_inc(s_sum, 1)
            pe.wait_ge(s_same, NJ)
            pe.matmul(psum[:, 0, (NJ - 1) * NE:NJ * NE], same[:, (NJ - 1) % 2, :], entry[:, NJ - 1, :],
                      start=True, stop=True).then_inc(s_sum, 1)

        @block.scalar
        def _(act):
            act.wait_ge(s_max, 1)
            act.activation(eaw_e[:], eaw_sb[:], ACT.Exp, bias=small[:, 0:1], accum_out=small[:, 1:2]).then_inc(s_exp, 1)
            act.wait_ge(s_impT, 1)
            act.activation(entry[:].rearrange("p j e -> p (j e)"), psum[:, 4, 0:NJ * NE], ACT.Exp,
                           scale=-1.0).then_inc(s_imp_e, 1)

        @block.vector
        def _(dve):
            chain = 0

            def after(ins):
                nonlocal chain
                chain += 1
                ins.then_inc(s_chain, 1)
                dve.wait_ge(s_chain, chain)

            dve.memset(R.rows[:], 0.0).then_inc(R.s_x1_out, 16)
            dve.memset(R.place_tile[:], 0)
            dve.memset(R.ranks[:], 0.0).then_inc(R.s_ranks_read, 1)
            dve.wait_ge(s_eaw_in, 16)
            dve.tensor_reduce(small[:, 0:1], eaw_sb[:], AX.X, ALU.max, negate=True).then_inc(s_max, 1)
            dve.wait_ge(s_idx_in, 16)
            dve.tensor_copy(idx_f[:], idx_i[:])
            dve.tensor_scalar(idx_r_i[:], idx_i[:], SHIFT, None, ALU.logical_shift_right)
            after(dve.tensor_scalar(idx_c_i[:], idx_i[:], DM - 1, SHIFT, ALU.bitwise_and, ALU.logical_shift_left))
            dve.wait_ge(s_exp, 1)
            after(dve.reciprocal(small[:, 2:3], small[:, 1:2]))
            dve.tensor_scalar(eaw_e[:], eaw_e[:], small[:, 2:3], None, ALU.mult).then_inc(s_mix, 1)
            after(dve.tensor_tensor(row_f[:], idx_r_i[:], idx_c_i[:], ALU.add))
            for c in range(C):
                dve.wait_ge(s_wT_pe, c + 1)
                dve.tensor_copy(wT[:, c], psum[:, c, :]).then_inc(s_wT, 1)
            dve.wait_ge(s_mixT_pe, 1)
            dve.tensor_copy(eawT[:], psum[0:NA, 5, 64:64 + NE]).then_inc(s_mixT, 1)
            dve.wait_ge(s_const, 4)
            after(dve.tensor_copy(spare_f[:], spare_i[:]))
            dve.tensor_scalar(gap_f[:], row_f[:], -1.0, spare_f[:, 0:1], ALU.mult, ALU.add).then_inc(s_gap, 1)
            flat = entry[:].rearrange("p j e -> p (j e)")
            dve.wait_ge(s_imp_e, 1)
            after(dve.tensor_scalar(flat, flat, 1.0, None, ALU.add))
            after(dve.reciprocal(flat, flat))
            dve.wait_ge(s_mixed, 1)
            dve.tensor_tensor(flat, psum[:, 6, 0:NJ * NE], flat, ALU.mult).then_inc(s_entry, 1)
            for j in range(NJ):
                dve.wait_ge(s_idx_row, j + 1)
                if j >= 2:
                    dve.wait_ge(s_sum, j - 1)
                dve.tensor_scalar(same[:, j % 2], psum[:, (5, 7)[j % 2], 0:P], idx_f[:, j:j + 1], None,
                                  ALU.is_equal).then_inc(s_same, 1)
                dve.wait_ge(s_same, j + 1)
                after(dve.tensor_tensor_reduce(lower_out[:], same[:, j % 2], lower[:], 1.0, 0.0, ALU.mult, ALU.add,
                                               dup[:, j:j + 1]))
            dve.wait_ge(s_gap, 1)
            after(dve.tensor_scalar(dup[:], dup[:], 1.0, None, ALU.min))
            after(dve.tensor_tensor(dup[:], dup[:], gap_f[:], ALU.mult))
            after(dve.tensor_tensor(dup[:], dup[:], row_f[:], ALU.add))
            after(dve.tensor_copy(row_i[:], dup[:]))
            dve.wait_ge(s_sum, NJ)
            after(dve.tensor_copy(entry_sum[:].rearrange("p j e -> p (j e)"), psum[:, 0, 0:NJ * NE]))


def wait_apart(eng, semaphore, count, passed):
    eng.wait_ge(semaphore, count)
    eng.sem_inc(passed, 1)


def pool_round(pool, out, in_):
    return pool.tensor_scalar(out, in_, 1.0, 1.0, ALU.mult, ALU.mult)


def run(eng, iteration):
    def batch(b, last_kind, route):
        with eng.Fori(0, HKV - 1) as g:
            iteration(b, g, b * HKV + g, "group", route)
        iteration(b, HKV - 1, b * HKV + HKV - 1, last_kind, route)

    batch(0, "batch", False)
    with eng.Fori(1, NB - 1) as b:
        batch(b, "batch", True)
    batch(NB - 1, "end", True)


def next_batch(b):
    return (b + 2) % NB


def attention(nc, sem, s_passed, psum, ident, ident_bf, causal_bf, upper, ones, R, row_i, entry_sum, x_rows, r_store,
              d_dram, wq_v, wk_v, wv_v, wo_v):
    with ExitStack() as ctx:
        def sb(name, shape, dt=F32):
            return ctx.enter_context(nc.sbuf_tensor(name, shape, dt))

        x_in = sb("x_in", [P, TT, DM])
        y_acc = sb("y_acc", [P, TT, DM])
        xT_hi, xT_lo = sb("xT_hi", [P, C, T], F32R), sb("xT_lo", [P, C, T], F32R)
        wo_raw = sb("wo_raw", [P, G, DM])
        wo_hi, wo_lo = sb("wo_hi", [P, G, DM], F32R), sb("wo_lo", [P, G, DM], F32R)
        wv_hi, wv_lo = sb("wv_hi", [P, C, HKV * HD], F32R), sb("wv_lo", [P, C, HKV * HD], F32R)
        w_raw = sb("w_raw", [P, 1 + G, C, HD])
        w_hi, w_lo = sb("w_hi", [P, 1 + G, C, HD], F32R), sb("w_lo", [P, 1 + G, C, HD], F32R)
        v_raw = sb("v_raw", [P, TT, HKV * HD])
        v_hi, v_lo = sb("v_hi", [P, TT, HD], F32R), sb("v_lo", [P, TT, HD], F32R)
        kT_hi, kT_lo = sb("kT_hi", [P, T], F32R), sb("kT_lo", [P, T], F32R)
        qT_hi, qT_lo = sb("qT_hi", [P, 2, T], F32R), sb("qT_lo", [P, 2, T], F32R)
        probs = sb("probs", [P, 2, PACK])
        pT_hi, pT_lo = sb("pT_hi", [P, PACK], F32R), sb("pT_lo", [P, PACK], F32R)
        oT_hi, oT_lo = sb("oT_hi", [P, G, T], F32R), sb("oT_lo", [P, G, T], F32R)
        neg_max = sb("neg_max", [P, 2, TT])
        row_sum = sb("row_sum", [P, 2, TT])
        row_inv = sb("row_inv", [P, 2, TT])
        row_now = sb("row_now", [P, 1], I32)
        entry_now = sb("entry_now", [P, NE])

        s_x_in = sem("x_loaded")
        s_w_in = [sem(f"weight_slot_{j}_loaded") for j in range(1 + G)]
        s_wo_in = [sem(f"wo_head_{h}_loaded") for h in range(G)]
        s_wv_in = sem("wv_loaded")
        s_scatter = sem("entries_scattered")
        s_r_out = sem("residual_stored")
        s_w_split = sem("weight_slots_split")
        s_vg = sem("v_group_split")
        s_wo = sem("wo_heads_split")
        s_wv_hi, s_wv = sem("wv_hi_ready"), sem("wv_split")
        s_pool_step = sem("pool_step")
        s_seed = sem("y_seeded")
        s_norm = sem("probs_normalized")
        s_qk = sem("score_banks_ready")
        s_max = sem("score_maxima_ready")
        s_exp = sem("score_banks_exped")
        s_inv = sem("row_inv_ready")
        s_pt, s_pt_hi, s_pt_lo = sem("pT_units_ready"), sem("pT_hi_ready"), sem("pT_lo_ready")
        s_q, s_q_hi, s_q_lo = sem("qT_ready"), sem("qT_hi_ready"), sem("qT_lo_ready")
        s_k, s_k_hi, s_k_lo = sem("kT_ready"), sem("kT_hi_ready"), sem("kT_lo_ready")
        s_o, s_o_hi, s_o_lo = sem("oT_ready"), sem("oT_hi_ready"), sem("oT_lo_ready")
        s_xt, s_xt_hi, s_xt_lo = sem("xT_ready"), sem("xT_hi_ready"), sem("xT_lo_ready")
        s_v, s_v_raw = sem("v_ready"), sem("v_raw_ready")
        s_y, s_y_acc = sem("y_tiles_ready"), sem("y_tiles_added")
        s_entry = sem("entry_copied")
        block = ctx.enter_context(nc.Block())

        @block.sync
        def _(sp):
            sp.dma_start(x_in[:], x_rows[0]).then_inc(s_x_in, 16)

            def load_slot(j, g):
                src = wk_v[:, :, bass.ds(g * HD, HD)] if j == 0 else wq_v[:, :, bass.ds((g * G + j - 1) * HD, HD)]
                sp.dma_start(w_raw[:, j], src).then_inc(s_w_in[j], 16)

            for j in range(1 + G):
                load_slot(j, 0)
            sp.dma_start(wo_raw[:, 0:C, :], wv_v).then_inc(s_wv_in, 16)

            def load_wo(h, g):
                src = wo_v[:, bass.ds(g * G + h, 1), :].rearrange("p a n -> p (a n)")
                sp.dma_start(wo_raw[:, h], src).then_inc(s_wo_in[h], 16)

            for j in range(1 + G):
                sp.wait_ge(s_w_split, j + 1)
                load_slot(j, 1)
            sp.wait_ge(s_wv, 1)
            for h in range(G):
                load_wo(h, 0)
            sp.wait_ge(s_seed, 1)
            sp.wait_ge(s_xt, C)
            sp.dma_start(x_in[:], x_rows[1]).then_inc(s_x_in, 16)

            def iteration(b, g, it, kind, route):
                if route:
                    wait_apart(sp, s_r_out, 16 * b, s_passed)
                    route_load(sp, R, it - TT, R.r_dram[bass.ds(it - TT, 1)].rearrange("a p d -> (a p) d"))
                if kind != "end":
                    for j in range(1 + G):
                        sp.wait_ge(s_w_split, (it + 1) * (1 + G) + j + 1)
                        load_slot(j, (g + 2) % HKV)
                        if 1 <= j < G:
                            sp.wait_ge(s_wo, it * G + j)
                            load_wo(j - 1, (g + 1) % HKV)
                        if route and j == G - 1:
                            route_store(sp, R, it - TT, R.x1_dram[bass.ds((it - TT) * P, P), :])
                    sp.wait_ge(s_wo, it * G + G)
                    load_wo(G - 1, (g + 1) % HKV)
                elif route:
                    route_store(sp, R, it - TT, R.x1_dram[bass.ds((it - TT) * P, P), :])
                if kind != "group":
                    wait_apart(sp, s_y_acc, TT + (it + 1) * TT, s_passed)
                    sp.dma_start(r_store[bass.ds(b, 1)].rearrange("a p t d -> (a p) t d"), y_acc[:]).then_inc(s_r_out, 16)
                if kind == "batch":
                    wait_apart(sp, s_seed, b + 2, s_passed)
                    wait_apart(sp, s_xt, (b + 2) * C, s_passed)
                    sp.dma_start(x_in[:], x_rows[bass.ds(next_batch(b), 1)].rearrange("a p t d -> (a p) t d")).then_inc(s_x_in, 16)

            run(sp, iteration)
            sp.wait_ge(s_r_out, 16 * NB)
            sp.wait_ge(s_x_in, 16 * (NB + 1))
            for j in range(1 + G):
                sp.wait_ge(s_w_in[j], 16 * (NIT + 1))
            sp.wait_ge(R.s_x1_out, 16 * (NT - TT + 1))

        @block.gpsimd
        def _(pool):
            def split_slot(j, k):
                pool_round(pool, w_hi[:, j], w_raw[:, j]).then_inc(s_pool_step, 1)
                wait_apart(pool, s_pool_step, k + 1, s_passed)
                pool.tensor_tensor(w_lo[:, j], w_raw[:, j], w_hi[:, j].bitcast(F32), ALU.subtract).then_inc(s_w_split, 1)

            def split_v(g, k):
                src = v_raw[:, :, bass.ds(g * HD, HD)]
                pool.tensor_copy(v_hi[:], src).then_inc(s_pool_step, 1)
                wait_apart(pool, s_pool_step, k + 1, s_passed)
                pool.tensor_tensor(v_lo[:], src, v_hi[:].bitcast(F32), ALU.subtract).then_inc(s_vg, 1)

            def split_wo(h, it, k):
                wait_apart(pool, s_wo_in[h], 16 * (it + 1), s_passed)
                pool_round(pool, wo_hi[:, h], wo_raw[:, h]).then_inc(s_pool_step, 1)
                wait_apart(pool, s_pool_step, k + 1, s_passed)
                pool.tensor_tensor(wo_lo[:, h], wo_raw[:, h], wo_hi[:, h].bitcast(F32), ALU.subtract).then_inc(s_wo, 1)

            def normalize(n, buf):
                wait_apart(pool, s_inv, n + 1, s_passed)
                for i in range(TT):
                    a = ROW_AT[i]
                    p = probs[:, buf, a:a + (i + 1) * P]
                    last = pool.tensor_scalar(p, p, row_inv[:, buf, i:i + 1], 1.0, ALU.mult, ALU.mult)
                last.then_inc(s_norm, 1)

            def slot(it_next, j, k):
                wait_apart(pool, s_w_in[j], 16 * (it_next + 1), s_passed)
                if j == 0:
                    wait_apart(pool, s_k, it_next, s_passed)
                else:
                    wait_apart(pool, s_q, (it_next - 1) * G + j, s_passed)
                split_slot(j, k)

            for j in range(1 + G):
                pool.wait_ge(s_w_in[j], 16)
                split_slot(j, j)
            pool.wait_ge(s_x_in, 16)
            pool_round(pool, y_acc[:], x_in[:]).then_inc(s_seed, 1)
            pool.wait_ge(s_v_raw, TT)
            split_v(0, 1 + G)
            normalize(0, 0)
            SETUP_STEPS = 1 + G + 1
            STEPS = 1 + G + 1 + G

            def iteration(b, g, it, kind, route):
                k0 = SETUP_STEPS + it * STEPS
                n0 = it * G
                k = 0
                has_next = kind != "end"
                if has_next:
                    slot(it + 1, 0, k0)
                    k = 1
                normalize(n0 + 1, 1)
                if route:
                    route_rstd(pool, R, it - TT)
                split_wo(0, it, k0 + k)
                k += 1
                if has_next:
                    slot(it + 1, 1, k0 + k)
                    k += 1
                normalize(n0 + 2, 0)
                split_wo(1, it, k0 + k)
                k += 1
                if has_next:
                    slot(it + 1, 2, k0 + k)
                    k += 1
                normalize(n0 + 3, 1)
                split_wo(2, it, k0 + k)
                split_wo(3, it, k0 + k + 1)
                k += 2
                wait_apart(pool, s_scatter, 16 * (it + 1), s_passed)
                pool.tensor_copy(row_now[:], row_i[:, bass.ds(it, 1)]).then_inc(s_entry, 1)
                pool.tensor_copy(entry_now[:], entry_sum[:, bass.ds(it, 1), :].rearrange("p a e -> p (a e)")).then_inc(s_entry, 1)
                wait_apart(pool, s_entry, 2 * it + 2, s_passed)
                pool.indirect_dma_start(out=d_dram, out_offset=bass.IndirectOffsetOnAxis(ap=row_now[:, 0:1], axis=0),
                                        in_=entry_now[:], in_offset=None, compute_op=ALU.add).then_inc(s_scatter, 16)
                if has_next:
                    slot(it + 1, 3, k0 + k)
                    k += 1
                    normalize(n0 + 4, 0)
                if kind == "group":
                    wait_apart(pool, s_o, n0 + G, s_passed)
                    split_v(g + 1, k0 + k)
                    k += 1
                if has_next:
                    slot(it + 1, 4, k0 + k)
                    k += 1
                if route:
                    route_place(pool, R, it - TT)
                if kind == "batch":
                    wait_apart(pool, s_x_in, 16 * (b + 2), s_passed)
                    wait_apart(pool, s_r_out, 16 * (b + 1), s_passed)
                    pool_round(pool, y_acc[:], x_in[:]).then_inc(s_seed, 1)
                    wait_apart(pool, s_v_raw, (b + 2) * TT, s_passed)
                    split_v(0, k0 + k)

            pool.dma_start(d_dram[DM * DM:DM * DM + P, :], entry_sum[:, 0, :]).then_inc(s_scatter, 16)
            run(pool, iteration)
            pool.wait_ge(s_scatter, 16 * (NIT + 1))
            pool.wait_ge(R.s_placed, 32 * (NT - TT + 1))

        @block.tensor
        def _(pe):
            def three(dst, hi_s, lo_s, hi_m, lo_m, start, stop, skip=False):
                pe.matmul(dst, hi_s, hi_m, start=start, stop=False)
                pe.matmul(dst, hi_s, lo_m, start=False, stop=False)
                return pe.matmul(dst, lo_s, hi_m, start=False, stop=stop)

            def scores(n, buf, first=False):
                pe.wait_ge(s_q_lo, n + 1)
                for i, bank, col in ROWS:
                    w = (i + 1) * P
                    dst = psum[:, BANK_S + bank, col:col + w]
                    if not first and col == 0:
                        pe.wait_ge(s_exp, 3 * n - 3 + bank + 1)
                    q = (qT_hi[:, buf, i * P:(i + 1) * P], qT_lo[:, buf, i * P:(i + 1) * P])
                    three(dst, *q, kT_hi[:, 0:w], kT_lo[:, 0:w], True, False)
                    last = pe.matmul(dst[:, i * P:w], ident_bf[:], causal_bf[:], start=False, stop=True)
                    if i != 2:
                        last.then_inc(s_qk, 1)

            def transposes(n, buf, last_unit):
                if last_unit:
                    pe.wait_ge(s_pt_lo, 3 * n + 4)
                else:
                    pe.wait_ge(s_norm, n + 1)
                    pe.wait_ge(s_pt_lo, 3 * n + 3)
                for j, unit, col in KEYS:
                    if (unit == 2) != last_unit:
                        continue
                    for i in range(j, TT):
                        at = col + (i - j) * P
                        src = ROW_AT[i] + j * P
                        last = pe.transpose(psum[:, BANK_PT + unit % 2, at:at + P], probs[:, buf, src:src + P], ident[:])
                    if j != 1:
                        last.then_inc(s_pt, 1)

            def values(n, first_of_group, it):
                if first_of_group:
                    pe.wait_ge(s_vg, it + 1)
                    pe.wait_ge(s_y_acc, it * TT + TT)
                else:
                    pe.wait_ge(s_o_lo, n)
                for j, unit, _ in KEYS:
                    if j != 3:
                        pe.wait_ge(s_pt_lo, 3 * n + 3 + unit + 1)
                    a, w = KEY_AT[j], T - j * P
                    last = three(psum[:, BANK_B, j * P:T], v_hi[:, j], v_lo[:, j], pT_hi[:, a:a + w], pT_lo[:, a:a + w],
                                 j == 0, j == KEYS[-1][0])
                last.then_inc(s_o, 1)

            def project(slot, done):
                for c in range(C):
                    last = three(psum[:, BANK_A, :], w_hi[:, slot, c], w_lo[:, slot, c], xT_hi[:, c], xT_lo[:, c],
                                 c == 0, c == C - 1)
                last.then_inc(done, 1)

            def query(n, h, it):
                pe.wait_ge(s_w_split, it * (1 + G) + h + 2)
                if h == 0:
                    pe.wait_ge(s_k_lo, it + 1)
                else:
                    pe.wait_ge(s_q_lo, n)
                project(1 + h, s_q)

            def key(it):
                pe.wait_ge(s_w_split, it * (1 + G) + 1)
                project(0, s_k)

            def turn_x(b, first):
                pe.wait_ge(s_x_in, 16 * (b + 1))
                if not first:
                    pe.wait_ge(s_q_lo, b * HKV * G)
                    pe.wait_ge(s_y_acc, TT + (b * HKV - 1) * TT)
                for c in range(C):
                    if c >= 2:
                        pe.wait_ge(s_xt_lo, b * C + c - 1)
                    for t in range(TT):
                        last = pe.transpose(psum[:, (BANK_A, BANK_C)[c % 2], t * P:(t + 1) * P],
                                            x_in[:, t, c * P:(c + 1) * P], ident[:])
                    last.then_inc(s_xt, 1)

            def value_rows(b, first):
                for t in range(TT):
                    if t >= 2:
                        pe.wait_ge(s_v_raw, b * TT + t - 1)
                    elif not first:
                        pe.wait_ge(s_y_acc, TT + b * HKV * TT - 1 + t)
                    for c in range(C):
                        last = three(psum[:, (BANK_C, BANK_B)[t % 2], :], xT_hi[:, c, t * P:(t + 1) * P],
                                     xT_lo[:, c, t * P:(t + 1) * P], wv_hi[:, c], wv_lo[:, c], c == 0, c == C - 1)
                    last.then_inc(s_v, 1)

            def out_rows(t, it):
                if t == 0:
                    pe.wait_ge(s_o_lo, (it + 1) * G)
                    pe.wait_ge(s_wo, (it + 1) * G)
                if t != 1:
                    pe.wait_ge(s_y_acc, TT + it * TT + t - 1)
                for h in range(G):
                    last = three(psum[:, (BANK_C, BANK_B)[t % 2], :], oT_hi[:, h, t * P:(t + 1) * P],
                                 oT_lo[:, h, t * P:(t + 1) * P], wo_hi[:, h], wo_lo[:, h], h == 0, h == G - 1)
                last.then_inc(s_y, 1)

            turn_x(0, True)
            pe.wait_ge(s_xt_lo, C)
            key(0)
            query(0, 0, 0)
            scores(0, 0, True)
            query(1, 1, 0)
            pe.wait_ge(s_wv, 2)
            value_rows(0, True)

            def iteration(b, g, it, kind, route):
                n = it * G
                scores(n + 1, 1)
                transposes(n, 0, False)
                if route:
                    pe.wait_ge(R.s_ranks_read, it - TT + 1)
                query(n + 2, 2, it)
                transposes(n, 0, True)
                values(n, True, it)
                scores(n + 2, 0)
                transposes(n + 1, 1, False)
                query(n + 3, 3, it)
                transposes(n + 1, 1, True)
                values(n + 1, False, it)
                scores(n + 3, 1)
                transposes(n + 2, 0, False)
                if kind == "batch":
                    turn_x(b + 1, False)
                    transposes(n + 2, 0, True)
                    values(n + 2, False, it)
                    pe.wait_ge(s_xt_lo, (b + 2) * C)
                    key(it + 1)
                elif kind == "group":
                    pe.wait_ge(s_q_lo, n + 4)
                    key(it + 1)
                    transposes(n + 2, 0, True)
                    values(n + 2, False, it)
                else:
                    transposes(n + 2, 0, True)
                    values(n + 2, False, it)
                transposes(n + 3, 1, False)
                if kind != "end":
                    query(n + 4, 0, it + 1)
                transposes(n + 3, 1, True)
                values(n + 3, False, it)
                if kind != "end":
                    scores(n + 4, 0)
                out_rows(0, it)
                out_rows(1, it)
                if kind != "end":
                    query(n + 5, 1, it + 1)
                out_rows(2, it)
                out_rows(3, it)
                if route:
                    pe.wait_ge(s_q_lo, n + (6 if kind != "end" else 4))
                    route_ranks(pe, R, it - TT, upper, ones, BANK_A)
                if kind == "batch":
                    value_rows(b + 1, False)

            run(pe, iteration)

        @block.scalar
        def _(act):
            def exps(n, buf):
                for i, bank, col in ROWS:
                    if i != 0:
                        act.wait_ge(s_max, 3 * n + bank + 1)
                    w, a = (i + 1) * P, ROW_AT[i]
                    last = act.activation(probs[:, buf, a:a + w], psum[:, BANK_S + bank, col:col + w], ACT.Exp,
                                          bias=neg_max[:, buf, i:i + 1],
                                          accum_out=row_sum[:, buf, i:i + 1])
                    if i != 2:
                        last.then_inc(s_exp, 1)

            def pT(n, units):
                for u in units:
                    a, z = UNIT[u]
                    act.wait_ge(s_pt, 3 * n + u + 1)
                    act.copy(pT_hi[:, a:z], psum[:, BANK_PT + u % 2, 0:z - a]).then_inc(s_pt_hi, 1)

            def qT(n, buf):
                act.wait_ge(s_q, n + 1)
                act.mul(qT_hi[:, buf], psum[:, BANK_A, :], SCALE).then_inc(s_q_hi, 1)

            def kT(it):
                act.wait_ge(s_k, it + 1)
                act.copy(kT_hi[:], psum[:, BANK_A, :]).then_inc(s_k_hi, 1)

            def oT(n, h):
                act.wait_ge(s_o, n + 1)
                act.copy(oT_hi[:, h], psum[:, BANK_B, :]).then_inc(s_o_hi, 1)

            def xT(b):
                for c in range(C):
                    act.wait_ge(s_xt, b * C + c + 1)
                    act.copy(xT_hi[:, c], psum[:, (BANK_A, BANK_C)[c % 2], :]).then_inc(s_xt_hi, 1)

            def v(b):
                for t in range(TT):
                    act.wait_ge(s_v, b * TT + t + 1)
                    act.copy(v_raw[:, t], psum[:, (BANK_C, BANK_B)[t % 2], :]).then_inc(s_v_raw, 1)

            xT(0)
            kT(0)
            qT(0, 0)
            exps(0, 0)
            qT(1, 1)
            act.wait_ge(s_wv_in, 16)
            act.copy(wv_hi[:], wo_raw[:, 0:C, :]).then_inc(s_wv_hi, 1)
            v(0)

            def iteration(b, g, it, kind, route):
                n = it * G
                exps(n + 1, 1)
                pT(n, (0, 1))
                pT(n, (2,))
                qT(n + 2, 0)
                oT(n, 0)
                exps(n + 2, 0)
                pT(n + 1, (0, 1))
                pT(n + 1, (2,))
                qT(n + 3, 1)
                oT(n + 1, 1)
                exps(n + 3, 1)
                pT(n + 2, (0, 1))
                if kind == "batch":
                    xT(b + 1)
                if kind == "group":
                    kT(it + 1)
                pT(n + 2, (2,))
                oT(n + 2, 2)
                if kind == "batch":
                    kT(it + 1)
                pT(n + 3, (0, 1))
                if kind != "end":
                    qT(n + 4, 0)
                pT(n + 3, (2,))
                oT(n + 3, 3)
                if kind != "end":
                    exps(n + 4, 0)
                if route:
                    route_exp(act, R, it - TT)
                if kind != "end":
                    qT(n + 5, 1)
                if kind == "batch":
                    v(b + 1)

            run(act, iteration)

        @block.vector
        def _(dve):
            def maxima(n, buf):
                for i, bank, col in ROWS:
                    if i != 0:
                        dve.wait_ge(s_qk, 3 * n + bank + 1)
                    last = dve.tensor_reduce(neg_max[:, buf, i:i + 1], psum[:, BANK_S + bank, col:col + (i + 1) * P],
                                             AX.X, ALU.max, negate=True)
                    if i != 2:
                        last.then_inc(s_max, 1)

            def inverse(n, buf):
                dve.wait_ge(s_exp, 3 * n + 3)
                dve.reciprocal(row_inv[:, buf], row_sum[:, buf]).then_inc(s_inv, 1)

            def softmax(n, buf):
                maxima(n, buf)
                inverse(n, buf)

            def low(lo, hi, src, done):
                dve.tensor_tensor(lo, src, hi.bitcast(F32), ALU.subtract).then_inc(done, 1)

            def pT(n, units):
                for u in units:
                    a, z = UNIT[u]
                    dve.wait_ge(s_pt_hi, 3 * n + u + 1)
                    low(pT_lo[:, a:z], pT_hi[:, a:z], psum[:, BANK_PT + u % 2, 0:z - a], s_pt_lo)

            def qT(n, buf):
                dve.wait_ge(s_q_hi, n + 1)
                dve.scalar_tensor_tensor(out=qT_lo[:, buf], in0=psum[:, BANK_A, :], scalar=SCALE,
                                         in1=qT_hi[:, buf].bitcast(F32), op0=ALU.mult, op1=ALU.subtract).then_inc(s_q_lo, 1)

            def kT(it):
                dve.wait_ge(s_k_hi, it + 1)
                low(kT_lo[:], kT_hi[:], psum[:, BANK_A, :], s_k_lo)

            def oT(n, h):
                dve.wait_ge(s_o_hi, n + 1)
                low(oT_lo[:, h], oT_hi[:, h], psum[:, BANK_B, :], s_o_lo)

            def xT(b):
                for c in range(C):
                    dve.wait_ge(s_xt_hi, b * C + c + 1)
                    low(xT_lo[:, c], xT_hi[:, c], psum[:, (BANK_A, BANK_C)[c % 2], :], s_xt_lo)

            def add_rows(it, t):
                dve.wait_ge(s_y, it * TT + t + 1)
                dve.tensor_tensor(y_acc[:, t], psum[:, (BANK_C, BANK_B)[t % 2], :], y_acc[:, t], ALU.add).then_inc(s_y_acc, 1)

            dve.memset(neg_max[:], 0.0).then_inc(s_pt_lo, 3)
            dve.memset(row_inv[:], 0.0).then_inc(s_y_acc, TT)
            xT(0)
            kT(0)
            qT(0, 0)
            softmax(0, 0)
            qT(1, 1)
            dve.wait_ge(s_wv_hi, 1)
            dve.tensor_tensor(wv_lo[:], wo_raw[:, 0:C, :], wv_hi[:].bitcast(F32), ALU.subtract).then_inc(s_wv, 2)

            def iteration(b, g, it, kind, route):
                n = it * G
                tt = it - TT
                softmax(n + 1, 1)
                pT(n, (0, 1))
                pT(n, (2,))
                qT(n + 2, 0)
                oT(n, 0)
                if route:
                    route_variance(dve, R, tt)
                softmax(n + 2, 0)
                pT(n + 1, (0, 1))
                pT(n + 1, (2,))
                qT(n + 3, 1)
                oT(n + 1, 1)
                if route:
                    route_normalize(dve, R, tt)
                    route_logits(dve, R, tt, (0, 1))
                softmax(n + 3, 1)
                pT(n + 2, (0, 1))
                if kind == "batch":
                    xT(b + 1)
                if kind == "group":
                    kT(it + 1)
                pT(n + 2, (2,))
                oT(n + 2, 2)
                if route:
                    route_logits(dve, R, tt, (2, 3, 4))
                if kind == "batch":
                    kT(it + 1)
                pT(n + 3, (0, 1))
                if kind != "end":
                    qT(n + 4, 0)
                pT(n + 3, (2,))
                oT(n + 3, 3)
                if route:
                    route_logits(dve, R, tt, (5, 6, 7))
                if kind != "end":
                    softmax(n + 4, 0)
                add_rows(it, 0)
                if route:
                    route_choose(dve, R, tt)
                add_rows(it, 1)
                if kind != "end":
                    qT(n + 5, 1)
                add_rows(it, 2)
                add_rows(it, 3)
                if route:
                    route_locate(dve, R, tt, BANK_A)

            run(dve, iteration)


def experts(nc, sem, s_passed, psum, ident, upper, ones, R, d_dram, y_dram, out_rows):
    LAST = NT - TT
    with ExitStack() as ctx:
        def sb(name, shape, dt=F32):
            return ctx.enter_context(nc.sbuf_tensor(name, shape, dt))

        d_hi, d_lo = sb("d_hi", [P, C, NE, DM], F32R), sb("d_lo", [P, C, NE, DM], F32R)
        stage = sb("stage", [P, 2, DM * NE // 2])
        token_rows, y_rows = stage[:, 0].rearrange("p (k d) -> p k d", d=DM), stage[:, 1].rearrange("p (k d) -> p k d", d=DM)
        xT_hi, xT_lo = sb("tokT_hi", [P, 2, C, P], F32R), sb("tokT_lo", [P, 2, C, P], F32R)
        token_ids, ids_now = sb("token_ids", [P, NE * ETILES], I32), sb("ids_now", [P, GROUP], I32)
        tile_at_i, tile_at = sb("tile_at_i", [P, JT], I32), sb("tile_at", [P, JT])
        counts_i, tiles_i, tiles = sb("counts_i", [P, NE], I32), sb("tiles_i", [P, NE], I32), sb("tiles", [P, NE])
        ends, starts = sb("ends", [P, NE]), sb("starts", [P, NE])
        tile_expert, tile_start, tile_step = sb("tile_expert", [P, JT]), sb("tile_start", [P, JT]), sb("tile_step", [P, JT])
        tile_expert_i, tile_number_i = sb("tile_expert_i", [P, JT], I32), sb("tile_number_i", [P, JT], I32)
        row, row_step = sb("row", [P, 2 * NT]), sb("row_step", [P, 2 * NT])

        HALF = NE // 2
        s_d_in = [sem("d_even_loaded"), sem("d_odd_loaded")]
        s_d_hi, s_d_lo, s_d_lo_pool = sem("d_hi_ready"), sem("d_lo_ready"), sem("d_lo_pool_ready")
        s_ids_in, s_tile_at, s_counts, s_tiles = (sem("token_ids_loaded"), sem("tile_numbers_ready"),
                                                  sem("expert_counts_ready"), sem("expert_tiles_ready"))
        s_step = sem("dve_step_experts")
        s_ids_now = sem("ids_copied")
        s_tok_in = [sem(f"token_rows_{k}_loaded") for k in range(GROUP)]
        s_turn, s_hi, s_lo = sem("tokens_turned"), sem("tokT_hi_ready"), sem("tokT_lo_ready")
        s_y, s_y_sb = sem("expert_rows_ready"), sem("expert_rows_copied")
        s_y_out = [sem(f"expert_rows_{k}_stored") for k in range(GROUP)]
        s_row = sem("rows_of_choices_ready")
        block = ctx.enter_context(nc.Block())
        DVE_E = 5
        PARTS = 2 * C

        def part(q, e):
            return stage[:, q % 2].rearrange("p (r e) -> p e r", e=NE)[:, e]

        def place(w, q, e):
            return w[:, q // 2, e, (q % 2) * (DM // 2):(q % 2 + 1) * (DM // 2)]

        @block.sync
        def _(sp):
            route_load(sp, R, LAST, R.r_dram[LAST])
            rows = d_dram[0:DM * DM, :].rearrange("(c p h r) e -> c h p (r e)", c=C, p=P, h=2)
            for q in range(PARTS):
                if q >= 2:
                    sp.wait_ge(s_d_lo, DVE_E * (q - 1))
                    sp.wait_ge(s_d_lo_pool, (NE - DVE_E) * (q - 1))
                sp.dma_start(stage[:, q % 2], rows[q // 2, q % 2]).then_inc(s_d_in[q % 2], 16)
                if q in (1, 3, 5):
                    route_store(sp, R, LAST + q // 2, R.x1_dram[(LAST + q // 2) * P:(LAST + q // 2 + 1) * P, :])
                if q in (2, 4, 6):
                    route_load(sp, R, LAST + q // 2, R.r_dram[LAST + q // 2])
            route_store(sp, R, NT - 1, R.x1_dram[(NT - 1) * P:, :])
            sp.wait_ge(R.s_placed, 32 * (NT + 1))
            sp.dma_start(token_ids[:], R.table.rearrange("(p n) a -> p (n a)", p=P)).then_inc(s_ids_in, 16)
            with sp.Fori(0, TURNS) as i:
                for k in range(GROUP):
                    wait_apart(sp, s_y_sb, i * GROUP + k + 1, s_passed)
                    sp.dma_start(y_dram[bass.ds((i * GROUP + k) * P, P), :], y_rows[:, k]).then_inc(s_y_out[k], 16)
            for k in range(GROUP):
                sp.wait_ge(s_y_out[k], 16 * (TURNS + 1))

        @block.gpsimd
        def _(pool):
            pool.iota(tile_at_i[:], pattern=[[1, JT]], base=0, channel_multiplier=0).then_inc(s_tile_at, 1)
            for q in range(PARTS):
                for e in range(DVE_E, NE):
                    pool.wait_ge(s_d_hi, q * NE + e + 1)
                    pool.tensor_tensor(place(d_lo, q, e), part(q, e), place(d_hi, q, e).bitcast(F32),
                                       ALU.subtract).then_inc(s_d_lo_pool, 1)
                if q % 2 == 0:
                    route_rstd(pool, R, LAST + q // 2)
                else:
                    route_place(pool, R, LAST + q // 2)
            pool.wait_ge(s_ids_in, 16)
            pool.wait_ge(R.s_x1_out, 16 * (NT + 1))
            pool.wait_ge(s_d_lo, DVE_E * PARTS)
            pool.wait_ge(s_tiles, 1)
            with pool.Fori(0, TURNS) as i:
                for k in range(GROUP):
                    j = i * GROUP + k
                    number = pool.value_load(tile_number_i[0:1, bass.ds(j, 1)], min_val=0, max_val=NE * ETILES - 1)
                    wait_apart(pool, s_turn, j + 1, s_passed)
                    pool.tensor_copy(ids_now[:, k:k + 1], token_ids[:, bass.ds(number, 1)]).then_inc(s_ids_now, 1)
                    wait_apart(pool, s_ids_now, j + 1, s_passed)
                    pool.indirect_dma_start(out=token_rows[:, k], out_offset=None, in_=R.x1_dram,
                                            in_offset=bass.IndirectOffsetOnAxis(ap=ids_now[:, k:k + 1], axis=0)
                                            ).then_inc(s_tok_in[k], 16)

        @block.tensor
        def _(pe):
            for t in range(LAST, NT):
                route_ranks(pe, R, t, upper, ones, 0)
            pe.wait_ge(s_counts, 1)
            pe.matmul(psum[:, 1, 0:NE], ones[:], R.counts[:], start=True, stop=True).then_inc(s_counts, 1)
            pe.wait_ge(s_tiles, 1)
            pe.wait_ge(s_d_lo, DVE_E * PARTS)
            pe.wait_ge(s_d_lo_pool, (NE - DVE_E) * PARTS)

            def turn(j, k, loaded):
                pe.wait_ge(s_tok_in[k], loaded)
                for c in range(C):
                    last = pe.transpose(psum[:, 2 + k % 2, c * P:(c + 1) * P], token_rows[:, k, c * P:(c + 1) * P], ident[:])
                last.then_inc(s_turn, 1)

            def multiply(j, k):
                e = pe.value_load(tile_expert_i[0:1, bass.ds(j, 1)], min_val=0, max_val=NE - 1)
                pe.wait_ge(s_lo, j + 1)
                dst = psum[:, 4 + k, :]
                for c in range(C):
                    hi = d_hi[:, c, bass.ds(e, 1), :].rearrange("p a n -> p (a n)")
                    lo = d_lo[:, c, bass.ds(e, 1), :].rearrange("p a n -> p (a n)")
                    pe.matmul(dst, xT_hi[:, k % 2, c], hi, start=c == 0, stop=False)
                    pe.matmul(dst, xT_hi[:, k % 2, c], lo, start=False, stop=False)
                    last = pe.matmul(dst, xT_lo[:, k % 2, c], hi, start=False, stop=c == C - 1)
                last.then_inc(s_y, 1)

            def turn_of_loop(i, more):
                for k in range(GROUP):
                    j = i * GROUP + k
                    if k < GROUP - 1:
                        turn(j + 1, k + 1, 16 * (i + 1))
                    elif more:
                        turn(j + 1, 0, 16 * (i + 2))
                    multiply(j, k)

            turn(0, 0, 16)
            with pe.Fori(0, TURNS - 1) as i:
                turn_of_loop(i, True)
            turn_of_loop(TURNS - 1, False)

        @block.scalar
        def _(act):
            for q in range(PARTS):
                act.wait_ge(s_d_in[q % 2], 16 * (q // 2 + 1))
                for e in range(NE):
                    act.copy(place(d_hi, q, e), part(q, e)).then_inc(s_d_hi, 1)
                    if q % 2 and e == 3:
                        route_exp(act, R, LAST + q // 2)

            def high(j, k):
                act.wait_ge(s_turn, GROUP + j + 1)
                act.copy(xT_hi[:, k % 2].rearrange("p c n -> p (c n)"), psum[:, 2 + k % 2, :]).then_inc(s_hi, 1)

            def turn_of_loop(i, more):
                for k in range(GROUP):
                    j = i * GROUP + k
                    if k < GROUP - 1 or more:
                        high(j + 1, (k + 1) % GROUP)
                    act.wait_ge(s_y, j + 1)
                    act.wait_ge(s_y_out[k], 16 * (i + 1))
                    act.copy(y_rows[:, k], psum[:, 4 + k, :]).then_inc(s_y_sb, 1)

            high(0, 0)
            with act.Fori(0, TURNS - 1) as i:
                turn_of_loop(i, True)
            turn_of_loop(TURNS - 1, False)

        @block.vector
        def _(dve):
            steps = 0

            def after(ins):
                nonlocal steps
                steps += 1
                ins.then_inc(s_step, 1)
                dve.wait_ge(s_step, steps)

            for k in range(GROUP):
                dve.memset(row[:, k:k + 1], 0.0).then_inc(s_y_out[k], 16)
            dve.memset(row_step[:], 0.0).then_inc(s_turn, GROUP)
            for q in range(PARTS):
                t = LAST + q // 2
                for e in range(DVE_E):
                    dve.wait_ge(s_d_hi, q * NE + e + 1)
                    dve.tensor_tensor(place(d_lo, q, e), part(q, e), place(d_hi, q, e).bitcast(F32),
                                      ALU.subtract).then_inc(s_d_lo, 1)
                if q % 2 == 0:
                    route_variance(dve, R, t)
                    route_normalize(dve, R, t)
                    route_logits(dve, R, t, range(NE))
                    route_choose(dve, R, t)
                else:
                    route_locate(dve, R, t, 0)
            dve.tensor_copy(row[:, 0:1], R.counts[:, 0:1]).then_inc(s_counts, 1)
            dve.wait_ge(s_counts, 2)
            after(dve.tensor_scalar(counts_i[:], psum[:, 1, 0:NE], float(P - 1), None, ALU.add))
            after(dve.tensor_scalar(tiles_i[:], counts_i[:], P_SHIFT, None, ALU.logical_shift_right))
            after(dve.tensor_copy(tiles[:], tiles_i[:]))
            after(dve.tensor_copy(ends[:, 0:1], tiles[:, 0:1]))
            for e in range(1, NE):
                after(dve.tensor_tensor(ends[:, e:e + 1], ends[:, e - 1:e], tiles[:, e:e + 1], ALU.add))
            after(dve.tensor_tensor(starts[:], ends[:], tiles[:], ALU.subtract))
            dve.wait_ge(s_tile_at, 1)
            after(dve.tensor_copy(tile_at[:], tile_at_i[:]))
            after(dve.tensor_scalar(tile_expert[:], tile_at[:], ends[:, 0:1], None, ALU.is_ge))
            after(dve.tensor_scalar(tile_start[:], tile_expert[:], tiles[:, 0:1], None, ALU.mult))
            for e in range(1, NE):
                after(dve.tensor_scalar(tile_step[:], tile_at[:], ends[:, e:e + 1], None, ALU.is_ge))
                after(dve.tensor_tensor(tile_expert[:], tile_expert[:], tile_step[:], ALU.add))
                after(dve.scalar_tensor_tensor(out=tile_start[:], in0=tile_step[:], scalar=tiles[:, e:e + 1],
                                               in1=tile_start[:], op0=ALU.mult, op1=ALU.add))
            after(dve.tensor_scalar(tile_expert[:], tile_expert[:], float(NE - 1), None, ALU.min))
            after(dve.tensor_tensor(tile_step[:], tile_at[:], tile_start[:], ALU.subtract))
            after(dve.tensor_scalar(tile_step[:], tile_step[:], float(ETILES - 1), None, ALU.min))
            after(dve.scalar_tensor_tensor(out=tile_number_i[:], in0=tile_expert[:], scalar=float(ETILES),
                                           in1=tile_step[:], op0=ALU.mult, op1=ALU.add))
            dve.tensor_copy(tile_expert_i[:], tile_expert[:]).then_inc(s_tiles, 1)

            def low(j, k):
                dve.wait_ge(s_hi, j + 1)
                dve.tensor_tensor(xT_lo[:, k % 2].rearrange("p c n -> p (c n)"), psum[:, 2 + k % 2, :],
                                  xT_hi[:, k % 2].rearrange("p c n -> p (c n)").bitcast(F32), ALU.subtract).then_inc(s_lo, 1)

            with dve.Fori(0, TURNS) as i:
                for k in range(GROUP):
                    low(i * GROUP + k, k)
            flat = R.experts[:].rearrange("p k t -> p (k t)")
            after(dve.tensor_scalar(starts[:], starts[:], float(P), None, ALU.mult))
            after(dve.tensor_copy(row[:], R.all_ranks[:].rearrange("p k t -> p (k t)")))
            for e in range(NE):
                after(dve.tensor_scalar(row_step[:], flat, float(e), starts[:, e:e + 1], ALU.is_equal, ALU.mult))
                after(dve.tensor_tensor(row[:], row[:], row_step[:], ALU.add))
            after(dve.tensor_copy(R.row_i[:], row[:]))

    combine(nc, sem, s_passed, R, y_dram, out_rows)


def combine(nc, sem, s_passed, R, y_dram, out_rows):
    BUF = 4
    with ExitStack() as ctx:
        def sb(name, shape, dt=F32):
            return ctx.enter_context(nc.sbuf_tensor(name, shape, dt))

        x1, y0, y1 = sb("c_x1", [P, BUF, DM]), sb("c_y0", [P, BUF, DM]), sb("c_y1", [P, BUF, DM])
        first, z, y_out = sb("c_first", [P, 2, DM]), sb("c_z", [P, 2, DM]), sb("c_out", [P, BUF, DM])
        row_now, share = sb("c_row_now", [P, BUF, 2], I32), sb("c_share", [P, 2, 2])
        stats, mean_var, var_eps = sb("c_stats", [P, 2, 6]), sb("c_mean_var", [P, 2, 2]), sb("c_var_eps", [P, 2])
        rstd, shift = sb("c_rstd", [P, 2]), sb("c_shift", [P, 2])
        s_x1 = [sem(f"c_x1_{k}_loaded") for k in range(BUF)]
        s_y = [sem(f"c_rows_{k}_loaded") for k in range(BUF)]
        s_row_now, s_used, s_share, s_first = sem("c_row_copied"), sem("c_rows_used"), sem("c_share_ready"), sem("c_first_ready")
        s_step, s_var, s_rstd, s_shift, s_norm = (sem("c_step"), sem("c_var_ready"), sem("c_rstd_ready"),
                                                  sem("c_shift_ready"), sem("c_normalized"))
        s_out = [sem(f"c_out_{k}_stored") for k in range(BUF)]
        block = ctx.enter_context(nc.Block())
        OUTER = NT // BUF

        @block.sync
        def _(sp):
            with sp.Fori(0, OUTER) as i:
                for k in range(BUF):
                    t = i * BUF + k
                    wait_apart(sp, s_used, t + 1, s_passed)
                    sp.dma_start(x1[:, k], R.x1_dram[bass.ds(t * P, P), :]).then_inc(s_x1[k], 16)

        @block.gpsimd
        def _(pool):
            def gather(t, k):
                wait_apart(pool, s_used, t + 1, s_passed)
                for c in range(2):
                    pool.tensor_copy(row_now[:, k, c:c + 1], R.row_i[:, bass.ds(c * NT + t, 1)]).then_inc(s_row_now, 1)
                wait_apart(pool, s_row_now, 2 * t + 2, s_passed)
                for c, y in enumerate((y0, y1)):
                    pool.indirect_dma_start(out=y[:, k], out_offset=None, in_=y_dram,
                                            in_offset=bass.IndirectOffsetOnAxis(ap=row_now[:, k, c:c + 1], axis=0)
                                            ).then_inc(s_y[k], 16)

            def rstd_of(t, k):
                wait_apart(pool, s_var, t + 1, s_passed)
                pool.tensor_tensor(rstd[:, k % 2:k % 2 + 1], var_eps[:, k % 2:k % 2 + 1], R.minus_half[:], ALU.pow).then_inc(s_rstd, 1)

            def tiles(i, more):
                for k in range(BUF):
                    if k < 2 or more:
                        gather(i * BUF + k + 2, (k + 2) % BUF)
                    rstd_of(i * BUF + k, k)

            gather(0, 0)
            gather(1, 1)
            with pool.Fori(0, OUTER - 1) as i:
                tiles(i, True)
            tiles(OUTER - 1, False)

        @block.scalar
        def _(act):
            def weigh(t, k, i):
                act.wait_ge(s_share, t + 1)
                act.wait_ge(s_y[k], 32 * (i + 1))
                act.activation(first[:, k % 2], y0[:, k], ACT.Copy, scale=share[:, k % 2, 0:1]).then_inc(s_first, 1)

            def normalize(t, k, i):
                act.wait_ge(s_shift, t + 1)
                act.wait_ge(s_out[k], 16 * (i + 1))
                act.activation(y_out[:, k], z[:, k % 2], ACT.Identity, bias=shift[:, k % 2:k % 2 + 1],
                               scale=rstd[:, k % 2:k % 2 + 1]).then_inc(s_norm, 1)
                wait_apart(act, s_norm, t + 1, s_passed)
                act.dma_start(out_rows[bass.ds(t, 1)].rearrange("a p d -> (a p) d"), y_out[:, k]).then_inc(s_out[k], 16)

            weigh(0, 0, 0)

            def tiles(i, more):
                for k in range(BUF):
                    if k < BUF - 1:
                        weigh(i * BUF + k + 1, k + 1, i)
                    elif more:
                        weigh(i * BUF + k + 1, 0, i + 1)
                    normalize(i * BUF + k, k, i)

            with act.Fori(0, OUTER - 1) as i:
                tiles(i, True)
            tiles(OUTER - 1, False)
            for k in range(BUF):
                act.wait_ge(s_out[k], 16 * (OUTER + 1))

        @block.vector
        def _(dve):
            STEPS = 3

            def shares(t, k):
                dve.tensor_copy(share[:, k % 2], R.shares[:, :, bass.ds(t, 1)].rearrange("p c a -> p (c a)")).then_inc(s_share, 1)

            def total(t, k, i):
                b = k % 2
                dve.wait_ge(s_first, t + 1)
                dve.wait_ge(s_x1[k], 16 * (i + 1))
                dve.tensor_tensor(first[:, b], first[:, b], x1[:, k], ALU.add).then_inc(s_step, 1)
                wait_apart(dve, s_step, STEPS * t + 1, s_passed)
                dve.scalar_tensor_tensor(out=z[:, b], in0=y1[:, k], scalar=share[:, b, 1:2], in1=first[:, b],
                                         op0=ALU.mult, op1=ALU.add).then_inc(s_used, 1)
                wait_apart(dve, s_used, BUF + t + 1, s_passed)
                dve.bn_stats(stats[:, b], z[:, b]).then_inc(s_step, 1)
                wait_apart(dve, s_step, STEPS * t + 2, s_passed)
                dve.bn_aggr(mean_var[:, b], stats[:, b]).then_inc(s_step, 1)
                wait_apart(dve, s_step, STEPS * t + 3, s_passed)
                dve.tensor_scalar(var_eps[:, b:b + 1], mean_var[:, b, 1:2], EPS, None, ALU.add).then_inc(s_var, 1)

            def shift_of(t, k):
                b = k % 2
                dve.wait_ge(s_rstd, t + 1)
                dve.scalar_tensor_tensor(out=shift[:, b:b + 1], in0=mean_var[:, b, 0:1], scalar=-1.0, in1=rstd[:, b:b + 1],
                                         op0=ALU.mult, op1=ALU.mult).then_inc(s_shift, 1)

            dve.memset(x1[:, 0], 0.0).then_inc(s_used, BUF)
            for k in range(BUF):
                dve.memset(y_out[:, k], 0.0).then_inc(s_out[k], 16)
            shares(0, 0)
            total(0, 0, 0)

            def tiles(i, more):
                for k in range(BUF):
                    t = i * BUF + k
                    if k < BUF - 1:
                        shares(t + 1, k + 1)
                        total(t + 1, k + 1, i)
                    elif more:
                        shares(t + 1, 0)
                        total(t + 1, 0, i + 1)
                    shift_of(t, k)

            with dve.Fori(0, OUTER - 1) as i:
                tiles(i, True)
            tiles(OUTER - 1, False)


_INS = ['L0_attn_x', 'L0_attn_wq', 'L0_attn_wk', 'L0_attn_wv', 'L0_attn_wo', 'L0_ffn_gate_w', 'L0_ffn_W',
        'L0_ffn_atoms', 'L0_ffn_expert_atom_weights', 'L0_ffn_importance', 'L0_ffn_mask_idx']
_OUTS = [((NB, T, DM), 'float32')]


def kernel(**inputs):
    import numpy as _np
    import concourse.bacc as _bacc
    from concourse import mybir as _mybir
    from concourse.bass_utils import run_bass_kernel_spmd as _run

    nc = _bacc.Bacc("TRN2", target_bir_lowering=False, num_devices=1)
    arrays, args = {}, []
    for name in _INS:
        a = _np.ascontiguousarray(inputs[name])
        arrays[f"in_{name}_dram"] = a
        args.append(nc.dram_tensor(f"in_{name}_dram", a.shape, _mybir.dt.from_np(a.dtype), kind="ExternalInput").ap())
    for i, (shape, dtype) in enumerate(_OUTS):
        dt = _mybir.dt.from_np(_np.dtype(dtype))
        args.append(nc.dram_tensor(f"out_{i}_dram", shape, dt, kind="ExternalOutput").ap())
    build(nc, *args)
    r = _run(nc, [arrays], core_ids=[0])
    got = tuple(r.results[0][f"out_{i}_dram"] for i in range(len(_OUTS)))
    return got[0]
```

```python
from contextlib import ExitStack

import concourse.bass as bass
from concourse import mybir

F32 = mybir.dt.float32
F32R = mybir.dt.float32r
BF16 = mybir.dt.bfloat16
I32 = mybir.dt.int32
U32 = mybir.dt.uint32
ALU = mybir.AluOpType
ACT = mybir.ActivationFunctionType
AX = mybir.AxisListType

P = 128
NB, T, DM = 8, 512, 512
H, HKV, HD = 16, 4, 128
G = H // HKV
C = DM // P
TT = T // P
NIT = NB * HKV
NE, NA, NS = 8, 64, 4096
NJ = NS // P
QUAD = 4
NT = NB * TT
SCALE = float(HD) ** -0.5
EPS = 1e-5
MASKED = -1e38
CAP = NB * T
ETILES = CAP // P
TILES = (2 * CAP + NE * (P - 1)) // P
GROUP = 4
TURNS = -(-TILES // GROUP)
JT = GROUP * TURNS
P_SHIFT = P.bit_length() - 1
PLACE_SHIFT = (NE * ETILES).bit_length() - 1
SHIFT = DM.bit_length() - 1

ROWS = [(3, 0, 0), (2, 1, 0), (0, 1, 384), (1, 2, 0)]
KEYS = [(0, 0, 0), (1, 1, 0), (3, 1, 384), (2, 2, 0)]
PACK = 1280
ROW_AT = {i: 512 * bank + col for i, bank, col in ROWS}
KEY_AT = {j: 512 * bank + col for j, bank, col in KEYS}
UNIT = [(0, 512), (512, 1024), (1024, 1280)]

BANK_S, BANK_A, BANK_B, BANK_C = 0, 5, 6, 7
BANKS_PT = (3, 4, BANK_C)


class Routing:

    def __init__(self, sb, sem, psum, r_dram, x1_dram, table):
        self.psum, self.r_dram, self.x1_dram, self.table = psum, r_dram, x1_dram, table
        self.product8 = sb("route_product8", [P, 2, NE])
        self.stats = sb("route_stats", [P, 6])
        self.mean_var = sb("route_mean_var", [P, 2])
        self.var_eps = sb("route_var_eps", [P, 1])
        self.rstd = sb("route_rstd", [P, 1])
        self.minus_half = sb("route_minus_half", [P, 1])
        self.logits = sb("route_logits", [P, NE])
        self.clipped = sb("route_clipped", [P, NE])
        self.best = sb("route_best", [P, 8])
        self.best_at = sb("route_best_at", [P, 8], U32)
        self.gap = sb("route_gap", [P, 2])
        self.number = sb("route_number", [P, NE])
        self.expert = sb("route_expert", [P, 2])
        self.rank = sb("route_rank", [P, 2])
        self.chosen = sb("route_chosen", [P, 3, NE])
        self.counts = sb("route_counts", [P, NE])
        self.ranks = sb("route_ranks", [P, NE])
        self.rank_i = sb("route_rank_i", [P, 2], I32)
        self.tile_i = sb("route_tile_i", [P, 2], I32)
        self.place_i = sb("route_place_i", [P, 2], I32)
        self.tile_f = sb("route_tile_f", [P, 2])
        self.place_tile = sb("route_place_tile", [P, 2], I32)
        self.tokens = sb("route_tokens", [P, NT], I32)
        self.token_now = sb("route_token_now", [P, 1], I32)
        self.share_sum = sb("route_share_sum", [P, 1])
        self.row_i = sb("route_row_i", [P, 2 * NT], I32)
        self.experts = sb("route_experts", [P, 2, NT])
        self.all_ranks = sb("route_all_ranks", [P, 2, NT])
        self.shares = sb("route_shares", [P, 2, NT])
        self.passed = sem("route_waits_passed")
        self.s_rows_in = sem("route_rows_in")
        self.s_chain = sem("route_chain")
        self.s_var = sem("route_var")
        self.s_rstd_ready = sem("route_rstd_ready")
        self.s_x1_ready = sem("route_x1_ready")
        self.s_x1_out = sem("route_x1_out")
        self.s_gap_ready = sem("route_gap_ready")
        self.s_gap_exp = sem("route_gap_exp")
        self.s_chosen_ready = sem("route_chosen_ready")
        self.s_ranked = sem("route_ranked")
        self.s_ranks_read = sem("route_ranks_read")
        self.s_place_ready = sem("route_place_ready")
        self.s_placed = sem("route_placed")
        self.s_token_copied = sem("route_token_copied")

    def place_early(self, sb):
        self.gate = sb("route_gate", [P, NE, DM])
        self.rows = sb("route_rows", [P, DM])
        self.product = sb("route_product", [P, 2, DM])


class First:

    def __init__(self, sb, sem):
        self.x_in = sb("x_in", [P, TT, DM])
        self.xT_hi, self.xT_lo = sb("xT_hi", [P, C, T], F32R), sb("xT_lo", [P, C, T], F32R)
        self.w_raw = sb("w_raw", [P, 1 + G, C, HD])
        self.w_hi, self.w_lo = sb("w_hi", [P, 1 + G, C, HD], F32R), sb("w_lo", [P, 1 + G, C, HD], F32R)
        self.wo_raw = sb("wo_raw", [P, G, DM])
        self.wv_hi, self.wv_lo = sb("wv_hi", [P, C, HKV * HD], F32R), sb("wv_lo", [P, C, HKV * HD], F32R)
        self.s_x_in = sem("x_loaded")
        self.s_w_in = [sem(f"weight_slot_{j}_loaded") for j in range(1 + G)]
        self.s_wv_in = sem("wv_loaded")
        self.s_w_split = sem("weight_slots_split")
        self.s_wv_hi, self.s_wv = sem("wv_hi_ready"), sem("wv_split")
        self.s_pool_step = sem("pool_step")
        self.s_xt, self.s_xt_hi, self.s_xt_lo = sem("xT_ready"), sem("xT_hi_ready"), sem("xT_lo_ready")


def build(nc, x, wq, wk, wv, wo, gate_w, w_ffn, atoms, eaw, importance, mask_idx, out):
    r_dram = nc.dram_tensor("attn_residual", (NT - TT, P, DM), F32, kind="Internal").ap()
    d_dram = nc.dram_tensor("expert_weights", (DM * DM + P, NE), F32, kind="Internal").ap()
    x_rows = x.rearrange("b (t p) d -> b p t d", p=P)
    x1_dram = nc.dram_tensor("x1", (NT * P, DM), F32, kind="Internal").ap()
    table = nc.dram_tensor("expert_tokens", (NE * CAP, 1), I32, kind="Internal").ap()
    y_dram = nc.dram_tensor("expert_rows", (JT * P, DM), F32, kind="Internal").ap()
    r_store = r_dram.rearrange("(b t) p d -> b p t d", t=TT)
    out_rows = out.rearrange("b (t p) d -> (b t) p d", p=P)
    wq_v = wq.rearrange("(c p) n -> p c n", p=P)
    wk_v = wk.rearrange("(c p) n -> p c n", p=P)
    wv_v = wv.rearrange("(c p) n -> p c n", p=P)
    wo_v = wo.rearrange("(h p) n -> p h n", p=P)

    with ExitStack() as top:
        def sem(name):
            return top.enter_context(nc.semaphore(name))

        ident = top.enter_context(nc.sbuf_tensor("ident", [P, P], F32))
        lower = top.enter_context(nc.sbuf_tensor("lower", [P, P], F32))
        upper = top.enter_context(nc.sbuf_tensor("upper", [P, P], F32))
        ones = top.enter_context(nc.sbuf_tensor("ones", [P, P], F32))
        psum = top.enter_context(nc.psum_tensor("psum", [P, 8, 512], F32))
        causal_bf = top.enter_context(nc.sbuf_tensor("causal_bf", [P, P], BF16))
        ident_bf = top.enter_context(nc.sbuf_tensor("ident_bf", [P, P], BF16))
        row_i = top.enter_context(nc.sbuf_tensor("row_i", [P, NJ], I32))
        entry_sum = top.enter_context(nc.sbuf_tensor("entry_sum", [P, NJ, NE], F32))
        s_passed = sem("waits_passed")
        def sb(name, shape, dt=F32):
            return top.enter_context(nc.sbuf_tensor(name, shape, dt))

        R = Routing(sb, sem, psum, r_dram, x1_dram, table)
        y_acc = top.enter_context(nc.sbuf_tensor("y_acc", [P, TT, DM], F32))
        with ExitStack() as early:
            def early_sb(name, shape, dt=F32):
                return early.enter_context(nc.sbuf_tensor(name, shape, dt))

            F = First(early_sb, sem)
            R.place_early(early_sb)
            expert_entries(nc, sem, psum, ident, ident_bf, causal_bf, lower, upper, ones, R, F, row_i, entry_sum, d_dram,
                           x_rows, wq_v, wk_v, wv_v, gate_w, w_ffn, atoms, eaw, importance, mask_idx)
            attention(nc, sem, s_passed, psum, ident, ident_bf, causal_bf, upper, ones, R, F, row_i, entry_sum, y_acc, x_rows,
                      r_store, d_dram, wq_v, wk_v, wo_v)
        experts(nc, sem, s_passed, psum, ident, upper, ones, R, y_acc, gate_w, d_dram, y_dram)
        combine(nc, sem, s_passed, R, y_dram, out_rows)


def route_load(sp, R, tt, row):
    wait_apart(sp, R.s_x1_out, 16 * (tt + 1), R.passed)
    wait_apart(sp, R.s_ranks_read, tt + 1, R.passed)
    sp.dma_start(R.rows[:], row).then_inc(R.s_rows_in, 16)


def route_store(sp, R, tt, row):
    wait_apart(sp, R.s_x1_ready, tt + 1, R.passed)
    sp.dma_start(row, R.rows[:]).then_inc(R.s_x1_out, 16)


def route_rstd(pool, R, tt):
    wait_apart(pool, R.s_var, tt + 1, R.passed)
    pool.tensor_tensor(R.rstd[:], R.var_eps[:], R.minus_half[:], ALU.pow).then_inc(R.s_rstd_ready, 1)


def route_place(pool, R, tt):
    wait_apart(pool, R.s_placed, 32 * (tt + 1), R.passed)
    pool.tensor_copy(R.token_now[:], R.tokens[:, bass.ds(tt, 1)]).then_inc(R.s_token_copied, 1)
    wait_apart(pool, R.s_token_copied, tt + 1, R.passed)
    wait_apart(pool, R.s_place_ready, tt + 1, R.passed)
    for k in range(2):
        pool.indirect_dma_start(out=R.table, out_offset=bass.IndirectOffsetOnAxis(ap=R.place_tile[:, k:k + 1], axis=0),
                                in_=R.token_now[:], in_offset=None).then_inc(R.s_placed, 16)


def route_exp(act, R, tt):
    act.wait_ge(R.s_gap_ready, tt + 1)
    act.activation(R.gap[:, 1:2], R.gap[:, 0:1], ACT.Exp).then_inc(R.s_gap_exp, 1)


def route_ranks(pe, R, tt, upper, ones, bank):
    pe.wait_ge(R.s_chosen_ready, tt + 1)
    pe.wait_ge(R.s_ranks_read, tt + 1)
    pe.matmul(R.psum[:, bank, 0:NE], upper[:], R.chosen[:, 2], start=True, stop=False)
    pe.matmul(R.psum[:, bank, 0:NE], ones[:], R.counts[:], start=False, stop=True).then_inc(R.s_ranked, 1)


CHAIN = 24


def route_step(dve, R, tt, k, ins):
    ins.then_inc(R.s_chain, 1)
    wait_apart(dve, R.s_chain, tt * CHAIN + k, R.passed)


def route_variance(dve, R, tt):
    dve.wait_ge(R.s_rows_in, 16 * (tt + 1))
    route_step(dve, R, tt, 1, dve.bn_stats(R.stats[:], R.rows[:]))
    route_step(dve, R, tt, 2, dve.bn_aggr(R.mean_var[:], R.stats[:]))
    dve.tensor_scalar(R.var_eps[:], R.mean_var[:, 1:2], EPS, None, ALU.add).then_inc(R.s_var, 1)


def route_normalize(dve, R, tt):
    dve.wait_ge(R.s_rstd_ready, tt + 1)
    dve.tensor_scalar(R.rows[:], R.rows[:], R.mean_var[:, 0:1], R.rstd[:], ALU.subtract, ALU.mult).then_inc(R.s_x1_ready, 1)
    dve.wait_ge(R.s_x1_ready, tt + 1)


def route_logits(dve, R, tt, experts):
    for e in experts:
        dve.tensor_tensor_reduce(R.product[:, e % 2], R.rows[:], R.gate[:, e], 1.0, 0.0, ALU.mult, ALU.add,
                                 R.logits[:, e:e + 1]).then_inc(R.s_chain, 1)
        if e:
            wait_apart(dve, R.s_chain, tt * CHAIN + 2 + e, R.passed)


def route_choose(dve, R, tt):
    step = lambda k, ins: route_step(dve, R, tt, k, ins)
    wait_apart(dve, R.s_chain, tt * CHAIN + 10, R.passed)
    step(11, dve.tensor_scalar(R.clipped[:], R.logits[:], 50.0, -50.0, ALU.min, ALU.max))
    step(12, dve.max(R.best[:], R.clipped[:]))
    dve.tensor_tensor(R.gap[:, 0:1], R.best[:, 1:2], R.best[:, 0:1], ALU.subtract).then_inc(R.s_gap_ready, 1)
    step(13, dve.max_index(R.best_at[:], R.best[:], R.clipped[:]))
    step(14, dve.tensor_copy(R.expert[:], R.best_at[:, 0:2]))
    for k in range(2):
        last = dve.tensor_scalar(R.chosen[:, k], R.number[:], R.expert[:, k:k + 1], None, ALU.is_equal)
    step(15, last)
    dve.tensor_tensor(R.chosen[:, 2], R.chosen[:, 0], R.chosen[:, 1], ALU.add).then_inc(R.s_chosen_ready, 1)
    dve.tensor_copy(R.experts[:, :, bass.ds(tt, 1)].rearrange("p k a -> p (k a)"), R.expert[:])
    dve.wait_ge(R.s_gap_exp, tt + 1)
    step(16, dve.tensor_scalar(R.share_sum[:], R.gap[:, 1:2], 1.0, None, ALU.add))
    step(17, dve.reciprocal(R.share_sum[:], R.share_sum[:]))
    dve.tensor_copy(R.shares[:, 0, bass.ds(tt, 1)], R.share_sum[:])
    dve.tensor_tensor(R.shares[:, 1, bass.ds(tt, 1)], R.share_sum[:], R.gap[:, 1:2], ALU.mult)


def route_locate(dve, R, tt, bank):
    step = lambda k, ins: route_step(dve, R, tt, k, ins)
    dve.wait_ge(R.s_ranked, tt + 1)
    dve.tensor_copy(R.ranks[:], R.psum[:, bank, 0:NE]).then_inc(R.s_ranks_read, 1)
    wait_apart(dve, R.s_ranks_read, tt + 2, R.passed)
    step(18, dve.tensor_tensor(R.counts[:], R.counts[:], R.chosen[:, 2], ALU.add))
    for k in range(2):
        step(19 + k, dve.tensor_tensor_reduce(R.product8[:, k], R.ranks[:], R.chosen[:, k], 1.0, 0.0, ALU.mult, ALU.add,
                                              R.rank[:, k:k + 1]))
    step(21, dve.tensor_copy(R.rank_i[:], R.rank[:]))
    step(22, dve.tensor_scalar(R.tile_i[:], R.rank_i[:], P_SHIFT, None, ALU.logical_shift_right))
    step(23, dve.tensor_scalar(R.place_i[:], R.rank_i[:], P - 1, PLACE_SHIFT, ALU.bitwise_and, ALU.logical_shift_left))
    step(24, dve.scalar_tensor_tensor(out=R.tile_f[:], in0=R.expert[:], scalar=float(ETILES), in1=R.tile_i[:],
                                      op0=ALU.mult, op1=ALU.add))
    dve.tensor_copy(R.all_ranks[:, :, bass.ds(tt, 1)].rearrange("p k a -> p (k a)"), R.rank[:])
    dve.wait_ge(R.s_placed, 32 * (tt + 1))
    dve.tensor_tensor(R.place_tile[:], R.tile_f[:], R.place_i[:], ALU.add).then_inc(R.s_place_ready, 1)


def load_slot(sp, F, wq_v, wk_v, j, g):
    src = wk_v[:, :, bass.ds(g * HD, HD)] if j == 0 else wq_v[:, :, bass.ds((g * G + j - 1) * HD, HD)]
    sp.dma_start(F.w_raw[:, j], src).then_inc(F.s_w_in[j], 16)


def split_slot(pool, F, j, k, passed):
    pool_round(pool, F.w_hi[:, j], F.w_raw[:, j]).then_inc(F.s_pool_step, 1)
    wait_apart(pool, F.s_pool_step, k + 1, passed)
    pool.tensor_tensor(F.w_lo[:, j], F.w_raw[:, j], F.w_hi[:, j].bitcast(F32), ALU.subtract).then_inc(F.s_w_split, 1)


def high_xT(act, F, psum, b, chunks):
    for c in chunks:
        act.wait_ge(F.s_xt, b * C + c + 1)
        act.copy(F.xT_hi[:, c], psum[:, (BANK_A, BANK_C)[c % 2], :]).then_inc(F.s_xt_hi, 1)


def low_xT(dve, F, psum, b, chunks):
    for c in chunks:
        dve.wait_ge(F.s_xt_hi, b * C + c + 1)
        dve.tensor_tensor(F.xT_lo[:, c], psum[:, (BANK_A, BANK_C)[c % 2], :], F.xT_hi[:, c].bitcast(F32),
                          ALU.subtract).then_inc(F.s_xt_lo, 1)


def turn_xT(pe, F, psum, ident, b, chunks):
    for c in chunks:
        if c >= 2:
            pe.wait_ge(F.s_xt_lo, b * C + c - 1)
        for t in range(TT):
            last = pe.transpose(psum[:, (BANK_A, BANK_C)[c % 2], t * P:(t + 1) * P], F.x_in[:, t, c * P:(c + 1) * P],
                                ident[:])
        last.then_inc(F.s_xt, 1)


def expert_entries(nc, sem, psum, ident, ident_bf, causal_bf, lower, upper, ones, R, F, row_i, entry_sum, d_dram, x_rows,
                   wq_v, wk_v, wv_v, gate_w, w_ffn, atoms, eaw, importance, mask_idx):
    with ExitStack() as ctx:
        def sb(name, shape, dt=F32):
            return ctx.enter_context(nc.sbuf_tensor(name, shape, dt))

        idx_i, idx_r_i, idx_c_i = sb("idx_i", [P, NJ], I32), sb("idx_r_i", [P, NJ], I32), sb("idx_c_i", [P, NJ], I32)
        idx_f, row_f, dup, gap_f = sb("idx_f", [P, NJ]), sb("row_f", [P, NJ]), sb("dup", [P, NJ]), sb("gap_f", [P, NJ])
        spare_i, spare_f = sb("spare_i", [P, 1], I32), sb("spare_f", [P, 1])
        entry = sb("entry", [P, NJ, NE])
        same, same_lower = sb("same", [P, 2, QUAD, P]), sb("same_lower", [P, 2, QUAD, P])
        zeros_i = sb("zeros_i", [P, NE * ETILES], I32)
        number_i = sb("number_i", [P, NE], I32)
        small = sb("small", [NE, 4])
        eaw_sb, eaw_e, eawT = sb("eaw_sb", [NE, NA]), sb("eaw_e", [NE, NA]), sb("eawT", [NA, NE])
        atoms_sb, imp_sb = sb("atoms_sb", [NA, NS]), sb("imp_sb", [NE, NS])
        w_sb, wT = sb("w_sb", [P, TT, DM]), sb("wT", [P, C, DM])
        fill_sb = sb("fill_sb", [P, 2, DM * NE])

        s_const_step, s_const = sem("consts_step"), sem("consts_ready")
        s_idx_in, s_eaw_in, s_gate_in = sem("idx_loaded"), sem("mixture_loaded"), sem("gate_loaded")
        s_imp_in, s_w_in, s_atoms_in = sem("importance_loaded"), sem("w_ffn_loaded"), sem("atoms_loaded")
        s_fill, s_fill_out = sem("fill_ready"), [sem("fill_even_stored"), sem("fill_odd_stored")]
        s_chain, s_same_lower = sem("dve_chain"), sem("equal_lower_ready")
        s_max, s_exp, s_mix, s_mixT_pe, s_mixT = (sem("mixture_max"), sem("mixture_exp"), sem("mixture_ready"),
                                                  sem("mixture_turned"), sem("mixtureT_ready"))
        s_wT_pe, s_wT = sem("w_ffn_turned"), sem("w_ffnT_ready")
        s_impT, s_imp_e, s_mixed, s_entry = (sem("importance_turned"), sem("importance_exp"), sem("atoms_mixed"),
                                             sem("entries_ready"))
        s_gap, s_idx_row, s_same, s_sum = (sem("indices_ready"), sem("index_rows_ready"), sem("equal_indices_ready"),
                                           sem("entry_sums_ready"))
        block = ctx.enter_context(nc.Block())

        @block.sync
        def _(sp):
            sp.dma_start(w_sb[:], w_ffn.rearrange("(t p) d -> p t d", p=P)).then_inc(s_w_in, 16)
            sp.dma_start(atoms_sb[:], atoms).then_inc(s_atoms_in, 16)
            sp.dma_start(imp_sb[:], importance).then_inc(s_imp_in, 16)
            sp.dma_start(F.x_in[:], x_rows[0]).then_inc(F.s_x_in, 16)
            for j in range(1 + G):
                load_slot(sp, F, wq_v, wk_v, j, 0)
            sp.dma_start(F.wo_raw[:, 0:C, :], wv_v).then_inc(F.s_wv_in, 16)
            for c in range(C):
                sp.wait_ge(s_fill, c + 1)
                sp.dma_start(d_dram[c * P * DM:(c + 1) * P * DM, :].rearrange("(p r) e -> p (r e)", p=P),
                             fill_sb[:, c % 2]).then_inc(s_fill_out[c % 2], 16)
            sp.wait_ge(s_fill_out[0], 32)
            sp.wait_ge(s_fill_out[1], 32)

        @block.gpsimd
        def _(pool):
            pool.dma_start(idx_i[:], mask_idx.rearrange("(p j) -> p j", p=P)).then_inc(s_idx_in, 16)
            pool.dma_start(eaw_sb[:], eaw).then_inc(s_eaw_in, 16)
            pool.dma_start(R.gate[:].rearrange("p e d -> p (e d)"),
                           gate_w.rearrange("e d -> (e d)").unsqueeze(0).broadcast_to([P, NE * DM])).then_inc(s_gate_in, 16)
            pool.memset(ident[:], 0.0).then_inc(s_const_step, 1)
            pool.memset(ones[:], 1.0)
            pool.memset(upper[:], 1.0)
            pool.memset(R.minus_half[:], -0.5)
            pool.memset(R.counts[:], 0.0)
            pool.memset(zeros_i[:], 0)
            pool.memset(causal_bf[:], 0.0).then_inc(s_const_step, 1)
            pool.memset(lower[:], 1.0).then_inc(s_const_step, 1)
            pool.wait_ge(s_const_step, 3)
            pool.affine_select(out=ident[:], in_=ident[:], compare_op=ALU.not_equal, fill=1.0, base=0,
                               pattern=[[-1, P]], channel_multiplier=1).then_inc(s_const, 1)
            pool.affine_select(out=causal_bf[:], in_=causal_bf[:], compare_op=ALU.is_ge, fill=MASKED, base=0,
                               pattern=[[-1, P]], channel_multiplier=1).then_inc(s_const, 1)
            pool.affine_select(out=lower[:], in_=lower[:], compare_op=ALU.is_gt, fill=0.0, base=0,
                               pattern=[[-1, P]], channel_multiplier=1).then_inc(s_const, 1)
            pool.affine_select(out=upper[:], in_=upper[:], compare_op=ALU.is_gt, fill=0.0, base=0,
                               pattern=[[1, P]], channel_multiplier=-1)
            pool.iota(R.tokens[:], pattern=[[P, NT]], base=0, channel_multiplier=1)
            pool.iota(number_i[:], pattern=[[1, NE]], base=0, channel_multiplier=0)
            pool.iota(spare_i[:], pattern=[[0, 1]], base=DM * DM, channel_multiplier=1).then_inc(s_const, 1)
            pool.wait_ge(s_const, 4)
            pool.tensor_copy(ident_bf[:], ident[:]).then_inc(s_const, 1)
            pool.tensor_copy(R.number[:], number_i[:])
            halves = R.table.rearrange("(h p n) a -> h p (n a)", h=2, p=P // 2)
            for half in range(2):
                pool.dma_start(halves[half], zeros_i[0:P // 2]).then_inc(R.s_placed, 16)
            for c in range(C):
                pool.wait_ge(s_wT, c + 1)
                if c >= 2:
                    pool.wait_ge(s_fill_out[c % 2], 16)
                pool_round(pool, fill_sb[:, c % 2].rearrange("p (r e) -> p r e", e=NE),
                                 wT[:, c, :].unsqueeze(2).broadcast_to([P, DM, NE])).then_inc(s_fill, 1)
                for j in {1: (0, 1, 2), 2: (3, 4)}.get(c, ()):
                    pool.wait_ge(F.s_w_in[j], 16)
                    split_slot(pool, F, j, j, R.passed)
            pool.wait_ge(s_gate_in, 16)
            pool.wait_ge(R.s_placed, 32)

        @block.tensor
        def _(pe):
            pe.wait_ge(s_const, 5)
            pe.wait_ge(s_w_in, 16)
            for c in range(C):
                for t in range(TT):
                    last = pe.transpose(psum[:, c, t * P:(t + 1) * P], w_sb[:, t, c * P:(c + 1) * P], ident[:])
                last.then_inc(s_wT_pe, 1)
            pe.wait_ge(s_mix, 1)
            pe.transpose(psum[0:NA, 5, 64:64 + NE], eaw_e[:], ident[0:NE, 0:NE]).then_inc(s_mixT_pe, 1)
            pe.wait_ge(s_imp_in, 16)
            for j in range(NJ):
                last = pe.transpose(psum[:, 4, j * NE:(j + 1) * NE], imp_sb[:, j:NS:NJ], ident[0:NE, 0:NE])
            last.then_inc(s_impT, 1)
            pe.wait_ge(F.s_x_in, 16)
            pe.wait_ge(s_mixT, 1)
            turn_xT(pe, F, psum, ident, 0, range(C))
            pe.wait_ge(s_atoms_in, 16)
            pe.wait_ge(s_mixT, 1)
            for j in range(NJ):
                last = pe.matmul(psum[:, 6, j * NE:(j + 1) * NE], atoms_sb[:, j:NS:NJ], eawT[:], start=True, stop=True)
            last.then_inc(s_mixed, 1)
            pe.wait_ge(s_gap, 1)
            pe.wait_ge(s_entry, 1)
            pe.wait_ge(s_wT, C)
            pe.wait_ge(F.s_xt_lo, C)

            def sums(q):
                pe.wait_ge(s_same, q + 1)
                for j in range(QUAD * q, QUAD * (q + 1)):
                    last = pe.matmul(psum[:, 0, j * NE:(j + 1) * NE], same[:, q % 2, j % QUAD], entry[:, j, :],
                                     start=True, stop=True)
                last.then_inc(s_sum, 1)

            for q in range(NJ // QUAD):
                if q >= 2:
                    pe.wait_ge(s_same, q - 1)
                for j in range(QUAD):
                    last = pe.transpose(psum[:, (5, 7)[q % 2], j * P:(j + 1) * P],
                                        idx_f[:, QUAD * q + j:QUAD * q + j + 1].broadcast_to([P, P]), ident[:])
                last.then_inc(s_idx_row, 1)
                if q:
                    sums(q - 1)
            sums(NJ // QUAD - 1)

        @block.scalar
        def _(act):
            act.wait_ge(s_max, 1)
            act.activation(eaw_e[:], eaw_sb[:], ACT.Exp, bias=small[:, 0:1], accum_out=small[:, 1:2]).then_inc(s_exp, 1)
            act.wait_ge(s_impT, 1)
            act.activation(entry[:].rearrange("p j e -> p (j e)"), psum[:, 4, 0:NJ * NE], ACT.Exp,
                           scale=-1.0).then_inc(s_imp_e, 1)
            high_xT(act, F, psum, 0, range(C))
            act.wait_ge(F.s_wv_in, 16)
            act.copy(F.wv_hi[:], F.wo_raw[:, 0:C, :]).then_inc(F.s_wv_hi, 1)

        @block.vector
        def _(dve):
            chain = 0

            def after(ins):
                nonlocal chain
                chain += 1
                ins.then_inc(s_chain, 1)
                dve.wait_ge(s_chain, chain)

            dve.memset(R.rows[:], 0.0).then_inc(R.s_x1_out, 16)
            dve.memset(R.place_tile[:], 0)
            dve.memset(R.ranks[:], 0.0).then_inc(R.s_ranks_read, 1)
            dve.wait_ge(s_eaw_in, 16)
            dve.tensor_reduce(small[:, 0:1], eaw_sb[:], AX.X, ALU.max, negate=True).then_inc(s_max, 1)
            dve.wait_ge(s_idx_in, 16)
            dve.tensor_copy(idx_f[:], idx_i[:])
            dve.tensor_scalar(idx_r_i[:], idx_i[:], SHIFT, None, ALU.logical_shift_right)
            after(dve.tensor_scalar(idx_c_i[:], idx_i[:], DM - 1, SHIFT, ALU.bitwise_and, ALU.logical_shift_left))
            dve.wait_ge(s_exp, 1)
            after(dve.reciprocal(small[:, 2:3], small[:, 1:2]))
            dve.tensor_scalar(eaw_e[:], eaw_e[:], small[:, 2:3], None, ALU.mult).then_inc(s_mix, 1)
            after(dve.tensor_tensor(row_f[:], idx_r_i[:], idx_c_i[:], ALU.add))
            for c in range(C):
                dve.wait_ge(s_wT_pe, c + 1)
                dve.tensor_copy(wT[:, c], psum[:, c, :]).then_inc(s_wT, 1)
            dve.wait_ge(s_mixT_pe, 1)
            dve.tensor_copy(eawT[:], psum[0:NA, 5, 64:64 + NE]).then_inc(s_mixT, 1)
            dve.wait_ge(s_const, 4)
            after(dve.tensor_copy(spare_f[:], spare_i[:]))
            dve.tensor_scalar(gap_f[:], row_f[:], -1.0, spare_f[:, 0:1], ALU.mult, ALU.add).then_inc(s_gap, 1)
            flat = entry[:].rearrange("p j e -> p (j e)")
            dve.wait_ge(s_imp_e, 1)
            after(dve.tensor_scalar(flat, flat, 1.0, None, ALU.add))
            after(dve.reciprocal(flat, flat))
            low_xT(dve, F, psum, 0, range(C))
            dve.wait_ge(s_mixed, 1)
            dve.tensor_tensor(flat, psum[:, 6, 0:NJ * NE], flat, ALU.mult).then_inc(s_entry, 1)
            def count(q):
                dve.wait_ge(s_same_lower, q + 1)
                return dve.tensor_reduce(dup[:, QUAD * q:QUAD * (q + 1)], same_lower[:, q % 2], AX.X, ALU.add)

            for q in range(NJ // QUAD):
                dve.wait_ge(s_idx_row, q + 1)
                if q >= 2:
                    dve.wait_ge(s_sum, q - 1)
                dve.tensor_tensor(same[:, q % 2], psum[:, (5, 7)[q % 2], :].rearrange("p (j n) -> p j n", n=P),
                                  idx_f[:, QUAD * q:QUAD * (q + 1)].unsqueeze(2).broadcast_to([P, QUAD, P]),
                                  ALU.is_equal).then_inc(s_same, 1)
                if q:
                    count(q - 1)
                dve.wait_ge(s_same, q + 1)
                dve.tensor_tensor(same_lower[:, q % 2], same[:, q % 2], lower[:].unsqueeze(1).broadcast_to([P, QUAD, P]),
                                  ALU.mult).then_inc(s_same_lower, 1)
            after(count(NJ // QUAD - 1))
            dve.wait_ge(F.s_wv_hi, 1)
            dve.tensor_tensor(F.wv_lo[:], F.wo_raw[:, 0:C, :], F.wv_hi[:].bitcast(F32), ALU.subtract).then_inc(F.s_wv, 2)
            dve.wait_ge(s_gap, 1)
            after(dve.tensor_scalar(dup[:], dup[:], 1.0, None, ALU.min))
            after(dve.tensor_tensor(dup[:], dup[:], gap_f[:], ALU.mult))
            after(dve.tensor_tensor(dup[:], dup[:], row_f[:], ALU.add))
            after(dve.tensor_copy(row_i[:], dup[:]))
            dve.wait_ge(s_sum, NJ // QUAD)
            after(dve.tensor_copy(entry_sum[:].rearrange("p j e -> p (j e)"), psum[:, 0, 0:NJ * NE]))


def wait_apart(eng, semaphore, count, passed):
    eng.wait_ge(semaphore, count)
    eng.sem_inc(passed, 1)


def pool_round(pool, out, in_):
    return pool.tensor_scalar(out, in_, 1.0, 1.0, ALU.mult, ALU.mult)


def run(eng, iteration):
    def batch(b, last_kind, route):
        with eng.Fori(0, HKV - 1) as g:
            iteration(b, g, b * HKV + g, "group", route)
        iteration(b, HKV - 1, b * HKV + HKV - 1, last_kind, route)

    batch(0, "batch", False)
    with eng.Fori(1, NB - 1) as b:
        batch(b, "batch", True)
    batch(NB - 1, "end", True)


def next_batch(b):
    return (b + 2) % NB


def attention(nc, sem, s_passed, psum, ident, ident_bf, causal_bf, upper, ones, R, F, row_i, entry_sum, y_acc, x_rows, r_store,
              d_dram, wq_v, wk_v, wo_v):
    with ExitStack() as ctx:
        def sb(name, shape, dt=F32):
            return ctx.enter_context(nc.sbuf_tensor(name, shape, dt))

        x_in, xT_hi, xT_lo = F.x_in, F.xT_hi, F.xT_lo
        w_hi, w_lo, wo_raw, wv_hi, wv_lo = F.w_hi, F.w_lo, F.wo_raw, F.wv_hi, F.wv_lo
        s_x_in, s_w_in, s_w_split, s_wv, s_pool_step = F.s_x_in, F.s_w_in, F.s_w_split, F.s_wv, F.s_pool_step
        s_xt, s_xt_lo = F.s_xt, F.s_xt_lo
        wo_hi, wo_lo = sb("wo_hi", [P, G, DM], F32R), sb("wo_lo", [P, G, DM], F32R)
        v_raw = sb("v_raw", [P, TT, HKV * HD])
        v_hi, v_lo = sb("v_hi", [P, TT, HD], F32R), sb("v_lo", [P, TT, HD], F32R)
        kT_hi, kT_lo = sb("kT_hi", [P, T], F32R), sb("kT_lo", [P, T], F32R)
        qT_hi, qT_lo = sb("qT_hi", [P, 2, T], F32R), sb("qT_lo", [P, 2, T], F32R)
        probs = sb("probs", [P, 2, PACK])
        pT_hi, pT_lo = sb("pT_hi", [P, PACK], F32R), sb("pT_lo", [P, PACK], F32R)
        oT_hi, oT_lo = sb("oT_hi", [P, G, T], F32R), sb("oT_lo", [P, G, T], F32R)
        neg_max = sb("neg_max", [P, 2, TT])
        row_sum = sb("row_sum", [P, 2, TT])
        row_inv = sb("row_inv", [P, 2, TT])
        row_now = sb("row_now", [P, 1], I32)
        entry_now = sb("entry_now", [P, NE])

        s_wo_in = [sem(f"wo_head_{h}_loaded") for h in range(G)]
        s_scatter = sem("entries_scattered")
        s_r_out = sem("residual_stored")
        s_vg = sem("v_group_split")
        s_wo = sem("wo_heads_split")
        s_seed = sem("y_seeded")
        s_norm = sem("probs_normalized")
        s_qk = sem("score_banks_ready")
        s_max = sem("score_maxima_ready")
        s_exp = sem("score_banks_exped")
        s_inv = sem("row_inv_ready")
        s_pt, s_pt_hi, s_pt_lo = sem("pT_units_ready"), sem("pT_hi_ready"), sem("pT_lo_ready")
        s_q, s_q_hi, s_q_lo = sem("qT_ready"), sem("qT_hi_ready"), sem("qT_lo_ready")
        s_k, s_k_hi, s_k_lo = sem("kT_ready"), sem("kT_hi_ready"), sem("kT_lo_ready")
        s_o, s_o_hi, s_o_lo = sem("oT_ready"), sem("oT_hi_ready"), sem("oT_lo_ready")
        s_v, s_v_raw = sem("v_ready"), sem("v_raw_ready")
        s_y, s_y_acc = sem("y_tiles_ready"), sem("y_tiles_added")
        s_entry = sem("entry_copied")
        block = ctx.enter_context(nc.Block())

        @block.sync
        def _(sp):
            def load_wo(h, g):
                src = wo_v[:, bass.ds(g * G + h, 1), :].rearrange("p a n -> p (a n)")
                sp.dma_start(wo_raw[:, h], src).then_inc(s_wo_in[h], 16)

            for j in range(1 + G):
                sp.wait_ge(s_w_split, j + 1)
                load_slot(sp, F, wq_v, wk_v, j, 1)
            sp.wait_ge(s_wv, 1)
            for h in range(G):
                load_wo(h, 0)
            sp.wait_ge(s_seed, 1)
            sp.wait_ge(s_xt, C)
            sp.dma_start(x_in[:], x_rows[1]).then_inc(s_x_in, 16)

            def iteration(b, g, it, kind, route):
                if route:
                    wait_apart(sp, s_r_out, 16 * b, s_passed)
                    route_load(sp, R, it - TT, R.r_dram[bass.ds(it - TT, 1)].rearrange("a p d -> (a p) d"))
                if kind != "end":
                    for j in range(1 + G):
                        sp.wait_ge(s_w_split, (it + 1) * (1 + G) + j + 1)
                        load_slot(sp, F, wq_v, wk_v, j, (g + 2) % HKV)
                        if 1 <= j < G:
                            sp.wait_ge(s_wo, it * G + j)
                            load_wo(j - 1, (g + 1) % HKV)
                        if route and j == G - 1:
                            route_store(sp, R, it - TT, R.x1_dram[bass.ds((it - TT) * P, P), :])
                    sp.wait_ge(s_wo, it * G + G)
                    load_wo(G - 1, (g + 1) % HKV)
                elif route:
                    route_store(sp, R, it - TT, R.x1_dram[bass.ds((it - TT) * P, P), :])
                if kind == "batch":
                    wait_apart(sp, s_y_acc, TT + (it + 1) * TT, s_passed)
                    sp.dma_start(r_store[bass.ds(b, 1)].rearrange("a p t d -> (a p) t d"), y_acc[:]).then_inc(s_r_out, 16)
                    wait_apart(sp, s_seed, b + 2, s_passed)
                    wait_apart(sp, s_xt, (b + 2) * C, s_passed)
                    sp.dma_start(x_in[:], x_rows[bass.ds(next_batch(b), 1)].rearrange("a p t d -> (a p) t d")).then_inc(s_x_in, 16)

            run(sp, iteration)
            sp.wait_ge(s_r_out, 16 * (NB - 1))
            sp.wait_ge(s_x_in, 16 * (NB + 1))
            for j in range(1 + G):
                sp.wait_ge(s_w_in[j], 16 * (NIT + 1))
            sp.wait_ge(R.s_x1_out, 16 * (NT - TT + 1))

        @block.gpsimd
        def _(pool):
            def split_v(g, k):
                src = v_raw[:, :, bass.ds(g * HD, HD)]
                pool.tensor_copy(v_hi[:], src).then_inc(s_pool_step, 1)
                wait_apart(pool, s_pool_step, k + 1, s_passed)
                pool.tensor_tensor(v_lo[:], src, v_hi[:].bitcast(F32), ALU.subtract).then_inc(s_vg, 1)

            def split_wo(h, it, k):
                wait_apart(pool, s_wo_in[h], 16 * (it + 1), s_passed)
                pool_round(pool, wo_hi[:, h], wo_raw[:, h]).then_inc(s_pool_step, 1)
                wait_apart(pool, s_pool_step, k + 1, s_passed)
                pool.tensor_tensor(wo_lo[:, h], wo_raw[:, h], wo_hi[:, h].bitcast(F32), ALU.subtract).then_inc(s_wo, 1)

            def normalize(n, buf):
                wait_apart(pool, s_inv, n + 1, s_passed)
                for i in range(TT):
                    a = ROW_AT[i]
                    p = probs[:, buf, a:a + (i + 1) * P]
                    last = pool.tensor_scalar(p, p, row_inv[:, buf, i:i + 1], 1.0, ALU.mult, ALU.mult)
                last.then_inc(s_norm, 1)

            def slot(it_next, j, k):
                wait_apart(pool, s_w_in[j], 16 * (it_next + 1), s_passed)
                if j == 0:
                    wait_apart(pool, s_k, it_next, s_passed)
                else:
                    wait_apart(pool, s_q, (it_next - 1) * G + j, s_passed)
                split_slot(pool, F, j, k, s_passed)

            pool.wait_ge(s_x_in, 16)
            pool_round(pool, y_acc[:], x_in[:]).then_inc(s_seed, 1)
            pool.wait_ge(s_v_raw, TT)
            split_v(0, 1 + G)
            normalize(0, 0)
            SETUP_STEPS = 1 + G + 1
            STEPS = 1 + G + 1 + G

            def iteration(b, g, it, kind, route):
                k0 = SETUP_STEPS + it * STEPS
                n0 = it * G
                k = 0
                has_next = kind != "end"
                if has_next:
                    slot(it + 1, 0, k0)
                    k = 1
                normalize(n0 + 1, 1)
                if route:
                    route_rstd(pool, R, it - TT)
                split_wo(0, it, k0 + k)
                k += 1
                if has_next:
                    slot(it + 1, 1, k0 + k)
                    k += 1
                normalize(n0 + 2, 0)
                split_wo(1, it, k0 + k)
                k += 1
                if has_next:
                    slot(it + 1, 2, k0 + k)
                    k += 1
                normalize(n0 + 3, 1)
                split_wo(2, it, k0 + k)
                split_wo(3, it, k0 + k + 1)
                k += 2
                wait_apart(pool, s_scatter, 16 * (it + 1), s_passed)
                pool.tensor_copy(row_now[:], row_i[:, bass.ds(it, 1)]).then_inc(s_entry, 1)
                pool.tensor_copy(entry_now[:], entry_sum[:, bass.ds(it, 1), :].rearrange("p a e -> p (a e)")).then_inc(s_entry, 1)
                wait_apart(pool, s_entry, 2 * it + 2, s_passed)
                pool.indirect_dma_start(out=d_dram, out_offset=bass.IndirectOffsetOnAxis(ap=row_now[:, 0:1], axis=0),
                                        in_=entry_now[:], in_offset=None, compute_op=ALU.add).then_inc(s_scatter, 16)
                if has_next:
                    slot(it + 1, 3, k0 + k)
                    k += 1
                    normalize(n0 + 4, 0)
                if kind == "group":
                    wait_apart(pool, s_o, n0 + G, s_passed)
                    split_v(g + 1, k0 + k)
                    k += 1
                if has_next:
                    slot(it + 1, 4, k0 + k)
                    k += 1
                if route:
                    route_place(pool, R, it - TT)
                if kind == "batch":
                    wait_apart(pool, s_x_in, 16 * (b + 2), s_passed)
                    wait_apart(pool, s_r_out, 16 * (b + 1), s_passed)
                    pool_round(pool, y_acc[:], x_in[:]).then_inc(s_seed, 1)
                    wait_apart(pool, s_v_raw, (b + 2) * TT, s_passed)
                    split_v(0, k0 + k)

            pool.dma_start(d_dram[DM * DM:DM * DM + P, :], entry_sum[:, 0, :]).then_inc(s_scatter, 16)
            run(pool, iteration)
            pool.wait_ge(s_scatter, 16 * (NIT + 1))
            pool.wait_ge(R.s_placed, 32 * (NT - TT + 1))

        @block.tensor
        def _(pe):
            def three(dst, hi_s, lo_s, hi_m, lo_m, start, stop):
                pe.matmul(dst, hi_s, hi_m, start=start, stop=False)
                pe.matmul(dst, hi_s, lo_m, start=False, stop=False)
                return pe.matmul(dst, lo_s, hi_m, start=False, stop=stop)

            def scores(n, buf, first=False):
                pe.wait_ge(s_q_lo, n + 1)
                for i, bank, col in ROWS:
                    w = (i + 1) * P
                    dst = psum[:, BANK_S + bank, col:col + w]
                    if not first and col == 0:
                        pe.wait_ge(s_exp, 3 * n - 3 + bank + 1)
                    q = (qT_hi[:, buf, i * P:(i + 1) * P], qT_lo[:, buf, i * P:(i + 1) * P])
                    three(dst, *q, kT_hi[:, 0:w], kT_lo[:, 0:w], True, False)
                    last = pe.matmul(dst[:, i * P:w], ident_bf[:], causal_bf[:], start=False, stop=True)
                    if i != 2:
                        last.then_inc(s_qk, 1)

            def transposes(n, buf, units):
                if 0 in units:
                    pe.wait_ge(s_norm, n + 1)
                    pe.wait_ge(s_pt_lo, 3 * n + 3)
                for j, unit, col in KEYS:
                    if unit not in units:
                        continue
                    for i in range(j, TT):
                        at = col + (i - j) * P
                        src = ROW_AT[i] + j * P
                        last = pe.transpose(psum[:, BANKS_PT[unit], at:at + P], probs[:, buf, src:src + P], ident[:])
                    if j != 1:
                        last.then_inc(s_pt, 1)

            def values(n, first_of_group, it):
                if first_of_group:
                    pe.wait_ge(s_vg, it + 1)
                    pe.wait_ge(s_y_acc, it * TT + TT)
                else:
                    pe.wait_ge(s_o_lo, n)
                for j, unit, _ in KEYS:
                    if j != 3:
                        pe.wait_ge(s_pt_lo, 3 * n + 3 + unit + 1)
                    a, w = KEY_AT[j], T - j * P
                    last = three(psum[:, BANK_B, j * P:T], v_hi[:, j], v_lo[:, j], pT_hi[:, a:a + w], pT_lo[:, a:a + w],
                                 j == 0, j == KEYS[-1][0])
                last.then_inc(s_o, 1)

            def project(slot, done):
                for c in range(C):
                    last = three(psum[:, BANK_A, :], w_hi[:, slot, c], w_lo[:, slot, c], xT_hi[:, c], xT_lo[:, c],
                                 c == 0, c == C - 1)
                last.then_inc(done, 1)

            def query(n, h, it):
                pe.wait_ge(s_w_split, it * (1 + G) + h + 2)
                if h == 0:
                    pe.wait_ge(s_k_lo, it + 1)
                else:
                    pe.wait_ge(s_q_lo, n)
                project(1 + h, s_q)

            def key(it):
                pe.wait_ge(s_w_split, it * (1 + G) + 1)
                project(0, s_k)

            def turn_x(b, chunks):
                if 0 in chunks:
                    pe.wait_ge(s_x_in, 16 * (b + 1))
                    pe.wait_ge(s_q_lo, b * HKV * G)
                turn_xT(pe, F, psum, ident, b, chunks)

            def value_rows(b, first):
                for t in range(TT):
                    if t >= 2:
                        pe.wait_ge(s_v_raw, b * TT + t - 1)
                    elif not first:
                        pe.wait_ge(s_y_acc, TT + b * HKV * TT - 1 + t)
                    for c in range(C):
                        last = three(psum[:, (BANK_C, BANK_B)[t % 2], :], xT_hi[:, c, t * P:(t + 1) * P],
                                     xT_lo[:, c, t * P:(t + 1) * P], wv_hi[:, c], wv_lo[:, c], c == 0, c == C - 1)
                    last.then_inc(s_v, 1)

            def out_rows(t, it):
                if t == 0:
                    pe.wait_ge(s_o_lo, (it + 1) * G)
                    pe.wait_ge(s_wo, (it + 1) * G)
                if t != 1:
                    pe.wait_ge(s_y_acc, TT + it * TT + t - 1)
                for h in range(G):
                    last = three(psum[:, (BANK_C, BANK_B)[t % 2], :], oT_hi[:, h, t * P:(t + 1) * P],
                                 oT_lo[:, h, t * P:(t + 1) * P], wo_hi[:, h], wo_lo[:, h], h == 0, h == G - 1)
                last.then_inc(s_y, 1)

            pe.wait_ge(s_xt_lo, C)
            key(0)
            query(0, 0, 0)
            scores(0, 0, True)
            query(1, 1, 0)
            pe.wait_ge(s_wv, 2)
            value_rows(0, True)

            def iteration(b, g, it, kind, route):
                n = it * G
                scores(n + 1, 1)
                transposes(n, 0, (0, 1))
                pe.wait_ge(s_y_acc, it * TT + TT - 1)
                pe.wait_ge(s_v_raw, b * TT + TT - 1)
                transposes(n, 0, (2,))
                if route:
                    pe.wait_ge(R.s_ranks_read, it - TT + 1)
                query(n + 2, 2, it)
                values(n, True, it)
                scores(n + 2, 0)
                transposes(n + 1, 1, (0, 1, 2))
                query(n + 3, 3, it)
                values(n + 1, False, it)
                scores(n + 3, 1)
                if kind == "batch":
                    turn_x(b + 1, (0, 1))
                    transposes(n + 2, 0, (0, 1))
                    turn_x(b + 1, (2, 3))
                    pe.wait_ge(s_xt_lo, (b + 2) * C)
                    transposes(n + 2, 0, (2,))
                    key(it + 1)
                    values(n + 2, False, it)
                else:
                    transposes(n + 2, 0, (0, 1, 2))
                    if kind == "group":
                        pe.wait_ge(s_q_lo, n + 4)
                        key(it + 1)
                    values(n + 2, False, it)
                transposes(n + 3, 1, (0, 1, 2))
                if kind != "end":
                    query(n + 4, 0, it + 1)
                values(n + 3, False, it)
                if kind != "end":
                    scores(n + 4, 0)
                out_rows(0, it)
                out_rows(1, it)
                if kind != "end":
                    query(n + 5, 1, it + 1)
                out_rows(2, it)
                if route:
                    pe.wait_ge(s_q_lo, n + (6 if kind != "end" else 4))
                    route_ranks(pe, R, it - TT, upper, ones, BANK_A)
                out_rows(3, it)
                if kind == "batch":
                    value_rows(b + 1, False)

            run(pe, iteration)

        @block.scalar
        def _(act):
            def exps(n, buf, banks=(0, 1, 2)):
                for i, bank, col in ROWS:
                    if bank not in banks:
                        continue
                    if i != 0:
                        act.wait_ge(s_max, 3 * n + bank + 1)
                    w, a = (i + 1) * P, ROW_AT[i]
                    last = act.activation(probs[:, buf, a:a + w], psum[:, BANK_S + bank, col:col + w], ACT.Exp,
                                          bias=neg_max[:, buf, i:i + 1],
                                          accum_out=row_sum[:, buf, i:i + 1])
                    if i != 2:
                        last.then_inc(s_exp, 1)

            def pT(n, units):
                for u in units:
                    a, z = UNIT[u]
                    act.wait_ge(s_pt, 3 * n + u + 1)
                    act.copy(pT_hi[:, a:z], psum[:, BANKS_PT[u], 0:z - a]).then_inc(s_pt_hi, 1)

            def exps_between(n, buf):
                exps(n + 1, buf, (0, 1))
                pT(n, (0,))
                exps(n + 1, buf, (2,))
                pT(n, (1, 2))

            def qT(n, buf):
                act.wait_ge(s_q, n + 1)
                act.mul(qT_hi[:, buf], psum[:, BANK_A, :], SCALE).then_inc(s_q_hi, 1)

            def kT(it):
                act.wait_ge(s_k, it + 1)
                act.copy(kT_hi[:], psum[:, BANK_A, :]).then_inc(s_k_hi, 1)

            def oT(n, h):
                act.wait_ge(s_o, n + 1)
                act.copy(oT_hi[:, h], psum[:, BANK_B, :]).then_inc(s_o_hi, 1)

            def v(b):
                for t in range(TT):
                    act.wait_ge(s_v, b * TT + t + 1)
                    act.copy(v_raw[:, t], psum[:, (BANK_C, BANK_B)[t % 2], :]).then_inc(s_v_raw, 1)

            kT(0)
            qT(0, 0)
            exps(0, 0)
            qT(1, 1)
            v(0)

            def iteration(b, g, it, kind, route):
                n = it * G
                exps_between(n, 1)
                qT(n + 2, 0)
                oT(n, 0)
                exps_between(n + 1, 0)
                qT(n + 3, 1)
                oT(n + 1, 1)
                if kind == "batch":
                    exps(n + 3, 1)
                    high_xT(act, F, psum, b + 1, (0, 1))
                    pT(n + 2, (0, 1))
                    high_xT(act, F, psum, b + 1, (2, 3))
                    pT(n + 2, (2,))
                else:
                    exps_between(n + 2, 1)
                if kind != "end":
                    kT(it + 1)
                oT(n + 2, 2)
                pT(n + 3, (0, 1, 2))
                if kind != "end":
                    qT(n + 4, 0)
                oT(n + 3, 3)
                if kind != "end":
                    exps(n + 4, 0)
                if route:
                    route_exp(act, R, it - TT)
                if kind != "end":
                    qT(n + 5, 1)
                if kind == "batch":
                    v(b + 1)

            run(act, iteration)

        @block.vector
        def _(dve):
            def maxima(n, buf):
                for i, bank, col in ROWS:
                    if i != 0:
                        dve.wait_ge(s_qk, 3 * n + bank + 1)
                    last = dve.tensor_reduce(neg_max[:, buf, i:i + 1], psum[:, BANK_S + bank, col:col + (i + 1) * P],
                                             AX.X, ALU.max, negate=True)
                    if i != 2:
                        last.then_inc(s_max, 1)

            def inverse(n, buf):
                dve.wait_ge(s_exp, 3 * n + 3)
                dve.reciprocal(row_inv[:, buf], row_sum[:, buf]).then_inc(s_inv, 1)

            def softmax(n, buf):
                maxima(n, buf)
                inverse(n, buf)

            def low(lo, hi, src, done):
                dve.tensor_tensor(lo, src, hi.bitcast(F32), ALU.subtract).then_inc(done, 1)

            def pT(n, units):
                for u in units:
                    a, z = UNIT[u]
                    dve.wait_ge(s_pt_hi, 3 * n + u + 1)
                    low(pT_lo[:, a:z], pT_hi[:, a:z], psum[:, BANKS_PT[u], 0:z - a], s_pt_lo)

            def softmax_between(n, buf):
                maxima(n + 1, buf)
                pT(n, (0,))
                inverse(n + 1, buf)
                pT(n, (1, 2))

            def qT(n, buf):
                dve.wait_ge(s_q_hi, n + 1)
                dve.scalar_tensor_tensor(out=qT_lo[:, buf], in0=psum[:, BANK_A, :], scalar=SCALE,
                                         in1=qT_hi[:, buf].bitcast(F32), op0=ALU.mult, op1=ALU.subtract).then_inc(s_q_lo, 1)

            def kT(it):
                dve.wait_ge(s_k_hi, it + 1)
                low(kT_lo[:], kT_hi[:], psum[:, BANK_A, :], s_k_lo)

            def oT(n, h):
                dve.wait_ge(s_o_hi, n + 1)
                low(oT_lo[:, h], oT_hi[:, h], psum[:, BANK_B, :], s_o_lo)

            def add_rows(it, t):
                dve.wait_ge(s_y, it * TT + t + 1)
                dve.tensor_tensor(y_acc[:, t], psum[:, (BANK_C, BANK_B)[t % 2], :], y_acc[:, t], ALU.add).then_inc(s_y_acc, 1)

            dve.memset(neg_max[:], 0.0).then_inc(s_pt_lo, 3)
            dve.memset(row_inv[:], 0.0).then_inc(s_y_acc, TT)
            kT(0)
            qT(0, 0)
            softmax(0, 0)
            qT(1, 1)

            def iteration(b, g, it, kind, route):
                n = it * G
                tt = it - TT
                softmax_between(n, 1)
                qT(n + 2, 0)
                if route:
                    route_variance(dve, R, tt)
                oT(n, 0)
                softmax_between(n + 1, 0)
                qT(n + 3, 1)
                if route:
                    route_normalize(dve, R, tt)
                oT(n + 1, 1)
                if kind == "batch":
                    softmax(n + 3, 1)
                    low_xT(dve, F, psum, b + 1, (0, 1))
                    pT(n + 2, (0, 1))
                    low_xT(dve, F, psum, b + 1, (2, 3))
                    pT(n + 2, (2,))
                else:
                    softmax_between(n + 2, 1)
                if kind != "end":
                    kT(it + 1)
                oT(n + 2, 2)
                pT(n + 3, (0, 1, 2))
                if kind != "end":
                    qT(n + 4, 0)
                if route:
                    route_logits(dve, R, tt, (0, 1))
                oT(n + 3, 3)
                if kind != "end":
                    maxima(n + 4, 0)
                if route:
                    route_logits(dve, R, tt, (2, 3, 4))
                if kind != "end":
                    inverse(n + 4, 0)
                if route:
                    route_logits(dve, R, tt, (5, 6, 7))
                add_rows(it, 0)
                if route:
                    route_choose(dve, R, tt)
                add_rows(it, 1)
                if kind != "end":
                    qT(n + 5, 1)
                add_rows(it, 2)
                if route:
                    route_locate(dve, R, tt, BANK_A)
                add_rows(it, 3)

            run(dve, iteration)


def experts(nc, sem, s_passed, psum, ident, upper, ones, R, rows, gate_w, d_dram, y_dram):
    LAST = NT - TT
    with ExitStack() as ctx:
        def sb(name, shape, dt=F32):
            return ctx.enter_context(nc.sbuf_tensor(name, shape, dt))

        d_hi, d_lo = sb("d_hi", [P, C, NE, DM], F32R), sb("d_lo", [P, C, NE, DM], F32R)
        STAGES = 3
        stage = sb("stage", [P, STAGES, DM * NE // 2])
        token_rows, y_rows = stage[:, 0].rearrange("p (k d) -> p k d", d=DM), stage[:, 1].rearrange("p (k d) -> p k d", d=DM)
        xT_hi, xT_lo = sb("tokT_hi", [P, 2, C, P], F32R), sb("tokT_lo", [P, 2, C, P], F32R)
        token_ids, ids_now = sb("token_ids", [P, NE * ETILES], I32), sb("ids_now", [P, GROUP], I32)
        tile_at_i, tile_at = sb("tile_at_i", [P, JT], I32), sb("tile_at", [P, JT])
        counts_i, tiles_i, tiles = sb("counts_i", [P, NE], I32), sb("tiles_i", [P, NE], I32), sb("tiles", [P, NE])
        ends, starts = sb("ends", [P, NE]), sb("starts", [P, NE])
        tile_expert, tile_start, tile_step = sb("tile_expert", [P, JT]), sb("tile_start", [P, JT]), sb("tile_step", [P, JT])
        tile_expert_i, tile_number_i = sb("tile_expert_i", [P, JT], I32), sb("tile_number_i", [P, JT], I32)
        behind, behind_tiles = sb("behind", [P, NE, JT]), sb("behind_tiles", [P, NE, JT])
        row, row_step = sb("row", [P, 2 * NT]), sb("row_step", [P, 2 * NT])

        gate_rows, gateT = sb("gate_rows", [NE, DM]), sb("gateT", [P, C, NE])
        x1T, logitsT = sb("x1T", [P, C, TT * P]), sb("logitsT", [NE, TT * P])
        stats, mean_var, var_eps = sb("last_stats", [P, TT, 6]), sb("last_mean_var", [P, TT, 2]), sb("last_var_eps", [P, TT])
        rstd, halves = sb("last_rstd", [P, TT]), sb("minus_halves", [P, TT])
        clipped, best = sb("last_clipped", [P, TT, NE]), sb("last_best", [P, TT, 8])
        best_at, gap, share_sum = sb("last_best_at", [P, TT, 8], U32), sb("last_gap", [P, 2, TT]), sb("last_share_sum", [P, TT])
        expert, chosen = sb("last_expert", [P, TT, 2]), sb("last_chosen", [P, 3, TT, NE])
        before = sb("chosen_before", [P, TT + 1, NE])
        ranks, rank, product8 = sb("last_ranks", [P, TT, NE]), sb("last_rank", [P, TT, 2]), sb("last_product8", [P, TT, 2, NE])
        rank_i, tile_i, place_i = sb("last_rank_i", [P, TT, 2], I32), sb("last_tile_i", [P, TT, 2], I32), sb("last_place_i", [P, TT, 2], I32)
        tile_f, place_tile = sb("last_tile_f", [P, TT, 2]), sb("last_place_tile", [P, TT, 2], I32)
        s_d_in = [sem(f"d_stage_{k}_loaded") for k in range(STAGES)]
        s_d_hi, s_d_lo, s_d_lo_pool = sem("d_hi_ready"), sem("d_lo_ready"), sem("d_lo_pool_ready")
        s_ids_in, s_tile_at, s_counts, s_tiles = (sem("token_ids_loaded"), sem("tile_numbers_ready"),
                                                  sem("expert_counts_ready"), sem("expert_tiles_ready"))
        s_step, s_behind = sem("dve_step_experts"), sem("behind_ready")
        s_ids_now = sem("ids_copied")
        s_tok_in = [sem(f"token_rows_{k}_loaded") for k in range(GROUP)]
        s_turn, s_hi, s_lo = sem("tokens_turned"), sem("tokT_hi_ready"), sem("tokT_lo_ready")
        s_y, s_y_sb = sem("expert_rows_ready"), sem("expert_rows_copied")
        s_y_out = [sem(f"expert_rows_{k}_stored") for k in range(GROUP)]
        s_gate_in, s_var, s_rstd, s_x1, s_x1_out = (sem("gate_rows_loaded"), sem("last_variances_ready"),
                                                    sem("last_rstd_ready"), sem("last_x1_ready"), sem("last_x1_stored"))
        s_gate, s_gateT, s_x1T_pe, s_x1T = sem("gate_turned"), sem("gateT_ready"), sem("x1_turned"), sem("x1T_ready")
        s_logitT, s_logitT_sb, s_logit = sem("logitsT_ready"), sem("logitsT_copied"), sem("last_logits_ready")
        s_gap, s_gap_exp = sem("last_gaps_ready"), sem("last_gaps_exped")
        s_chosen, s_ranked, s_place, s_halves = (sem("last_chosen_ready"), sem("last_ranks_ready"),
                                                 sem("last_places_ready"), sem("minus_halves_ready"))
        block = ctx.enter_context(nc.Block())
        PARTS = 2 * C
        DVE_E = [NE // 2] * (PARTS // 2) + [NE] * (PARTS - PARTS // 2)

        def part(q, e):
            return stage[:, q % STAGES].rearrange("p (r e) -> p e r", e=NE)[:, e]

        def place(w, q, e):
            return w[:, q // 2, e, (q % 2) * (DM // 2):(q % 2 + 1) * (DM // 2)]

        @block.sync
        def _(sp):
            sp.dma_start(gate_rows[:], gate_w).then_inc(s_gate_in, 16)
            weights = d_dram[0:DM * DM, :].rearrange("(c p h r) e -> c h p (r e)", c=C, p=P, h=2)
            for q in range(PARTS):
                if q >= STAGES:
                    sp.wait_ge(s_d_lo, sum(DVE_E[:q - STAGES + 1]))
                    sp.wait_ge(s_d_lo_pool, NE * (q - STAGES + 1) - sum(DVE_E[:q - STAGES + 1]))
                sp.dma_start(stage[:, q % STAGES], weights[q // 2, q % 2]).then_inc(s_d_in[q % STAGES], 16)
                if q == 3:
                    sp.wait_ge(s_x1, TT)
                    sp.dma_start(R.x1_dram[LAST * P:, :].rearrange("(t p) d -> p t d", p=P), rows[:]).then_inc(s_x1_out, 16)
            sp.wait_ge(R.s_placed, 32 * (NT + 1))
            sp.dma_start(token_ids[:], R.table.rearrange("(p n) a -> p (n a)", p=P)).then_inc(s_ids_in, 16)
            with sp.Fori(0, TURNS) as i:
                for k in range(GROUP):
                    wait_apart(sp, s_y_sb, i * GROUP + k + 1, s_passed)
                    sp.dma_start(y_dram[bass.ds((i * GROUP + k) * P, P), :], y_rows[:, k]).then_inc(s_y_out[k], 16)
            for k in range(GROUP):
                sp.wait_ge(s_y_out[k], 16 * (TURNS + 1))

        @block.gpsimd
        def _(pool):
            pool.iota(tile_at_i[:], pattern=[[1, JT]], base=0, channel_multiplier=0).then_inc(s_tile_at, 1)
            pool.memset(halves[:], -0.5).then_inc(s_halves, 1)
            pool.wait_ge(s_halves, 1)
            pool.wait_ge(s_var, 1)
            pool.tensor_tensor(rstd[:], var_eps[:], halves[:], ALU.pow).then_inc(s_rstd, 1)
            for q in range(PARTS):
                for e in range(DVE_E[q], NE):
                    pool.wait_ge(s_d_hi, q * NE + e + 1)
                    pool.tensor_tensor(place(d_lo, q, e), part(q, e), place(d_hi, q, e).bitcast(F32),
                                       ALU.subtract).then_inc(s_d_lo_pool, 1)
                if q == PARTS // 2 - 1:
                    pool.wait_ge(s_place, 1)
                    for t in range(TT):
                        for k in range(2):
                            pool.indirect_dma_start(
                                out=R.table, out_offset=bass.IndirectOffsetOnAxis(ap=place_tile[:, t, k:k + 1], axis=0),
                                in_=R.tokens[:, LAST + t:LAST + t + 1], in_offset=None).then_inc(R.s_placed, 16)
            pool.wait_ge(s_ids_in, 16)
            pool.wait_ge(s_x1_out, 16)
            pool.wait_ge(s_d_lo, sum(DVE_E))
            pool.wait_ge(s_tiles, 1)
            with pool.Fori(0, TURNS) as i:
                for k in range(GROUP):
                    j = i * GROUP + k
                    number = pool.value_load(tile_number_i[0:1, bass.ds(j, 1)], min_val=0, max_val=NE * ETILES - 1)
                    wait_apart(pool, s_turn, j + 1, s_passed)
                    pool.tensor_copy(ids_now[:, k:k + 1], token_ids[:, bass.ds(number, 1)]).then_inc(s_ids_now, 1)
                    wait_apart(pool, s_ids_now, j + 1, s_passed)
                    pool.indirect_dma_start(out=token_rows[:, k], out_offset=None, in_=R.x1_dram,
                                            in_offset=bass.IndirectOffsetOnAxis(ap=ids_now[:, k:k + 1], axis=0)
                                            ).then_inc(s_tok_in[k], 16)

        @block.tensor
        def _(pe):
            pe.wait_ge(s_gate_in, 16)
            for c in range(C):
                last = pe.transpose(psum[:, 1, c * NE:(c + 1) * NE], gate_rows[:, c * P:(c + 1) * P], ident[0:NE, 0:NE])
            last.then_inc(s_gate, 1)
            pe.wait_ge(s_x1, TT)
            for c in range(C):
                for t in range(TT):
                    last = pe.transpose(psum[:, 4 + c, t * P:(t + 1) * P], rows[:, t, c * P:(c + 1) * P], ident[:])
                last.then_inc(s_x1T_pe, 1)
            pe.wait_ge(s_gateT, 1)
            for c in range(C):
                pe.wait_ge(s_x1T, c + 1)
                last = pe.matmul(psum[0:NE, 0, :], gateT[:, c], x1T[:, c], start=c == 0, stop=c == C - 1)
            last.then_inc(s_logitT, 1)
            pe.wait_ge(s_logitT_sb, 1)
            for t in range(TT):
                last = pe.transpose(psum[:, 3, t * NE:(t + 1) * NE], logitsT[:, t * P:(t + 1) * P], ident[0:NE, 0:NE])
            last.then_inc(s_logit, 1)
            pe.wait_ge(s_chosen, 2)
            pe.matmul(psum[:, 0, 0:TT * NE], upper[:], chosen[:, 2].rearrange("p t e -> p (t e)"), start=True, stop=False)
            pe.matmul(psum[:, 0, 0:TT * NE], ones[:], before[:, 0:TT].rearrange("p t e -> p (t e)"), start=False,
                      stop=True).then_inc(s_ranked, 1)
            pe.matmul(psum[:, 1, 0:NE], ones[:], before[:, TT], start=True, stop=True).then_inc(s_counts, 1)
            pe.wait_ge(s_tiles, 1)
            pe.wait_ge(s_d_lo, sum(DVE_E))
            pe.wait_ge(s_d_lo_pool, NE * PARTS - sum(DVE_E))

            def turn(j, k, loaded):
                pe.wait_ge(s_tok_in[k], loaded)
                for c in range(C):
                    last = pe.transpose(psum[:, 2 + k % 2, c * P:(c + 1) * P], token_rows[:, k, c * P:(c + 1) * P], ident[:])
                last.then_inc(s_turn, 1)

            def multiply(j, k):
                e = pe.value_load(tile_expert_i[0:1, bass.ds(j, 1)], min_val=0, max_val=NE - 1)
                pe.wait_ge(s_lo, j + 1)
                dst = psum[:, 4 + k, :]
                for c in range(C):
                    hi = d_hi[:, c, bass.ds(e, 1), :].rearrange("p a n -> p (a n)")
                    lo = d_lo[:, c, bass.ds(e, 1), :].rearrange("p a n -> p (a n)")
                    pe.matmul(dst, xT_hi[:, k % 2, c], hi, start=c == 0, stop=False)
                    pe.matmul(dst, xT_hi[:, k % 2, c], lo, start=False, stop=False)
                    last = pe.matmul(dst, xT_lo[:, k % 2, c], hi, start=False, stop=c == C - 1)
                last.then_inc(s_y, 1)

            def turn_of_loop(i, more):
                for k in range(GROUP):
                    j = i * GROUP + k
                    if k < GROUP - 1:
                        turn(j + 1, k + 1, 16 * (i + 1))
                    elif more:
                        turn(j + 1, 0, 16 * (i + 2))
                    multiply(j, k)

            turn(0, 0, 16)
            with pe.Fori(0, TURNS - 1) as i:
                turn_of_loop(i, True)
            turn_of_loop(TURNS - 1, False)

        @block.scalar
        def _(act):
            for q in range(PARTS):
                act.wait_ge(s_d_in[q % STAGES], 16 * (q // STAGES + 1))
                for e in range(NE):
                    act.copy(place(d_hi, q, e), part(q, e)).then_inc(s_d_hi, 1)
                if q == 0:
                    for c in range(C):
                        act.wait_ge(s_x1T_pe, c + 1)
                        act.copy(x1T[:, c], psum[:, 4 + c, :]).then_inc(s_x1T, 1)
                if q == 2:
                    act.wait_ge(s_gap, 1)
                    act.activation(gap[:, 1], gap[:, 0], ACT.Exp).then_inc(s_gap_exp, 1)


            def high(j, k):
                act.wait_ge(s_turn, GROUP + j + 1)
                act.copy(xT_hi[:, k % 2].rearrange("p c n -> p (c n)"), psum[:, 2 + k % 2, :]).then_inc(s_hi, 1)

            def turn_of_loop(i, more):
                for k in range(GROUP):
                    j = i * GROUP + k
                    if k < GROUP - 1 or more:
                        high(j + 1, (k + 1) % GROUP)
                    act.wait_ge(s_y, j + 1)
                    act.wait_ge(s_y_out[k], 16 * (i + 1))
                    act.copy(y_rows[:, k], psum[:, 4 + k, :]).then_inc(s_y_sb, 1)

            high(0, 0)
            with act.Fori(0, TURNS - 1) as i:
                turn_of_loop(i, True)
            turn_of_loop(TURNS - 1, False)

        @block.vector
        def _(dve):
            steps = 0

            def after(ins):
                nonlocal steps
                steps += 1
                ins.then_inc(s_step, 1)
                dve.wait_ge(s_step, steps)

            for k in range(GROUP):
                dve.memset(row[:, k:k + 1], 0.0).then_inc(s_y_out[k], 16)
            dve.memset(row_step[:], 0.0).then_inc(s_turn, GROUP)
            for t in range(TT):
                last = dve.bn_stats(stats[:, t], rows[:, t])
            after(last)
            for t in range(TT):
                last = dve.bn_aggr(mean_var[:, t], stats[:, t])
            after(last)
            dve.tensor_scalar(var_eps[:], mean_var[:, :, 1], EPS, None, ALU.add).then_inc(s_var, 1)
            dve.wait_ge(s_rstd, 1)
            for t in range(TT):
                dve.tensor_scalar(rows[:, t], rows[:, t], mean_var[:, t, 0:1], rstd[:, t:t + 1], ALU.subtract,
                                  ALU.mult).then_inc(s_x1, 1)
            dve.wait_ge(s_x1, TT)
            dve.wait_ge(s_gate, 1)
            dve.tensor_copy(gateT[:].rearrange("p c e -> p (c e)"), psum[:, 1, 0:C * NE]).then_inc(s_gateT, 1)

            def lows(q):
                for e in range(DVE_E[q]):
                    dve.wait_ge(s_d_hi, q * NE + e + 1)
                    dve.tensor_tensor(place(d_lo, q, e), part(q, e), place(d_hi, q, e).bitcast(F32),
                                      ALU.subtract).then_inc(s_d_lo, 1)

            lows(0)
            dve.wait_ge(s_logitT, 1)
            dve.tensor_copy(logitsT[:], psum[0:NE, 0, :]).then_inc(s_logitT_sb, 1)
            lows(1)
            dve.wait_ge(s_logit, 1)
            after(dve.tensor_scalar(clipped[:].rearrange("p t e -> p (t e)"), psum[:, 3, 0:TT * NE], 50.0, -50.0, ALU.min,
                                    ALU.max))
            for t in range(TT):
                last = dve.max(best[:, t], clipped[:, t])
            after(last)
            dve.tensor_tensor(gap[:, 0], best[:, :, 1], best[:, :, 0], ALU.subtract).then_inc(s_gap, 1)
            for t in range(TT):
                last = dve.max_index(best_at[:, t], best[:, t], clipped[:, t])
            after(last)
            after(dve.tensor_copy(expert[:], best_at[:, :, 0:2]))
            for t in range(TT):
                for k in range(2):
                    last = dve.tensor_scalar(chosen[:, k, t], R.number[:], expert[:, t, k:k + 1], None, ALU.is_equal)
            after(last)
            after(dve.tensor_tensor(chosen[:, 2], chosen[:, 0], chosen[:, 1], ALU.add))
            after(dve.tensor_copy(before[:, 0], R.counts[:]))
            for t in range(TT):
                after(dve.tensor_tensor(before[:, t + 1], before[:, t], chosen[:, 2, t], ALU.add))
            dve.tensor_copy(share_sum[:], gap[:, 0]).then_inc(s_chosen, 2)
            for k in range(2):
                dve.tensor_copy(R.experts[:, k, LAST:NT], expert[:, :, k])
            lows(2)
            dve.wait_ge(s_ranked, 1)
            after(dve.tensor_copy(ranks[:].rearrange("p t e -> p (t e)"), psum[:, 0, 0:TT * NE]))
            for t in range(TT):
                for k in range(2):
                    last = dve.tensor_tensor_reduce(product8[:, t, k], ranks[:, t], chosen[:, k, t], 1.0, 0.0, ALU.mult,
                                                    ALU.add, rank[:, t, k:k + 1])
            after(last)
            after(dve.tensor_copy(rank_i[:], rank[:]))
            dve.tensor_scalar(tile_i[:], rank_i[:], P_SHIFT, None, ALU.logical_shift_right)
            after(dve.tensor_scalar(place_i[:], rank_i[:], P - 1, PLACE_SHIFT, ALU.bitwise_and, ALU.logical_shift_left))
            after(dve.scalar_tensor_tensor(out=tile_f[:], in0=expert[:], scalar=float(ETILES), in1=tile_i[:],
                                           op0=ALU.mult, op1=ALU.add))
            dve.tensor_tensor(place_tile[:], tile_f[:], place_i[:], ALU.add).then_inc(s_place, 1)
            for k in range(2):
                dve.tensor_copy(R.all_ranks[:, k, LAST:NT], rank[:, :, k])
            lows(3)
            dve.wait_ge(s_gap_exp, 1)
            after(dve.tensor_scalar(share_sum[:], gap[:, 1], 1.0, None, ALU.add))
            after(dve.reciprocal(share_sum[:], share_sum[:]))
            dve.tensor_copy(R.shares[:, 0, LAST:NT], share_sum[:])
            dve.tensor_tensor(R.shares[:, 1, LAST:NT], share_sum[:], gap[:, 1], ALU.mult)
            lows(4)
            dve.wait_ge(s_counts, 1)
            after(dve.tensor_scalar(counts_i[:], psum[:, 1, 0:NE], float(P - 1), None, ALU.add))
            after(dve.tensor_scalar(tiles_i[:], counts_i[:], P_SHIFT, None, ALU.logical_shift_right))
            after(dve.tensor_copy(tiles[:], tiles_i[:]))
            after(dve.tensor_copy(ends[:, 0:1], tiles[:, 0:1]))
            for e in range(1, NE):
                after(dve.tensor_tensor(ends[:, e:e + 1], ends[:, e - 1:e], tiles[:, e:e + 1], ALU.add))
            after(dve.tensor_tensor(starts[:], ends[:], tiles[:], ALU.subtract))
            lows(5)
            dve.wait_ge(s_tile_at, 1)
            after(dve.tensor_copy(tile_at[:], tile_at_i[:]))
            after(dve.tensor_tensor(behind[:], tile_at[:].unsqueeze(1).broadcast_to([P, NE, JT]),
                                    ends[:].unsqueeze(2).broadcast_to([P, NE, JT]), ALU.is_ge))
            dve.tensor_tensor(behind_tiles[:], behind[:], tiles[:].unsqueeze(2).broadcast_to([P, NE, JT]),
                              ALU.mult).then_inc(s_behind, 1)
            after(dve.tensor_reduce(tile_expert[:], behind[:].rearrange("p e j -> p j e"), AX.X, ALU.add))
            dve.wait_ge(s_behind, 1)
            after(dve.tensor_reduce(tile_start[:], behind_tiles[:].rearrange("p e j -> p j e"), AX.X, ALU.add))
            lows(6)
            after(dve.tensor_scalar(tile_expert[:], tile_expert[:], float(NE - 1), None, ALU.min))
            after(dve.tensor_tensor(tile_step[:], tile_at[:], tile_start[:], ALU.subtract))
            after(dve.tensor_scalar(tile_step[:], tile_step[:], float(ETILES - 1), None, ALU.min))
            after(dve.scalar_tensor_tensor(out=tile_number_i[:], in0=tile_expert[:], scalar=float(ETILES),
                                           in1=tile_step[:], op0=ALU.mult, op1=ALU.add))
            dve.tensor_copy(tile_expert_i[:], tile_expert[:]).then_inc(s_tiles, 1)
            lows(7)

            def low(j, k):
                dve.wait_ge(s_hi, j + 1)
                dve.tensor_tensor(xT_lo[:, k % 2].rearrange("p c n -> p (c n)"), psum[:, 2 + k % 2, :],
                                  xT_hi[:, k % 2].rearrange("p c n -> p (c n)").bitcast(F32), ALU.subtract).then_inc(s_lo, 1)

            with dve.Fori(0, TURNS) as i:
                for k in range(GROUP):
                    low(i * GROUP + k, k)
            flat = R.experts[:].rearrange("p k t -> p (k t)")
            after(dve.tensor_scalar(starts[:], starts[:], float(P), None, ALU.mult))
            after(dve.tensor_copy(row[:], R.all_ranks[:].rearrange("p k t -> p (k t)")))
            for e in range(NE):
                after(dve.tensor_scalar(row_step[:], flat, float(e), starts[:, e:e + 1], ALU.is_equal, ALU.mult))
                after(dve.tensor_tensor(row[:], row[:], row_step[:], ALU.add))
            after(dve.tensor_copy(R.row_i[:], row[:]))


def combine(nc, sem, s_passed, R, y_dram, out_rows):
    BUF = 4
    PAIRS = NT // 2
    OUTER = PAIRS // BUF
    with ExitStack() as ctx:
        def sb(name, shape, dt=F32):
            return ctx.enter_context(nc.sbuf_tensor(name, shape, dt))

        x1, y0, y1 = sb("c_x1", [P, BUF, 2, DM]), sb("c_y0", [P, BUF, 2, DM]), sb("c_y1", [P, BUF, 2, DM])
        first, z, y_out = sb("c_first", [P, BUF, 2, DM]), sb("c_z", [P, BUF, 2, DM]), sb("c_out", [P, BUF, 2, DM])
        row_now, share = sb("c_row_now", [P, BUF, 2, 2], I32), sb("c_share", [P, BUF, 2, 2])
        stats, mean_var, var_eps = sb("c_stats", [P, 2, 2, 6]), sb("c_mean_var", [P, BUF, 2, 2]), sb("c_var_eps", [P, BUF, 2])
        rstd, shift = sb("c_rstd", [P, BUF, 2]), sb("c_shift", [P, BUF, 2])
        halves = sb("c_minus_half", [P, 2])
        s_x1 = [sem(f"c_x1_{k}_loaded") for k in range(BUF)]
        s_y = [sem(f"c_rows_{k}_loaded") for k in range(BUF)]
        s_row_now, s_used, s_share, s_first = sem("c_row_copied"), sem("c_rows_used"), sem("c_share_ready"), sem("c_first_ready")
        s_step, s_var, s_rstd, s_shift, s_norm = (sem("c_step"), sem("c_var_ready"), sem("c_rstd_ready"),
                                                  sem("c_shift_ready"), sem("c_normalized"))
        s_out = [sem(f"c_out_{k}_stored") for k in range(BUF)]
        s_halves = sem("c_minus_half_ready")
        block = ctx.enter_context(nc.Block())
        x1_pairs = R.x1_dram.rearrange("(u t p) d -> u p t d", t=2, p=P)
        out_pairs = out_rows.rearrange("(u t) p d -> u p t d", t=2)

        @block.sync
        def _(sp):
            def load(u, k):
                wait_apart(sp, s_used, 2 * u + 2, s_passed)
                sp.dma_start(x1[:, k], x1_pairs[bass.ds(u, 1)].rearrange("a p t d -> (a p) t d")).then_inc(s_x1[k], 16)

            def store(u, k):
                wait_apart(sp, s_norm, 2 * u + 2, s_passed)
                sp.dma_start(out_pairs[bass.ds(u, 1)].rearrange("a p t d -> (a p) t d"), y_out[:, k]).then_inc(s_out[k], 16)

            for k in range(2):
                load(k, k)

            def pairs(i, more):
                for k in range(BUF):
                    if k < BUF - 2 or more:
                        load(i * BUF + k + 2, (k + 2) % BUF)
                    store(i * BUF + k, k)

            with sp.Fori(0, OUTER - 1) as i:
                pairs(i, True)
            pairs(OUTER - 1, False)
            for k in range(BUF):
                sp.wait_ge(s_out[k], 16 * (OUTER + 1))

        @block.gpsimd
        def _(pool):
            def gather(u, k):
                wait_apart(pool, s_used, 2 * u + 2, s_passed)
                for c in range(2):
                    pool.tensor_copy(row_now[:, k, c], R.row_i[:, bass.ds(c * NT + u * 2, 2)]).then_inc(s_row_now, 1)
                wait_apart(pool, s_row_now, 2 * u + 2, s_passed)
                for t in range(2):
                    for c, y in enumerate((y0, y1)):
                        pool.indirect_dma_start(out=y[:, k, t], out_offset=None, in_=y_dram,
                                                in_offset=bass.IndirectOffsetOnAxis(ap=row_now[:, k, c, t:t + 1], axis=0)
                                                ).then_inc(s_y[k], 16)

            def rstd_of(u, k):
                wait_apart(pool, s_var, u + 1, s_passed)
                pool.tensor_tensor(rstd[:, k], var_eps[:, k], halves[:], ALU.pow).then_inc(s_rstd, 1)

            def pairs(i, more):
                for k in range(BUF):
                    if k < BUF - 3 or more:
                        gather(i * BUF + k + 3, (k + 3) % BUF)
                    rstd_of(i * BUF + k, k)

            pool.memset(halves[:], -0.5).then_inc(s_halves, 1)
            pool.wait_ge(s_halves, 1)
            for k in range(3):
                gather(k, k)
            with pool.Fori(0, OUTER - 1) as i:
                pairs(i, True)
            pairs(OUTER - 1, False)

        @block.scalar
        def _(act):
            def weigh(u, k, i):
                act.wait_ge(s_share, u + 1)
                act.wait_ge(s_y[k], 64 * (i + 1))
                for t in range(2):
                    act.activation(first[:, k, t], y0[:, k, t], ACT.Copy, scale=share[:, k, 0, t:t + 1]).then_inc(s_first, 1)

            def normalize(u, k, i):
                act.wait_ge(s_shift, 2 * u + 2)
                act.wait_ge(s_out[k], 16 * (i + 1))
                for t in range(2):
                    act.activation(y_out[:, k, t], z[:, k, t], ACT.Identity, bias=shift[:, k, t:t + 1],
                                   scale=rstd[:, k, t:t + 1]).then_inc(s_norm, 1)

            weigh(0, 0, 0)
            weigh(1, 1, 0)

            def pairs(i, more):
                for k in range(BUF):
                    if k < BUF - 2:
                        weigh(i * BUF + k + 2, k + 2, i)
                    elif more:
                        weigh(i * BUF + k + 2, k + 2 - BUF, i + 1)
                    normalize(i * BUF + k, k, i)

            with act.Fori(0, OUTER - 1) as i:
                pairs(i, True)
            pairs(OUTER - 1, False)

        @block.vector
        def _(dve):
            STEPS = 6

            def shares(u, k):
                dve.tensor_copy(share[:, k], R.shares[:, :, bass.ds(u * 2, 2)]).then_inc(s_share, 1)

            def total(u, k, i):
                dve.wait_ge(s_x1[k], 16 * (i + 1))
                for t in range(2):
                    dve.wait_ge(s_first, 2 * u + t + 1)
                    dve.tensor_tensor(first[:, k, t], first[:, k, t], x1[:, k, t], ALU.add).then_inc(s_step, 1)
                for t in range(2):
                    wait_apart(dve, s_step, STEPS * u + 1 + t, s_passed)
                    dve.scalar_tensor_tensor(out=z[:, k, t], in0=y1[:, k, t], scalar=share[:, k, 1, t:t + 1], in1=first[:, k, t],
                                             op0=ALU.mult, op1=ALU.add).then_inc(s_used, 1)
                for t in range(2):
                    wait_apart(dve, s_used, 2 * (BUF + u) + t + 1, s_passed)
                    dve.bn_stats(stats[:, k % 2, t], z[:, k, t]).then_inc(s_step, 1)
                for t in range(2):
                    wait_apart(dve, s_step, STEPS * u + 3 + t, s_passed)
                    dve.bn_aggr(mean_var[:, k, t], stats[:, k % 2, t]).then_inc(s_step, 1)
                wait_apart(dve, s_step, STEPS * u + 6, s_passed)
                dve.tensor_scalar(var_eps[:, k], mean_var[:, k, :, 1], EPS, None, ALU.add).then_inc(s_var, 1)

            def shift_of(u, k):
                dve.wait_ge(s_rstd, u + 1)
                for t in range(2):
                    dve.scalar_tensor_tensor(out=shift[:, k, t:t + 1], in0=mean_var[:, k, t, 0:1], scalar=-1.0,
                                             in1=rstd[:, k, t:t + 1], op0=ALU.mult, op1=ALU.mult).then_inc(s_shift, 1)

            dve.memset(x1[:, 0], 0.0).then_inc(s_used, 2 * BUF)
            for k in range(BUF):
                dve.memset(y_out[:, k, 0, 0:1], 0.0).then_inc(s_out[k], 16)
            for k in range(2):
                shares(k, k)
            total(0, 0, 0)

            def pairs(i, more):
                for k in range(BUF):
                    u = i * BUF + k
                    if k < BUF - 2 or more:
                        shares(u + 2, (k + 2) % BUF)
                    if k < BUF - 1:
                        total(u + 1, k + 1, i)
                    elif more:
                        total(u + 1, 0, i + 1)
                    shift_of(u, k)

            with dve.Fori(0, OUTER - 1) as i:
                pairs(i, True)
            pairs(OUTER - 1, False)


_INS = ['L0_attn_x', 'L0_attn_wq', 'L0_attn_wk', 'L0_attn_wv', 'L0_attn_wo', 'L0_ffn_gate_w', 'L0_ffn_W',
        'L0_ffn_atoms', 'L0_ffn_expert_atom_weights', 'L0_ffn_importance', 'L0_ffn_mask_idx']
_OUTS = [((NB, T, DM), 'float32')]


def kernel(**inputs):
    import numpy as _np
    import concourse.bacc as _bacc
    from concourse import mybir as _mybir
    from concourse.bass_utils import run_bass_kernel_spmd as _run

    nc = _bacc.Bacc("TRN2", target_bir_lowering=False, num_devices=1)
    arrays, args = {}, []
    for name in _INS:
        a = _np.ascontiguousarray(inputs[name])
        arrays[f"in_{name}_dram"] = a
        args.append(nc.dram_tensor(f"in_{name}_dram", a.shape, _mybir.dt.from_np(a.dtype), kind="ExternalInput").ap())
    for i, (shape, dtype) in enumerate(_OUTS):
        dt = _mybir.dt.from_np(_np.dtype(dtype))
        args.append(nc.dram_tensor(f"out_{i}_dram", shape, dt, kind="ExternalOutput").ap())
    build(nc, *args)
    r = _run(nc, [arrays], core_ids=[0])
    got = tuple(r.results[0][f"out_{i}_dram"] for i in range(len(_OUTS)))
    return got[0]
```
